# Optimizing a Trainium2 kernel written in Bass

```python
import numpy as np
import jax
import jax.numpy as jnp

def _softmax(x, axis=-1):
    return jax.nn.softmax(x, axis=axis)

def _gelu(x):
    return jax.nn.gelu(x, approximate=True)

def _silu(x):
    return jax.nn.silu(x)

def _sigmoid(x):
    return jax.nn.sigmoid(x)

def _layernorm(x, axis=-1, eps=1e-05):
    m = jnp.mean(x, axis=axis, keepdims=True)
    v = jnp.var(x, axis=axis, keepdims=True)
    return (x - m) / jnp.sqrt(v + eps)

def _scatter_add(tgt, idx, src, axis=0):
    return tgt.at[idx].add(src)

def _segment_sum(src, seg, n):
    return jax.ops.segment_sum(src, seg, n)
kernel_name = 'mk_recurrent_d2_jaxref_r8_cfabb5'

def setup_inputs(seed: int=0):
    np.random.seed(seed)
    _w = jnp.asarray

    def _L0_attn_setup():
        import jax, jax.numpy as jnp
        import numpy as np
        B, S, E = (4, 256, 128)
        H = 16
        D = E // H
        WIN = 64

        def _sliding_window_attention(q, k, v, win):
            b, h, s, d = q.shape
            nb = s // win
            scale = 1.0 / jnp.sqrt(jnp.float32(d))
            qb = q.reshape(b, h, nb, win, d)
            kb = k.reshape(b, h, nb, win, d)
            vb = v.reshape(b, h, nb, win, d)
            zpad = jnp.zeros_like(kb[:, :, :1])
            k2 = jnp.concatenate([jnp.concatenate([zpad, kb[:, :, :-1]], axis=2), kb], axis=3)
            v2 = jnp.concatenate([jnp.concatenate([zpad, vb[:, :, :-1]], axis=2), vb], axis=3)
            scores = jnp.einsum('bhnqd,bhnkd->bhnqk', qb, k2) * scale
            qi = jnp.arange(win)[:, None]
            kj = jnp.arange(2 * win)[None, :]
            delta = qi - kj + win
            valid = (delta >= 0) & (delta <= win)
            blk = jnp.arange(nb)[:, None, None]
            valid = valid[None] & (blk * win + (kj[None] - win) >= 0)
            slopes = jnp.exp2(-(jnp.arange(H, dtype=jnp.float32) + 1.0) * 8.0 / H)
            bias = slopes[:, None, None] * delta.astype(jnp.float32)
            scores = jnp.where(valid[None, :, :, :, :][:, None].squeeze(0)[None] if False else valid[None, None], scores + bias[None, :, None], -jnp.inf)
            p = jax.nn.softmax(scores, axis=-1)
            out = jnp.einsum('bhnqk,bhnkd->bhnqd', p, v2)
            return out.reshape(b, h, s, d)
        key = jax.random.key(seed)
        k1, k2, k3 = jax.random.split(key, 3)
        x = jax.random.normal(k1, (B, S, E), dtype=jnp.float32)
        w_in = jax.random.normal(k2, (3 * E, E), dtype=jnp.float32) * 0.02
        w_out = jax.random.normal(k3, (E, E), dtype=jnp.float32) * 0.02
        return {'x': x, 'w_in': w_in, 'w_out': w_out}
    _L0_attn_in = _L0_attn_setup()

    def _L0_ffn_setup():
        import jax, jax.numpy as jnp
        import numpy as np
        HIDDEN = 128
        N_EXPERTS = 8
        TOP_K = 2
        INTER = 176
        N_SHARED = 2
        SCALE = 1.0
        key = jax.random.key(seed)
        ks = jax.random.split(key, 9)
        s_h = 1.0 / np.sqrt(HIDDEN)
        s_i = 1.0 / np.sqrt(INTER)
        x = jax.random.normal(ks[0], (2, 256, HIDDEN), dtype=jnp.float32)
        gate_w = jax.random.uniform(ks[1], (N_EXPERTS, HIDDEN), jnp.float32, -s_h, s_h)
        wg = jax.random.uniform(ks[2], (N_EXPERTS, HIDDEN, INTER), jnp.float32, -s_h, s_h)
        wu = jax.random.uniform(ks[3], (N_EXPERTS, HIDDEN, INTER), jnp.float32, -s_h, s_h)
        wd = jax.random.uniform(ks[4], (N_EXPERTS, INTER, HIDDEN), jnp.float32, -s_i, s_i)
        si = INTER * N_SHARED
        s_si = 1.0 / np.sqrt(si)
        swg = jax.random.uniform(ks[5], (HIDDEN, si), jnp.float32, -s_h, s_h)
        swu = jax.random.uniform(ks[6], (HIDDEN, si), jnp.float32, -s_h, s_h)
        swd = jax.random.uniform(ks[7], (si, HIDDEN), jnp.float32, -s_si, s_si)
        return {'x': x, 'gate_w': gate_w, 'wg': wg, 'wu': wu, 'wd': wd, 'swg': swg, 'swu': swu, 'swd': swd}
    _L0_ffn_in = _L0_ffn_setup()

    def _L1_attn_setup():
        import jax, jax.numpy as jnp
        import numpy as np
        import math
        D_MODEL = 128
        N_HEADS = 16
        D_K = D_MODEL // N_HEADS
        MAX_REL = 128

        def _rel_bias_matrix(rel_bias, seq_len):
            pos = jnp.arange(seq_len)
            rel = pos[:, None] - pos[None, :]
            idx = jnp.clip(rel, -MAX_REL, MAX_REL) + MAX_REL
            return rel_bias[:, idx]
        key = jax.random.key(seed)
        ks = jax.random.split(key, 10)
        B, S = (2, 256)
        std = 1.0 / math.sqrt(D_MODEL)
        inp = {'x': jax.random.normal(ks[0], (B, S, D_MODEL), dtype=jnp.float32), 'Wq': jax.random.normal(ks[1], (D_MODEL, D_MODEL), dtype=jnp.float32) * std, 'bq': jnp.zeros((D_MODEL,), dtype=jnp.float32), 'Wk': jax.random.normal(ks[2], (D_MODEL, D_MODEL), dtype=jnp.float32) * std, 'bk': jnp.zeros((D_MODEL,), dtype=jnp.float32), 'Wv': jax.random.normal(ks[3], (D_MODEL, D_MODEL), dtype=jnp.float32) * std, 'bv': jnp.zeros((D_MODEL,), dtype=jnp.float32), 'Wo': jax.random.normal(ks[4], (D_MODEL, D_MODEL), dtype=jnp.float32) * std, 'bo': jnp.zeros((D_MODEL,), dtype=jnp.float32), 'rel_bias': jax.random.normal(ks[5], (N_HEADS, 2 * MAX_REL + 1), dtype=jnp.float32) * 0.02}
        return inp
    _L1_attn_in = _L1_attn_setup()

    def _L1_ffn_setup():
        import jax, jax.numpy as jnp
        import numpy as np
        DIM = 128
        DEPTH = 2
        HEADS = 8
        DIM_HEAD = 64
        WINDOW = 64
        INNER = HEADS * DIM_HEAD
        HID = int(DIM * 4 * 2 / 3)
        B, N = (2, 1024)
        QK_SCALE = 8.0

        def shift_token(t):
            t1, t2 = jnp.split(t, 2, axis=-1)
            t2 = jnp.pad(t2, ((0, 0), (1, 0), (0, 0)))[:, :-1]
            return jnp.concatenate([t1, t2], axis=-1)

        def l2norm(t):
            return t / jnp.clip(jnp.linalg.norm(t, axis=-1, keepdims=True), 1e-12)

        def rotate_half(x):
            x1, x2 = jnp.split(x, 2, axis=-1)
            return jnp.concatenate([-x2, x1], axis=-1)

        def rotary_xpos(q, k):
            n = q.shape[-2]
            half_idx = jnp.arange(0, DIM_HEAD, 2, dtype=jnp.float32)
            inv_freq = 1.0 / 10000.0 ** (half_idx / DIM_HEAD)
            t = jnp.arange(n, dtype=jnp.float32)
            freqs = t[:, None] * inv_freq[None, :]
            freqs = jnp.concatenate([freqs, freqs], axis=-1)
            base = (half_idx + 0.4 * DIM_HEAD) / (1.4 * DIM_HEAD)
            power = (t - n // 2) / float(WINDOW // 2)
            scale = base[None, :] ** power[:, None]
            scale = jnp.concatenate([scale, scale], axis=-1)
            cos, sin = (jnp.cos(freqs), jnp.sin(freqs))
            q = q * cos * scale + rotate_half(q) * sin * scale
            k = k * cos / scale + rotate_half(k) * sin / scale
            return (q, k)

        def local_attention(q, k, v):
            b, h, n, d = q.shape
            w = n // WINDOW
            bq = q.reshape(b, h, w, WINDOW, d) * QK_SCALE
            bk = k.reshape(b, h, w, WINDOW, d)
            bv = v.reshape(b, h, w, WINDOW, d)

            def look_around(t):
                p = jnp.pad(t, ((0, 0), (0, 0), (1, 0), (0, 0), (0, 0)))
                return jnp.concatenate([p[:, :, :w], p[:, :, 1:]], axis=3)
            bk, bv = (look_around(bk), look_around(bv))
            bt = jnp.arange(n).reshape(w, WINDOW)
            btp = jnp.pad(bt, ((1, 0), (0, 0)), constant_values=-1)
            btk = jnp.concatenate([btp[:w], btp[1:]], axis=1)
            sim = jnp.einsum('bhwid,bhwjd->bhwij', bq, bk)
            i = bt[:, :, None]
            j = btk[:, None, :]
            mask = (i < j) | (i > j + WINDOW) | (j == -1)
            sim = jnp.where(mask, -jnp.finfo(sim.dtype).max, sim)
            attn = jax.nn.softmax(sim, axis=-1)
            out = jnp.einsum('bhwij,bhwjd->bhwid', attn, bv)
            return out.reshape(b, h, n, d)

        def _layer(x, wqkv, qs, ksc, wo, lg, lb, w1, b1, w2, b2):
            b, n, _ = x.shape
            h = shift_token(x)
            qkv = h @ wqkv
            q, k, v = jnp.split(qkv, 3, axis=-1)
            to_heads = lambda t: t.reshape(b, n, HEADS, DIM_HEAD).transpose(0, 2, 1, 3)
            q, k, v = (to_heads(q), to_heads(k), to_heads(v))
            q = l2norm(q) * qs
            k = l2norm(k) * ksc
            q, k = rotary_xpos(q, k)
            o = local_attention(q, k, v)
            o = o.transpose(0, 2, 1, 3).reshape(b, n, INNER)
            x = x + o @ wo
            h = shift_token(x)
            mu = h.mean(-1, keepdims=True)
            var = h.var(-1, keepdims=True)
            h = (h - mu) / jnp.sqrt(var + 1e-05) * lg + lb
            h = h @ w1 + b1
            a, g = jnp.split(h, 2, axis=-1)
            h = a * jax.nn.gelu(g, approximate=False)
            x = x + h @ w2 + b2
            return x
        key = jax.random.key(seed)
        ks = jax.random.split(key, 6)
        return {'x': jax.random.normal(ks[0], (B, N, DIM), jnp.float32), 'wqkv': jax.random.normal(ks[1], (DEPTH, DIM, 3 * INNER), jnp.float32) * 0.02, 'q_scale': jnp.ones((DEPTH, DIM_HEAD), jnp.float32), 'k_scale': jnp.ones((DEPTH, DIM_HEAD), jnp.float32), 'wo': jax.random.normal(ks[2], (DEPTH, INNER, DIM), jnp.float32) * 0.02, 'ln_g': jnp.ones((DEPTH, DIM), jnp.float32), 'ln_b': jnp.zeros((DEPTH, DIM), jnp.float32), 'w1': jax.random.normal(ks[3], (DEPTH, DIM, 2 * HID), jnp.float32) * 0.02, 'b1': jnp.zeros((DEPTH, 2 * HID), jnp.float32), 'w2': jax.random.normal(ks[4], (DEPTH, HID, DIM), jnp.float32) * 0.02, 'b2': jnp.zeros((DEPTH, DIM), jnp.float32)}
    _L1_ffn_in = _L1_ffn_setup()
    _d = {'L0_attn_x': _L0_attn_in['x'], 'L0_attn_w_in': _L0_attn_in['w_in'], 'L0_attn_w_out': _L0_attn_in['w_out'], 'L0_ffn_gate_w': _L0_ffn_in['gate_w'], 'L0_ffn_wg': _L0_ffn_in['wg'], 'L0_ffn_wu': _L0_ffn_in['wu'], 'L0_ffn_wd': _L0_ffn_in['wd'], 'L0_ffn_swg': _L0_ffn_in['swg'], 'L0_ffn_swu': _L0_ffn_in['swu'], 'L0_ffn_swd': _L0_ffn_in['swd'], 'L1_attn_Wq': _L1_attn_in['Wq'], 'L1_attn_bq': _L1_attn_in['bq'], 'L1_attn_Wk': _L1_attn_in['Wk'], 'L1_attn_bk': _L1_attn_in['bk'], 'L1_attn_Wv': _L1_attn_in['Wv'], 'L1_attn_bv': _L1_attn_in['bv'], 'L1_attn_Wo': _L1_attn_in['Wo'], 'L1_attn_bo': _L1_attn_in['bo'], 'L1_attn_rel_bias': _L1_attn_in['rel_bias'], 'L1_ffn_wqkv': _L1_ffn_in['wqkv'], 'L1_ffn_q_scale': _L1_ffn_in['q_scale'], 'L1_ffn_k_scale': _L1_ffn_in['k_scale'], 'L1_ffn_wo': _L1_ffn_in['wo'], 'L1_ffn_ln_g': _L1_ffn_in['ln_g'], 'L1_ffn_ln_b': _L1_ffn_in['ln_b'], 'L1_ffn_w1': _L1_ffn_in['w1'], 'L1_ffn_b1': _L1_ffn_in['b1'], 'L1_ffn_w2': _L1_ffn_in['w2'], 'L1_ffn_b2': _L1_ffn_in['b2']}
    _x0 = _d['L0_attn_x']
    _d['L0_attn_x'] = jax.random.normal(jax.random.fold_in(jax.random.key(seed), 1), (16, 256, 128), dtype=_x0.dtype)
    del _x0
    return _d

def reference(L0_attn_x, L0_attn_w_in, L0_attn_w_out, L0_ffn_gate_w, L0_ffn_wg, L0_ffn_wu, L0_ffn_wd, L0_ffn_swg, L0_ffn_swu, L0_ffn_swd, L1_attn_Wq, L1_attn_bq, L1_attn_Wk, L1_attn_bk, L1_attn_Wv, L1_attn_bv, L1_attn_Wo, L1_attn_bo, L1_attn_rel_bias, L1_ffn_wqkv, L1_ffn_q_scale, L1_ffn_k_scale, L1_ffn_wo, L1_ffn_ln_g, L1_ffn_ln_b, L1_ffn_w1, L1_ffn_b1, L1_ffn_w2, L1_ffn_b2):

    def _L0_attn_ref(x, w_in, w_out):
        import jax, jax.numpy as jnp
        import numpy as np
        B, S, E = (4, 256, 128)
        H = 16
        D = E // H
        WIN = 64

        def _sliding_window_attention(q, k, v, win):
            b, h, s, d = q.shape
            nb = s // win
            scale = 1.0 / jnp.sqrt(jnp.float32(d))
            qb = q.reshape(b, h, nb, win, d)
            kb = k.reshape(b, h, nb, win, d)
            vb = v.reshape(b, h, nb, win, d)
            zpad = jnp.zeros_like(kb[:, :, :1])
            k2 = jnp.concatenate([jnp.concatenate([zpad, kb[:, :, :-1]], axis=2), kb], axis=3)
            v2 = jnp.concatenate([jnp.concatenate([zpad, vb[:, :, :-1]], axis=2), vb], axis=3)
            scores = jnp.einsum('bhnqd,bhnkd->bhnqk', qb, k2) * scale
            qi = jnp.arange(win)[:, None]
            kj = jnp.arange(2 * win)[None, :]
            delta = qi - kj + win
            valid = (delta >= 0) & (delta <= win)
            blk = jnp.arange(nb)[:, None, None]
            valid = valid[None] & (blk * win + (kj[None] - win) >= 0)
            slopes = jnp.exp2(-(jnp.arange(H, dtype=jnp.float32) + 1.0) * 8.0 / H)
            bias = slopes[:, None, None] * delta.astype(jnp.float32)
            scores = jnp.where(valid[None, :, :, :, :][:, None].squeeze(0)[None] if False else valid[None, None], scores + bias[None, :, None], -jnp.inf)
            p = jax.nn.softmax(scores, axis=-1)
            out = jnp.einsum('bhnqk,bhnkd->bhnqd', p, v2)
            return out.reshape(b, h, s, d)
        b, s, e = x.shape
        qkv = jnp.einsum('bse,fe->bsf', x, w_in)
        q, k, v = jnp.split(qkv, 3, axis=-1)

        def heads(t):
            return t.reshape(b, s, H, D).transpose(0, 2, 1, 3)
        o = _sliding_window_attention(heads(q), heads(k), heads(v), WIN)
        o = o.transpose(0, 2, 1, 3).reshape(b, s, e)
        return jnp.einsum('bse,fe->bsf', o, w_out)

    def _L0_ffn_ref(x, gate_w, wg, wu, wd, swg, swu, swd):
        import jax, jax.numpy as jnp
        import numpy as np
        HIDDEN = 128
        N_EXPERTS = 8
        TOP_K = 2
        INTER = 176
        N_SHARED = 2
        SCALE = 1.0
        B, S, H = x.shape
        xf = x.reshape(-1, H)
        T = xf.shape[0]
        logits = xf.astype(jnp.float32) @ gate_w.astype(jnp.float32).T
        scores = jax.nn.softmax(logits, axis=-1)
        topw, topi = jax.lax.top_k(scores, TOP_K)
        denom = topw.sum(axis=-1, keepdims=True) + 1e-20
        topw = topw / denom * SCALE
        wdense = jnp.zeros((T, N_EXPERTS), jnp.float32).at[jnp.arange(T)[:, None], topi].set(topw)
        hg = jnp.einsum('th,ehi->eti', xf, wg)
        hu = jnp.einsum('th,ehi->eti', xf, wu)
        eo = jnp.einsum('eti,eih->eth', jax.nn.silu(hg) * hu, wd)
        y = jnp.einsum('te,eth->th', wdense, eo)
        shared = jax.nn.silu(xf @ swg) * (xf @ swu) @ swd
        return (y + shared).reshape(B, S, H)

    def _L1_attn_ref(x, Wq, bq, Wk, bk, Wv, bv, Wo, bo, rel_bias):
        import jax, jax.numpy as jnp
        import numpy as np
        import math
        D_MODEL = 128
        N_HEADS = 16
        D_K = D_MODEL // N_HEADS
        MAX_REL = 128

        def _rel_bias_matrix(rel_bias, seq_len):
            pos = jnp.arange(seq_len)
            rel = pos[:, None] - pos[None, :]
            idx = jnp.clip(rel, -MAX_REL, MAX_REL) + MAX_REL
            return rel_bias[:, idx]
        B, S, _ = x.shape

        def proj(W, b):
            y = x @ W.T + b
            return y.reshape(B, S, N_HEADS, D_K).transpose(0, 2, 1, 3)
        Q, K, V = (proj(Wq, bq), proj(Wk, bk), proj(Wv, bv))
        scores = jnp.einsum('bhqd,bhkd->bhqk', Q, K) / math.sqrt(D_K)
        scores = scores + _rel_bias_matrix(rel_bias, S)[None]
        attn = jax.nn.softmax(scores, axis=-1)
        out = jnp.einsum('bhqk,bhkd->bhqd', attn, V)
        out = out.transpose(0, 2, 1, 3).reshape(B, S, D_MODEL)
        return out @ Wo.T + bo

    def _L1_ffn_ref(x, wqkv, q_scale, k_scale, wo, ln_g, ln_b, w1, b1, w2, b2):
        import jax, jax.numpy as jnp
        import numpy as np
        DIM = 128
        DEPTH = 2
        HEADS = 8
        DIM_HEAD = 64
        WINDOW = 64
        INNER = HEADS * DIM_HEAD
        HID = int(DIM * 4 * 2 / 3)
        B, N = (2, 1024)
        QK_SCALE = 8.0

        def shift_token(t):
            t1, t2 = jnp.split(t, 2, axis=-1)
            t2 = jnp.pad(t2, ((0, 0), (1, 0), (0, 0)))[:, :-1]
            return jnp.concatenate([t1, t2], axis=-1)

        def l2norm(t):
            return t / jnp.clip(jnp.linalg.norm(t, axis=-1, keepdims=True), 1e-12)

        def rotate_half(x):
            x1, x2 = jnp.split(x, 2, axis=-1)
            return jnp.concatenate([-x2, x1], axis=-1)

        def rotary_xpos(q, k):
            n = q.shape[-2]
            half_idx = jnp.arange(0, DIM_HEAD, 2, dtype=jnp.float32)
            inv_freq = 1.0 / 10000.0 ** (half_idx / DIM_HEAD)
            t = jnp.arange(n, dtype=jnp.float32)
            freqs = t[:, None] * inv_freq[None, :]
            freqs = jnp.concatenate([freqs, freqs], axis=-1)
            base = (half_idx + 0.4 * DIM_HEAD) / (1.4 * DIM_HEAD)
            power = (t - n // 2) / float(WINDOW // 2)
            scale = base[None, :] ** power[:, None]
            scale = jnp.concatenate([scale, scale], axis=-1)
            cos, sin = (jnp.cos(freqs), jnp.sin(freqs))
            q = q * cos * scale + rotate_half(q) * sin * scale
            k = k * cos / scale + rotate_half(k) * sin / scale
            return (q, k)

        def local_attention(q, k, v):
            b, h, n, d = q.shape
            w = n // WINDOW
            bq = q.reshape(b, h, w, WINDOW, d) * QK_SCALE
            bk = k.reshape(b, h, w, WINDOW, d)
            bv = v.reshape(b, h, w, WINDOW, d)

            def look_around(t):
                p = jnp.pad(t, ((0, 0), (0, 0), (1, 0), (0, 0), (0, 0)))
                return jnp.concatenate([p[:, :, :w], p[:, :, 1:]], axis=3)
            bk, bv = (look_around(bk), look_around(bv))
            bt = jnp.arange(n).reshape(w, WINDOW)
            btp = jnp.pad(bt, ((1, 0), (0, 0)), constant_values=-1)
            btk = jnp.concatenate([btp[:w], btp[1:]], axis=1)
            sim = jnp.einsum('bhwid,bhwjd->bhwij', bq, bk)
            i = bt[:, :, None]
            j = btk[:, None, :]
            mask = (i < j) | (i > j + WINDOW) | (j == -1)
            sim = jnp.where(mask, -jnp.finfo(sim.dtype).max, sim)
            attn = jax.nn.softmax(sim, axis=-1)
            out = jnp.einsum('bhwij,bhwjd->bhwid', attn, bv)
            return out.reshape(b, h, n, d)

        def _layer(x, wqkv, qs, ksc, wo, lg, lb, w1, b1, w2, b2):
            b, n, _ = x.shape
            h = shift_token(x)
            qkv = h @ wqkv
            q, k, v = jnp.split(qkv, 3, axis=-1)
            to_heads = lambda t: t.reshape(b, n, HEADS, DIM_HEAD).transpose(0, 2, 1, 3)
            q, k, v = (to_heads(q), to_heads(k), to_heads(v))
            q = l2norm(q) * qs
            k = l2norm(k) * ksc
            q, k = rotary_xpos(q, k)
            o = local_attention(q, k, v)
            o = o.transpose(0, 2, 1, 3).reshape(b, n, INNER)
            x = x + o @ wo
            h = shift_token(x)
            mu = h.mean(-1, keepdims=True)
            var = h.var(-1, keepdims=True)
            h = (h - mu) / jnp.sqrt(var + 1e-05) * lg + lb
            h = h @ w1 + b1
            a, g = jnp.split(h, 2, axis=-1)
            h = a * jax.nn.gelu(g, approximate=False)
            x = x + h @ w2 + b2
            return x
        for l in range(DEPTH):
            x = _layer(x, wqkv[l], q_scale[l], k_scale[l], wo[l], ln_g[l], ln_b[l], w1[l], b1[l], w2[l], b2[l])
        return x
    x = L0_attn_x
    xn = _layernorm(x, axis=-1)
    s = _L0_attn_ref(xn, L0_attn_w_in, L0_attn_w_out)
    g = _silu(_L0_ffn_ref(xn, L0_ffn_gate_w, L0_ffn_wg, L0_ffn_wu, L0_ffn_wd, L0_ffn_swg, L0_ffn_swu, L0_ffn_swd))
    x = x + s * g
    xn = _layernorm(x, axis=-1)
    s = _L1_attn_ref(xn, L1_attn_Wq, L1_attn_bq, L1_attn_Wk, L1_attn_bk, L1_attn_Wv, L1_attn_bv, L1_attn_Wo, L1_attn_bo, L1_attn_rel_bias)
    g = _silu(_L1_ffn_ref(xn, L1_ffn_wqkv, L1_ffn_q_scale, L1_ffn_k_scale, L1_ffn_wo, L1_ffn_ln_g, L1_ffn_ln_b, L1_ffn_w1, L1_ffn_b1, L1_ffn_w2, L1_ffn_b2))
    x = x + s * g
    return x

_drawn_inputs = setup_inputs


def setup_inputs(seed=0):
    import zlib

    import numpy as np

    out = dict(_drawn_inputs(seed))
    spreads = {'L1_attn_bq': (0.0, 0.8),
     'L1_attn_bk': (0.0, 2.0),
     'L1_attn_bv': (0.0, 0.1),
     'L1_attn_bo': (0.0, 0.1),
     'L1_ffn_q_scale': (1.0, 0.6),
     'L1_ffn_k_scale': (1.0, 0.6),
     'L1_ffn_ln_g': (1.0, 0.6),
     'L1_ffn_ln_b': (0.0, 0.8),
     'L1_ffn_b1': (0.0, 0.8),
     'L1_ffn_b2': (0.0, 2.0)}
    factors = {'L0_attn_w_in': 8.0,
     'L0_attn_w_out': 8.0,
     'L0_ffn_gate_w': 8.0,
     'L0_ffn_wg': 8.0,
     'L0_ffn_wu': 8.0,
     'L0_ffn_wd': 8.0,
     'L0_ffn_swg': 8.0,
     'L0_ffn_swu': 8.0,
     'L0_ffn_swd': 8.0,
     'L1_attn_rel_bias': 53.431,
     'L1_ffn_wqkv': 8.0,
     'L1_ffn_wo': 8.0,
     'L1_ffn_w1': 8.0,
     'L1_ffn_w2': 8.0}
    for name, (base, spread) in spreads.items():
        noise = np.random.default_rng([zlib.crc32(name.encode()), seed]).standard_normal(out[name].shape)
        drawn = base * np.exp(spread * noise) if base else spread * noise
        out[name] = jnp.asarray(drawn.astype(out[name].dtype))
    for name, factor in factors.items():
        out[name] = (out[name] * factor).astype(out[name].dtype)
    return out
```

```python
import numpy as np
import concourse.bass as bass
from concourse import mybir
from contextlib import ExitStack

F32 = mybir.dt.float32
I32 = mybir.dt.int32
ALU = mybir.AluOpType
ACT = mybir.ActivationFunctionType
AX = mybir.AxisListType

P = 128
NBATCH, SEQ = 16, 256
TPB = SEQ // P
NT = NBATCH * TPB
H, D = 16, 8
WIN = 64
HP = 4
HQ = H // HP
NE, INTER, SHARED = 8, 176, 352
ROUTED = NE * INTER
FEAT = ROUTED + SHARED
FH, FD = 8, 64
INNER = FH * FD
HID = 341
DEPTH = 2
MASKED = -1e30
START = 1
RSQRT_MAGIC = 1597463007.0


def chunks(n, size=P):
    return [(a, min(size, n - a)) for a in range(0, n, size)]


def window_masks():
    q = np.arange(P)[:, None] % WIN
    k = np.arange(2 * WIN)[None, :]
    delta = q - k + WIN
    valid = (delta >= 0) & (delta <= WIN)
    first = valid & ((np.arange(P)[:, None] >= WIN) | (k >= WIN))
    return np.stack([first, valid], 1), delta


def shape_constants():
    valid, delta = window_masks()
    ffn_mask = np.where(valid, 0.0, MASKED).astype(np.float32)
    slopes = np.exp2(-(np.arange(H, dtype=np.float32) + 1.0) * 8.0 / H).astype(np.float32)
    bias = slopes[None, :, None] * delta[:, None, :].astype(np.float32)
    l0_table = np.where(valid[:, :, None, :], bias[:, None], MASKED).astype(np.float32)
    half = np.arange(0, FD, 2, dtype=np.float32)
    t = np.arange(SEQ, dtype=np.float32)
    freqs = t[:, None] * (np.float32(1.0) / np.float32(10000.0) ** (half / np.float32(FD)))[None, :]
    freqs = np.concatenate([freqs, freqs], -1).astype(np.float32)
    base = (half + np.float32(0.4 * FD)) / np.float32(1.4 * FD)
    power = (t - SEQ // 2) / np.float32(WIN // 2)
    scale = base[None, :] ** power[:, None]
    scale = np.concatenate([scale, scale], -1).astype(np.float32)
    sign = np.where(np.arange(FD) < FD // 2, -1.0, 1.0).astype(np.float32)
    cos, sin = np.cos(freqs), np.sin(freqs) * sign
    rot = np.stack([cos * scale * 8.0, sin * scale * 8.0, cos / scale, sin / scale], 1)
    rotary = rot.reshape(TPB, P, 4, FD).transpose(1, 0, 2, 3).astype(np.float32)
    select = np.zeros((NE, ROUTED), np.float32)
    select[np.arange(ROUTED) // INTER, np.arange(ROUTED)] = 1.0
    below = (np.arange(NE)[None, :] < np.arange(NE)[:, None]).astype(np.float32)
    return {
        "c_ident": np.eye(P, dtype=np.float32),
        "c_flip": np.eye(P, dtype=np.float32)[::-1].copy(),
        "c_l0_table": l0_table,
        "c_ffn_mask": ffn_mask,
        "c_rotary": rotary,
        "c_select": select,
        "c_below": np.broadcast_to(below.reshape(1, NE * NE), (P, NE * NE)).copy(),
    }


def build_kernel(nc, t, out):
    ctx = ExitStack()
    with ctx:
        X = ctx.enter_context(nc.sbuf_tensor("X", [P, NT, P], F32))
        Y = ctx.enter_context(nc.sbuf_tensor("Y", [P, NT, P], F32))
        S = ctx.enter_context(nc.sbuf_tensor("S", [P, NT, P], F32))
        ident = ctx.enter_context(nc.sbuf_tensor("ident", [P, P], F32))
        wdense = ctx.enter_context(nc.sbuf_tensor("wdense", [P, NT, NE], F32))
        ps = ctx.enter_context(nc.psum_tensor("ps", [P, 8, 512], F32))
        skew = nc.dram_tensor("skew_scratch", (H, 512), F32, kind="Internal").ap()

        load_inputs(nc, t, X, ident)
        layernorm(nc, "ln0", X, Y)
        router(nc, t, ps, ident, Y, wdense)
        head_attention(nc, "a0", True, t, ps, ident, Y, S, skew)
        experts(nc, t, ps, ident, X, Y, S, wdense)
        layernorm(nc, "ln1", X, Y)
        head_attention(nc, "a1", False, t, ps, ident, Y, S, skew)
        inner_layers(nc, t, ps, ident, Y)
        finish(nc, X, Y, S, out)


def load_inputs(nc, t, X, ident):
    with nc.semaphore("x_loaded") as x_loaded, nc.Block() as block:
        @block.sync
        def _(sp):
            xv = t["L0_attn_x"].rearrange("b (t p) e -> p (b t) e", p=P)
            for q in range(4):
                sp.dma_start(X[:, 8 * q:8 * q + 8, :], xv[:, 8 * q:8 * q + 8, :]).then_inc(x_loaded, 16)
            sp.dma_start(ident[:, :], t["c_ident"]).then_inc(x_loaded, 16)
            sp.wait_ge(x_loaded, 80)


def rsqrt(nc, dve, r, v, tmp):
    nc.vector.tensor_scalar(r.bitcast(I32), v.bitcast(I32), -0.5, RSQRT_MAGIC, ALU.mult, ALU.add)
    dve.drain()
    for _ in range(3):
        nc.vector.scalar_tensor_tensor(tmp, v, -0.5, r, ALU.mult, ALU.mult)
        dve.drain()
        nc.vector.tensor_tensor(tmp, tmp, r, ALU.mult)
        dve.drain()
        nc.vector.scalar_tensor_tensor(r, tmp, 1.5, r, ALU.add, ALU.mult)
        dve.drain()


def moments(nc, dve, st, mean, rstd, tmp, n):
    nc.vector.tensor_tensor(mean, st[:, :, 1], st[:, :, 4], ALU.add)
    nc.vector.tensor_tensor(tmp[:, 0, :], st[:, :, 1], st[:, :, 4], ALU.subtract)
    nc.vector.tensor_tensor(tmp[:, 1, :], st[:, :, 2], st[:, :, 5], ALU.add)
    dve.drain()
    nc.vector.tensor_scalar_mul(mean, mean, 0.5)
    nc.vector.scalar_tensor_tensor(tmp[:, 0, :], tmp[:, 0, :], 0.25, tmp[:, 0, :], ALU.mult, ALU.mult)
    nc.vector.tensor_scalar(tmp[:, 1, :], tmp[:, 1, :], 1.0 / P, 1e-5, ALU.mult, ALU.add)
    dve.drain()
    nc.vector.tensor_tensor(tmp[:, 0, :], tmp[:, 0, :], tmp[:, 1, :], ALU.add)
    dve.drain()
    rsqrt(nc, dve, rstd, tmp[:, 0, :], tmp[:, 1, :])


def layernorm(nc, name, X, Y):
    with ExitStack() as c:
        st = c.enter_context(nc.sbuf_tensor(name + "_st", [P, NT, 6], F32))
        mean = c.enter_context(nc.sbuf_tensor(name + "_mean", [P, NT], F32))
        rstd = c.enter_context(nc.sbuf_tensor(name + "_rstd", [P, NT], F32))
        tmp = c.enter_context(nc.sbuf_tensor(name + "_tmp", [P, 2, NT], F32))
        block = c.enter_context(nc.Block())

        @block.vector
        def _(dve):
            with dve.Fori(0, NT) as i:
                nc.vector.bn_stats(st[:, bass.ds(i, 1), :], X[:, bass.ds(i, 1), :])
            dve.drain()
            moments(nc, dve, st, mean[:, :], rstd[:, :], tmp, NT)
            nc.vector.tensor_tensor(Y[:], X[:], mean[:, :].unsqueeze(2).broadcast_to([P, NT, P]), ALU.subtract)
            dve.drain()
            nc.vector.tensor_tensor(Y[:], Y[:], rstd[:, :].unsqueeze(2).broadcast_to([P, NT, P]), ALU.mult)
            dve.drain()


def router(nc, t, ps, ident, Y, wdense):
    with ExitStack() as c:
        gw = c.enter_context(nc.sbuf_tensor("r_gw", [NE, P], F32))
        gwT = c.enter_context(nc.sbuf_tensor("r_gwT", [P, NE], F32))
        below = c.enter_context(nc.sbuf_tensor("r_below", [P, NE * NE], F32))
        xs = c.enter_context(nc.sbuf_tensor("r_xs", [P, 4, P], F32))
        xT = c.enter_context(nc.sbuf_tensor("r_xT", [P, 512], F32))
        lg = c.enter_context(nc.sbuf_tensor("r_lg", [P, NT, NE], F32))
        st = c.enter_context(nc.sbuf_tensor("r_st", [P, NT], F32))
        gt = c.enter_context(nc.sbuf_tensor("r_gt", [P, NT, NE, NE], F32))
        eq = c.enter_context(nc.sbuf_tensor("r_eq", [P, NT, NE, NE], F32))
        rank = c.enter_context(nc.sbuf_tensor("r_rank", [P, NT, NE], F32))
        sem = lambda n: c.enter_context(nc.semaphore("r_" + n))
        loaded, gate_T, gate_sb, staged, x_T, x_sb, logits, lg_sb, shifted, exped = map(sem, (
            "loaded", "gate_T", "gate_sb", "staged", "x_T", "x_sb", "logits", "lg_sb", "shifted", "exped"))
        block = c.enter_context(nc.Block())
        released = (x_T, x_sb, lg_sb, logits)
        ROUNDS = NT // 4

        @block.sync
        def _(sp):
            for s in released:
                sp.sem_inc(s, START)
            sp.dma_start(gw[:, :], t["L0_ffn_gate_w"]).then_inc(loaded, 16)
            sp.dma_start(below[:, :], t["c_below"]).then_inc(loaded, 16)

        @block.gpsimd
        def _(pool):
            with pool.Fori(0, ROUNDS) as i:
                pool.wait_ge(x_T, i + START)
                nc.gpsimd.tensor_copy(xs[:], Y[:, bass.ds(i * 4, 4), :]).then_inc(staged, 1)

        @block.tensor
        def _(pe):
            pe.wait_ge(loaded, 32)
            nc.tensor.transpose(ps[:, 0, 0:NE], gw[:, :], ident[0:NE, 0:NE]).then_inc(gate_T, 1)
            pe.wait_ge(gate_sb, 1)
            with pe.Fori(0, ROUNDS) as i:
                pe.wait_ge(staged, i + 1)
                pe.wait_ge(x_sb, i + START)
                for k in range(4):
                    last = nc.tensor.transpose(ps[:, 1, k * P:(k + 1) * P], xs[:, k, :], ident[:, :])
                last.then_inc(x_T, 1)
                pe.wait_ge(x_sb, i + 1 + START)
                pe.wait_ge(lg_sb, i + START)
                for k in range(4):
                    last = nc.tensor.matmul(ps[:, 2, k * NE:(k + 1) * NE], xT[:, k * P:(k + 1) * P], gwT[:, :],
                                            start=True, stop=True)
                last.then_inc(logits, 1)

        @block.scalar
        def _(act):
            act.wait_ge(gate_T, 1)
            nc.scalar.activation(gwT[:, :], ps[:, 0, 0:NE], ACT.Copy).then_inc(gate_sb, 1)
            with act.Fori(0, ROUNDS) as i:
                act.wait_ge(x_T, i + 1 + START)
                act.wait_ge(logits, i + START)
                nc.scalar.activation(xT[:, :], ps[:, 1, :], ACT.Copy).then_inc(x_sb, 1)
            act.wait_ge(shifted, 1)
            nc.scalar.activation(lg[:], lg[:], ACT.Exp).then_inc(exped, 1)

        @block.vector
        def _(dve):
            with dve.Fori(0, ROUNDS) as i:
                dve.wait_ge(logits, i + 1 + START)
                nc.vector.tensor_copy(lg[:, bass.ds(i * 4, 4), :],
                                      ps[:, 2, 0:4 * NE].rearrange("p (k e) -> p k e", e=NE)).then_inc(lg_sb, 1)
            dve.drain()
            bc = lambda a: a[:, :].unsqueeze(2).broadcast_to([P, NT, NE])
            nc.vector.tensor_reduce(st[:, :], lg[:], AX.X, ALU.max)
            dve.drain()
            nc.vector.tensor_tensor(lg[:], lg[:], bc(st), ALU.subtract).then_inc(shifted, 1)
            dve.wait_ge(exped, 1)
            nc.vector.tensor_reduce(st[:, :], lg[:], AX.X, ALU.add)
            dve.drain()
            nc.vector.reciprocal(st[:, :], st[:, :])
            dve.drain()
            nc.vector.tensor_tensor(lg[:], lg[:], bc(st), ALU.mult)
            dve.drain()
            other = lg[:].unsqueeze(2).broadcast_to([P, NT, NE, NE])
            own = lg[:].unsqueeze(3).broadcast_to([P, NT, NE, NE])
            lower = below[:, :].rearrange("p (a b) -> p a b", b=NE).unsqueeze(1).broadcast_to([P, NT, NE, NE])
            nc.vector.tensor_tensor(gt[:], other, own, ALU.is_gt)
            nc.vector.tensor_tensor(eq[:], other, own, ALU.is_equal)
            dve.drain()
            dve.wait_ge(loaded, 32)
            nc.vector.tensor_tensor(eq[:], eq[:], lower, ALU.mult)
            dve.drain()
            nc.vector.tensor_tensor(gt[:], gt[:], eq[:], ALU.add)
            dve.drain()
            nc.vector.tensor_reduce(rank[:], gt[:], AX.X, ALU.add)
            dve.drain()
            nc.vector.tensor_scalar(rank[:], rank[:], 1.5, None, ALU.is_lt)
            dve.drain()
            nc.vector.tensor_tensor(wdense[:], lg[:], rank[:], ALU.mult)
            dve.drain()
            nc.vector.tensor_reduce(st[:, :], wdense[:], AX.X, ALU.add)
            dve.drain()
            nc.vector.tensor_scalar(st[:, :], st[:, :], 1e-20, None, ALU.add)
            dve.drain()
            nc.vector.reciprocal(st[:, :], st[:, :])
            dve.drain()
            nc.vector.tensor_tensor(wdense[:], wdense[:], bc(st), ALU.mult)
            dve.drain()


def head_attention(nc, name, windowed, t, ps, ident, Y, S, skew):
    KW = 2 * WIN if windowed else SEQ
    HG = 1024 // KW
    GPT = H // HG
    G = TPB * GPT
    PAD = WIN if windowed else 0
    NBUF = 4
    SCALE = float(1.0 / np.sqrt(np.float32(D)))
    NVT = 2 if windowed else 1
    HEADS = "(rp rb jp jx d)" if windowed else "(rp jp rb jx d)"
    AXES = dict(rp=2, rb=2, jp=2, jx=2, d=D)

    def place(h):
        rp, m, n, jx = h >> 3, h >> 2 & 1, h >> 1 & 1, h & 1
        rb, jp = (m, n) if windowed else (n, m)
        return 32 * (2 * rp + rb), 2 * jp + jx
    VW = D + 1

    with ExitStack() as c:
        sb = lambda n, s: c.enter_context(nc.sbuf_tensor(name + "_" + n, s, F32))
        sem = lambda n: c.enter_context(nc.semaphore(name + "_" + n))
        wnat = sb("wnat", [P, 4, P])
        wqk = sb("wqk", [P, 2, HQ, HP, 32])
        wvT = sb("wvT", [P, P])
        woT = sb("woT", [P, P])
        table = sb("table", [P, TPB, H, KW])
        xs = sb("xs", [P, TPB, P])
        xT = sb("xT", [P, PAD + SEQ])
        qT = sb("qT", [P, HQ, SEQ])
        kT = sb("kT", [P, HQ, PAD + SEQ])
        V = sb("V", [P, NVT, TPB, H, VW])
        prob = sb("prob", [P, NBUF, HG, KW])
        nmax = sb("nmax", [P, NBUF, HG])
        probT = sb("probT", [P, 2, 1024])
        o = sb("o", [P, H, D])
        rden = sb("rden", [P, H])
        oT = sb("oT", [P, P])
        if not windowed:
            bqk = sb("bqk", [P, 2, HQ])
            bvo = sb("bvo", [P, 2, P])
            rel = sb("rel", [H, 257])
            ext = sb("ext", [H, 512])
            flip = sb("flip", [P, P])
            rel_loaded, rel_ext, rel_out, rel_in, flipped, turned = map(sem, ("rel_loaded", "rel_ext", "rel_out", "rel_in", "flipped", "turned"))
        (w_loaded, b_loaded, zeroed, wT_ps, wT_sb, staged, x_T, x_sb, q_ps, k_ps, v_ps, q_sb, k_sb, v_sb,
         scores, biased, max_done, shifted, exped, p_T, pT_sb, pv_done, o_sb, o_T, oT_sb, y_ps, y_sb) = map(sem, (
            "w_loaded", "b_loaded", "zeroed", "wT_ps", "wT_sb", "staged", "x_T", "x_sb", "q_ps", "k_ps", "v_ps",
            "q_sb", "k_sb", "v_sb", "scores", "biased", "max_done", "shifted", "exped", "p_T", "pT_sb",
            "pv_done", "o_sb", "o_T", "oT_sb", "y_ps", "y_sb"))
        block = c.enter_context(nc.Block())
        released = (x_T, y_sb, biased, pT_sb, o_sb)
        NWL = 64 if not windowed else 32
        last_of_tile = lambda g: 0 <= g < G and g % GPT == GPT - 1
        STEPS = range(G + 4)

        @block.sync
        def _(sp):
            for s in released:
                sp.sem_inc(s, START)
            if windowed:
                wi = t["L0_attn_w_in"].rearrange("(c p) e -> p c e", p=P)
                sp.dma_start(wnat[:, 0:3, :], wi).then_inc(w_loaded, 16)
                sp.dma_start(wnat[:, 3, :], t["L0_attn_w_out"]).then_inc(w_loaded, 16)
                sp.dma_start(table[:], t["c_l0_table"]).then_inc(b_loaded, 16)
            else:
                for j, w in enumerate(("Wq", "Wk", "Wv", "Wo")):
                    sp.dma_start(wnat[:, j, :], t["L1_attn_" + w]).then_inc(w_loaded, 16)
                sp.dma_start(rel[:, :], t["L1_attn_rel_bias"]).then_inc(rel_loaded, 16)
                sp.dma_start(flip[:, :], t["c_flip"]).then_inc(b_loaded, 16)
                sp.wait_ge(zeroed, 1)
                for j, b in enumerate(("bq", "bk")):
                    bh = t["L1_attn_" + b].rearrange(HEADS + " -> rp rb d jp jx", **AXES)
                    for a in range(HP):
                        for jp in range(2):
                            sp.dma_start(bqk[32 * a:32 * a + D, j, 2 * jp:2 * jp + 2], bh[a // 2, a % 2, :, jp, :],
                                         allow_slow_non_contiguous=True).then_inc(b_loaded, 16)
                for j, b in enumerate(("bv", "bo")):
                    sp.dma_start(bvo[:, j, :], t["L1_attn_" + b].unsqueeze(0).broadcast_to([P, P])).then_inc(b_loaded, 16)
                sp.wait_ge(rel_ext, 3)
                sp.dma_start(skew, ext[:, :]).then_inc(rel_out, 16)
                sp.wait_ge(rel_out, 16)
                for tile in range(TPB):
                    sp.wait_ge(flipped, tile)
                    src = bass.AP(tensor=skew.tensor, offset=skew.offset + P - P * tile,
                                  ap=[[1, P], [512, H], [1, SEQ]])
                    sp.dma_start(prob[:].rearrange("p n a k -> p (n a) k"), src).then_inc(rel_in, 16)

        NBL = 16 if windowed else 16 * 19

        @block.gpsimd
        def _(pool):
            nc.gpsimd.memset(wqk[:], 0.0).then_inc(zeroed, 1) if windowed else None
            if not windowed:
                nc.gpsimd.memset(bqk[:], 0.0).then_inc(zeroed, 1)
                nc.gpsimd.memset(wqk[:], 0.0).then_inc(zeroed, 1)
            nc.gpsimd.memset(V[:, :, :, :, D:VW], 1.0).then_inc(zeroed, 1)
            if windowed:
                nc.gpsimd.memset(xT[:, 0:PAD], 0.0).then_inc(zeroed, 1)
                nc.gpsimd.memset(kT[:, :, 0:PAD], 0.0).then_inc(zeroed, 1)
            with pool.Fori(0, NBATCH) as i:
                pool.wait_ge(x_T, i + START)
                nc.gpsimd.tensor_copy(xs[:], Y[:, bass.ds(i * TPB, TPB), :]).then_inc(staged, 1)
                for g in range(G):
                    pool.wait_ge(max_done, i * G + g + 1)
                    s = prob[:, g % NBUF]
                    nc.gpsimd.tensor_tensor(s, s, nmax[:, g % NBUF].unsqueeze(2).broadcast_to([P, HG, KW]),
                                            ALU.add).then_inc(shifted, 1)

        NZERO = 4 if windowed else 3

        @block.tensor
        def _(pe):
            pe.wait_ge(w_loaded, NWL)
            for j in range(4):
                last = nc.tensor.transpose(ps[:, 0, j * P:(j + 1) * P], wnat[:, j, :], ident[:, :])
            last.then_inc(wT_ps, 1)
            pe.wait_ge(wT_sb, 2 * HP + 2)
            if not windowed:
                pe.wait_ge(b_loaded, NBL)
                rows = prob[:].rearrange("p n a k -> p (n a k)")
                for tile in range(TPB):
                    pe.wait_ge(rel_in, 16 * (tile + 1))
                    pe.wait_ge(turned, tile)
                    for b in range(8):
                        last = nc.tensor.matmul(ps[:, b, :], flip[:, :], rows[:, b * 512:(b + 1) * 512], start=True, stop=True)
                    last.then_inc(flipped, 1)
                pe.wait_ge(turned, TPB)
            pe.wait_ge(zeroed, NZERO)
            with pe.Fori(0, NBATCH) as i:
                pe.wait_ge(staged, i + 1)
                pe.wait_ge(y_sb, i * TPB + START)
                for k in range(TPB):
                    last = nc.tensor.transpose(ps[:, 6, k * P:(k + 1) * P], xs[:, k, :], ident[:, :])
                last.then_inc(x_T, 1)
                pe.wait_ge(x_sb, i + 1)
                pe.wait_ge(biased, i * G + START)
                for w, done in ((0, q_ps), (1, k_ps)):
                    for j in range(HQ):
                        last = nc.tensor.matmul(ps[:, 2 * w + j // 2, (j % 2) * SEQ:(j % 2 + 1) * SEQ],
                                                wqk[:, w, j].rearrange("p a d -> p (a d)"), xT[:, PAD:PAD + SEQ],
                                                start=True, stop=True)
                    last.then_inc(done, 1)
                pe.wait_ge(pT_sb, i * G + START)
                for v in range(NVT):
                    for k in range(TPB):
                        at = PAD + P * k - WIN * v
                        last = nc.tensor.matmul(ps[:, 4, (v * TPB + k) * P:(v * TPB + k + 1) * P],
                                                xT[:, at:at + P], wvT[:, :], start=True, stop=True)
                last.then_inc(v_ps, 1)
                pe.wait_ge(q_sb, (i + 1) * HQ)
                pe.wait_ge(k_sb, (i + 1) * HQ)

                def score(g):
                    if g >= 2:
                        pe.wait_ge(biased, i * G + g - 1 + START)
                    tile, h0 = g // GPT, (g % GPT) * HG
                    for a in range(HG):
                        h = h0 + a
                        r, j = place(h)
                        bank, col = 2 * (g % 2) + a * KW // 512, a * KW % 512
                        if windowed:
                            for n in range(2):
                                blk = 2 * tile + n
                                last = nc.tensor.matmul(ps[WIN * n:WIN * (n + 1), bank, col:col + KW],
                                                        qT[r:r + D, j, WIN * blk:WIN * (blk + 1)],
                                                        kT[r:r + D, j, WIN * blk:WIN * blk + KW],
                                                        start=True, stop=True)
                        else:
                            last = nc.tensor.matmul(ps[:, bank, col:col + KW], qT[r:r + D, j, P * tile:P * (tile + 1)],
                                                    kT[r:r + D, j, :], start=True, stop=True)
                    last.then_inc(scores, 1)

                score(0)
                score(1)
                for g in STEPS:
                    if g + 2 < G:
                        score(g + 2)
                    if g < G:
                        if g == 0:
                            pe.wait_ge(v_sb, (i + 1) * NVT)
                        else:
                            pe.wait_ge(pT_sb, i * G + g + START)
                        pe.wait_ge(exped, i * G + g + 1)
                        flat = prob[:, g % NBUF].rearrange("p a k -> p (a k)")
                        for b in range(8):
                            last = nc.tensor.transpose(ps[:, 4 + b // 4, (b % 4) * P:(b % 4 + 1) * P],
                                                       flat[:, b * P:(b + 1) * P], ident[:, :])
                        last.then_inc(p_T, 1)
                    if 1 <= g <= G:
                        gp = g - 1
                        tile, h0 = gp // GPT, (gp % GPT) * HG
                        if gp % GPT == 0:
                            pe.wait_ge(o_sb, i * TPB + tile + START)
                        pe.wait_ge(pT_sb, i * G + gp + 1 + START)
                        for a in range(HG):
                            h = h0 + a
                            if windowed:
                                for n in range(2):
                                    last = nc.tensor.matmul(ps[WIN * n:WIN * (n + 1), 7, h * VW:(h + 1) * VW],
                                                            probT[:, gp % 2, a * P + WIN * n:a * P + WIN * (n + 1)],
                                                            V[:, 1 - n, tile, h, :], start=True, stop=True)
                            else:
                                for k in range(TPB):
                                    b = a * TPB + k
                                    last = nc.tensor.matmul(ps[:, 7, h * VW:(h + 1) * VW],
                                                            probT[:, gp % 2, b * P:(b + 1) * P], V[:, 0, k, h, :],
                                                            start=(k == 0), stop=(k == TPB - 1))
                        if last_of_tile(gp):
                            last.then_inc(pv_done, 1)
                    if last_of_tile(g - 2):
                        tile = (g - 2) // GPT
                        pe.wait_ge(o_sb, i * TPB + tile + 1 + START)
                        pe.wait_ge(y_sb, i * TPB + tile + START)
                        nc.tensor.transpose(ps[:, 6, 0:P], o[:].rearrange("p h d -> p (h d)"), ident[:, :]).then_inc(o_T, 1)
                    if last_of_tile(g - 3):
                        pe.wait_ge(oT_sb, i * TPB + (g - 3) // GPT + 1)
                        nc.tensor.matmul(ps[:, 6, 0:P], oT[:, :], woT[:, :], start=True, stop=True).then_inc(y_ps, 1)

        @block.scalar
        def _(act):
            act.wait_ge(wT_ps, 1)
            act.wait_ge(zeroed, NZERO)
            for w in range(2):
                for a in range(HP):
                    src = ps[:, 0, w * P:(w + 1) * P].rearrange("p " + HEADS + " -> p rp rb jp jx d", **AXES)
                    nc.scalar.activation(wqk[:, w, :, a, 0:D].rearrange("p (jp jx) d -> p jp jx d", jp=2),
                                         src[:, a // 2, a % 2], ACT.Copy).then_inc(wT_sb, 1)
            nc.scalar.activation(wvT[:, :], ps[:, 0, 2 * P:3 * P], ACT.Copy).then_inc(wT_sb, 1)
            nc.scalar.activation(woT[:, :], ps[:, 0, 3 * P:4 * P], ACT.Copy).then_inc(wT_sb, 1)
            if not windowed:
                act.wait_ge(b_loaded, NBL)
                nc.scalar.activation(bqk[:, 0, :], bqk[:, 0, :], ACT.Copy, scale=SCALE)
                for tile in range(TPB):
                    act.wait_ge(flipped, tile + 1)
                    nc.scalar.activation(table[:, tile], ps[:].rearrange("p b (a k) -> p (b a) k", k=KW), ACT.Copy).then_inc(turned, 1)
                act.drain()
            with act.Fori(0, NBATCH) as i:
                act.wait_ge(x_T, i + 1 + START)
                nc.scalar.activation(xT[:, PAD:PAD + SEQ], ps[:, 6, 0:SEQ], ACT.Copy).then_inc(x_sb, 1)
                act.wait_ge(q_ps, i + 1)
                for j in range(HQ):
                    src = ps[:, j // 2, (j % 2) * SEQ:(j % 2 + 1) * SEQ]
                    if windowed:
                        nc.scalar.activation(qT[:, j, :], src, ACT.Copy, scale=SCALE).then_inc(q_sb, 1)
                    else:
                        nc.scalar.activation(qT[:, j, :], src, ACT.Identity, scale=SCALE,
                                             bias=bqk[:, 0, j:j + 1]).then_inc(q_sb, 1)
                for g in STEPS:
                    if g < G:
                        act.wait_ge(shifted, i * G + g + 1)
                        nc.scalar.activation(prob[:, g % NBUF], prob[:, g % NBUF], ACT.Exp).then_inc(exped, 1)
                        act.wait_ge(p_T, i * G + g + 1)
                        nc.scalar.activation(probT[:, g % 2, :].rearrange("p (b n) -> p b n", b=2), ps[:, 4:6, :],
                                             ACT.Copy).then_inc(pT_sb, 1)
                    if last_of_tile(g - 2):
                        act.wait_ge(o_T, i * TPB + (g - 2) // GPT + 1)
                        nc.scalar.activation(oT[:, :], ps[:, 6, 0:P], ACT.Copy).then_inc(oT_sb, 1)

        @block.vector
        def _(dve):
            if not windowed:
                dve.wait_ge(rel_loaded, 16)
                nc.vector.tensor_copy(ext[:, 127:384], rel[:, ::-1]).then_inc(rel_ext, 1)
                nc.vector.tensor_copy(ext[:, 0:127], rel[:, 256:257].broadcast_to([H, 127])).then_inc(rel_ext, 1)
                nc.vector.tensor_copy(ext[:, 384:512], rel[:, 0:1].broadcast_to([H, 128])).then_inc(rel_ext, 1)
            dve.wait_ge(b_loaded, NBL)
            dve.wait_ge(zeroed, NZERO)
            if not windowed:
                dve.wait_ge(turned, TPB)
            with dve.Fori(0, NBATCH) as i:
                dve.wait_ge(k_ps, i + 1)
                for j in range(HQ):
                    src = ps[:, 2 + j // 2, (j % 2) * SEQ:(j % 2 + 1) * SEQ]
                    if windowed:
                        nc.vector.tensor_copy(kT[:, j, PAD:PAD + SEQ], src).then_inc(k_sb, 1)
                    else:
                        nc.vector.tensor_scalar(kT[:, j, :], src, bqk[:, 1, j:j + 1], None, ALU.add).then_inc(k_sb, 1)
                dve.wait_ge(v_ps, i + 1)
                for v in range(NVT):
                    src = ps[:, 4, v * TPB * P:(v + 1) * TPB * P].rearrange("p (k h d) -> p k h d", k=TPB, h=H)
                    dst = V[:, v, :, :, 0:D]
                    if windowed:
                        nc.vector.tensor_copy(dst, src).then_inc(v_sb, 1)
                    else:
                        bias = bvo[:, 0, :].rearrange("p (h d) -> p h d", h=H).unsqueeze(1).broadcast_to([P, TPB, H, D])
                        nc.vector.tensor_tensor(dst, src, bias, ALU.add).then_inc(v_sb, 1)
                for g in STEPS:
                    if g < G:
                        tile, h0 = g // GPT, (g % GPT) * HG
                        dve.wait_ge(scores, i * G + g + 1)
                        s = prob[:, g % NBUF]
                        src = ps[:, 2 * (g % 2):2 * (g % 2) + 2, :]
                        nc.vector.tensor_tensor(s.rearrange("p (b a) k -> p b (a k)", b=2), src,
                                                table[:, tile, h0:h0 + HG, :].rearrange("p (b a) k -> p b (a k)", b=2),
                                                ALU.add).then_inc(biased, 1)
                        dve.drain()
                        nc.vector.tensor_reduce(nmax[:, g % NBUF], s, AX.X, ALU.max, negate=True).then_inc(max_done, 1)
                    if last_of_tile(g - 2):
                        tile = (g - 2) // GPT
                        dve.wait_ge(pv_done, i * TPB + tile + 1)
                        acc = ps[:, 7, 0:H * VW].rearrange("p (h d) -> p h d", d=VW)
                        nc.vector.reciprocal(rden[:, :], acc[:, :, D])
                        dve.drain()
                        nc.vector.tensor_tensor(o[:], acc[:, :, 0:D], rden[:, :].unsqueeze(2).broadcast_to([P, H, D]),
                                                ALU.mult).then_inc(o_sb, 1)
                    if last_of_tile(g - 3):
                        tile = (g - 3) // GPT
                        dve.wait_ge(y_ps, i * TPB + tile + 1)
                        dst = S[:, bass.ds(i * TPB + tile, 1), :]
                        src = ps[:, 6, 0:P].unsqueeze(1)
                        if windowed:
                            nc.vector.tensor_copy(dst, src).then_inc(y_sb, 1)
                        else:
                            nc.vector.tensor_tensor(dst, src, bvo[:, 1:2, :], ALU.add).then_inc(y_sb, 1)


def experts(nc, t, ps, ident, X, Y, S, wdense):
    CH = chunks(FEAT)
    NC, NR = len(CH), ROUTED // P
    N = 512
    ROUNDS = NBATCH * SEQ // N
    with ExitStack() as c:
        sb = lambda n, s: c.enter_context(nc.sbuf_tensor("e_" + n, s, F32))
        sem = lambda n: c.enter_context(nc.semaphore("e_" + n))
        wgu = sb("wgu", [P, 2, FEAT])
        wd = sb("wd", [P, NC, P])
        sel = sb("sel", [NE, ROUTED])
        xs = sb("xs", [P, 4, P])
        ws = sb("ws", [P, 4, NE])
        xT = sb("xT", [P, N])
        wT = sb("wT", [NE, N])
        sg = sb("sg", [P, 2, N])
        h = sb("h", [P, 2, N])
        gT = sb("gT", [P, N])
        upd = sb("upd", [P, 4, P])
        (loaded, staged, x_T, x_sb, w_T, w_sb, gate_ps, up_ps, route_ps, gate_sb, h1, h2, down, down_all, out_sb,
         out_T, x_new) = map(sem, (
            "loaded", "staged", "x_T", "x_sb", "w_T", "w_sb", "gate_ps", "up_ps", "route_ps", "gate_sb", "h1", "h2",
            "down", "down_all", "out_sb", "out_T", "x_new"))
        block = c.enter_context(nc.Block())
        released = (w_T, x_new, h2, gate_sb, h1, out_sb, down, out_T)

        @block.sync
        def _(sp):
            for s in released:
                sp.sem_inc(s, START)
            for j, (w, sw) in enumerate((("wg", "swg"), ("wu", "swu"))):
                sp.dma_start(wgu[:, j, 0:ROUTED].rearrange("p (e i) -> p e i", e=NE),
                             t["L0_ffn_" + w].rearrange("e h i -> h e i")).then_inc(loaded, 16)
                sp.dma_start(wgu[:, j, ROUTED:FEAT], t["L0_ffn_" + sw]).then_inc(loaded, 16)
            wdf = t["L0_ffn_wd"].rearrange("e i h -> (e i) h")
            sp.dma_start(wd[:, 0:NR, :], wdf.rearrange("(c p) h -> p c h", p=P)).then_inc(loaded, 16)
            full = SHARED // P
            sp.dma_start(wd[:, NR:NR + full, :],
                         t["L0_ffn_swd"][0:full * P, :].rearrange("(c p) h -> p c h", p=P)).then_inc(loaded, 16)
            sp.dma_start(wd[0:SHARED - full * P, NR + full, :], t["L0_ffn_swd"][full * P:SHARED, :]).then_inc(loaded, 16)
            sp.dma_start(sel[:, :], t["c_select"]).then_inc(loaded, 16)

        @block.gpsimd
        def _(pool):
            with pool.Fori(0, ROUNDS) as i:
                pool.wait_ge(w_T, i + START)
                nc.gpsimd.tensor_copy(xs[:], Y[:, bass.ds(i * 4, 4), :]).then_inc(staged, 1)
                nc.gpsimd.tensor_copy(ws[:], wdense[:, bass.ds(i * 4, 4), :]).then_inc(staged, 1)

        @block.tensor
        def _(pe):
            pe.wait_ge(loaded, 16 * 8)
            with pe.Fori(0, ROUNDS) as i:
                pe.wait_ge(staged, 2 * i + 2)
                pe.wait_ge(x_new, i + START)
                for k in range(4):
                    last = nc.tensor.transpose(ps[:, 6, k * P:(k + 1) * P], xs[:, k, :], ident[:, :])
                last.then_inc(x_T, 1)
                pe.wait_ge(h2, i * NR + START)
                for k in range(4):
                    last = nc.tensor.transpose(ps[0:NE, 4, k * P:(k + 1) * P], ws[:, k, :], ident[:, :])
                last.then_inc(w_T, 1)
                pe.wait_ge(x_sb, i + 1)
                pe.wait_ge(w_sb, i + 1)
                for s in range(NC + 1):
                    if s < NC:
                        a, n = CH[s]
                        pe.wait_ge(gate_sb, i * NC + max(s - 1, 0) + START)
                        nc.tensor.matmul(ps[0:n, s % 2, :], wgu[:, 0, a:a + n], xT[:, :], start=True, stop=True).then_inc(gate_ps, 1)
                        pe.wait_ge(h1, i * NC + max(s - 1, 0) + START)
                        nc.tensor.matmul(ps[0:n, 2 + s % 2, :], wgu[:, 1, a:a + n], xT[:, :], start=True, stop=True).then_inc(up_ps, 1)
                        if s < NR:
                            if s >= 2:
                                pe.wait_ge(h2, i * NR + s - 1 + START)
                            nc.tensor.matmul(ps[:, 4 + s % 2, :], sel[:, a:a + n], wT[:, :], start=True, stop=True).then_inc(route_ps, 1)
                    if s >= 1:
                        b = s - 1
                        n = CH[b][1]
                        if b < NR:
                            pe.wait_ge(h2, i * NR + b + 1 + START)
                        else:
                            pe.wait_ge(h1, i * NC + b + 1 + START)
                        if b == 0:
                            pe.wait_ge(out_sb, i + START)
                        nc.tensor.matmul(ps[:, 7, :], wd[0:n, b, :], h[0:n, b % 2, :],
                                         start=(b == 0), stop=(b == NC - 1)).then_inc(down, 1)
                pe.wait_ge(out_sb, i + 1 + START)
                for k in range(4):
                    last = nc.tensor.transpose(ps[:, 6, k * P:(k + 1) * P], gT[:, k * P:(k + 1) * P], ident[:, :])
                last.then_inc(out_T, 1)

        @block.scalar
        def _(act):
            nc.scalar.preload_act_table(ACT.Silu)
            with act.Fori(0, ROUNDS) as i:
                act.wait_ge(x_T, i + 1)
                nc.scalar.activation(xT[:, :], ps[:, 6, :], ACT.Copy).then_inc(x_sb, 1)
                act.wait_ge(w_T, i + 1 + START)
                nc.scalar.activation(wT[:, :], ps[0:NE, 4, :], ACT.Copy).then_inc(w_sb, 1)
                for s, (a, n) in enumerate(CH):
                    act.wait_ge(gate_ps, i * NC + s + 1)
                    act.wait_ge(h1, i * NC + max(s - 1, 0) + START)
                    nc.scalar.activation(sg[0:n, s % 2, :], ps[0:n, s % 2, :], ACT.Silu).then_inc(gate_sb, 1)
                act.wait_ge(down, (i + 1) * NC + START)
                act.wait_ge(out_T, i + START)
                nc.scalar.activation(gT[:, :], ps[:, 7, :], ACT.Silu).then_inc(out_sb, 1)

        @block.vector
        def _(dve):
            with dve.Fori(0, ROUNDS) as i:
                for s, (a, n) in enumerate(CH):
                    dve.wait_ge(gate_sb, i * NC + s + 1 + START)
                    dve.wait_ge(up_ps, i * NC + s + 1)
                    dve.wait_ge(down, i * NC + max(s - 1, 0) + START)
                    hs = h[0:n, s % 2, :]
                    nc.vector.tensor_tensor(hs, ps[0:n, 2 + s % 2, :], sg[0:n, s % 2, :], ALU.mult).then_inc(h1, 1)
                    if s < NR:
                        dve.drain()
                        dve.wait_ge(route_ps, i * NR + s + 1)
                        nc.vector.tensor_tensor(hs, ps[0:n, 4 + s % 2, :], hs, ALU.mult).then_inc(h2, 1)
                dve.wait_ge(out_T, i + 1 + START)
                nc.vector.tensor_tensor(upd[:], ps[:, 6, :].rearrange("p (k e) -> p k e", k=4),
                                        S[:, bass.ds(i * 4, 4), :], ALU.mult)
                dve.drain()
                nc.vector.tensor_tensor(X[:, bass.ds(i * 4, 4), :], X[:, bass.ds(i * 4, 4), :], upd[:],
                                        ALU.add).then_inc(x_new, 1)
                dve.drain()


def inner_layers(nc, t, ps, ident, Y):
    KW = 2 * WIN
    N = 512
    MLP_ROUNDS = NBATCH * SEQ // N
    CH = chunks(HID)
    NC = len(CH)
    VW = FD + 1
    with ExitStack() as c:
        sb = lambda n, s: c.enter_context(nc.sbuf_tensor("i_" + n, s, F32))
        sem = lambda n: c.enter_context(nc.semaphore("i_" + n))
        mask = sb("mask", [P, TPB, KW])
        rotary = sb("rotary", [P, TPB, 4, FD])
        scales = sb("scales", [P, 2, FD])
        rot = sb("rot", [P, TPB, 4, FD])
        wqkv = sb("wqkv", [P, 3 * INNER])
        wo = sb("wo", [P, 4, P])
        w1 = sb("w1", [P, 2 * HID])
        w2 = sb("w2", [P, NC, P])
        b1 = sb("b1", [P, 2, NC])
        vecs = sb("vecs", [P, 3])
        hs = sb("hs", [P, TPB, P])
        hT = sb("hT", [P, WIN + SEQ])
        qk = sb("qk", [P, TPB, 2, FH, FD])
        rt = sb("rt", [P, TPB, 2, FH, FD])
        sq = sb("sq", [P, TPB, 2, FH, FD])
        ss = sb("ss", [P, 2 * FH])
        rn = sb("rn", [P, 2 * FH])
        rtmp = sb("rtmp", [P, 2 * FH])
        qT = sb("qT", [P, 4, SEQ])
        kT = sb("kT", [P, 4, WIN + SEQ])
        V = sb("V", [P, 2, TPB, FH, VW])
        prob = sb("prob", [P, TPB, FH, KW])
        nmax = sb("nmax", [P, TPB, FH])
        probT = sb("probT", [P, TPB, 1024])
        o = sb("o", [P, TPB, FH, FD])
        rden = sb("rden", [P, FH])
        oT = sb("oT", [P, TPB, 4, P])
        ms = sb("ms", [P, 4, P])
        st = sb("st", [P, 4, 6])
        mean = sb("mean", [P, 4])
        rstd = sb("rstd", [P, 4])
        mtmp = sb("mtmp", [P, 2, 4])
        mT = sb("mT", [P, N])
        ge = sb("ge", [P, 2, N])
        hm = sb("hm", [P, 2, N])
        zT = sb("zT", [P, N])
        (once, w_loaded, zeroed, rot_done, staged, h_T, h_sb, qk_ps, qk_sb, sq_sb, ss_done, cos_done, sin_done,
         qk_done, v_ps, v_sb, qk_T, q_sbT, k_sbT, scores, biased, max_done, shifted, exped, p_T, pT_sb, pv_done,
         o_sb, o_T, oT_sb, y_ps, y_att, m_staged, m_norm, m_T, m_sb, a_ps, g_ps, g_sb, hm_done, z_ps, z_sb, z_T,
         y_mlp) = map(sem, (
            "once", "w_loaded", "zeroed", "rot_done", "staged", "h_T", "h_sb", "qk_ps", "qk_sb", "sq_sb", "ss_done",
            "cos_done", "sin_done", "qk_done", "v_ps", "v_sb", "qk_T", "q_sbT", "k_sbT", "scores", "biased",
            "max_done", "shifted", "exped", "p_T", "pT_sb", "pv_done", "o_sb", "o_T", "oT_sb", "y_ps", "y_att",
            "m_staged", "m_norm", "m_T", "m_sb", "a_ps", "g_ps", "g_sb", "hm_done", "z_ps", "z_sb", "z_T", "y_mlp"))
        block = c.enter_context(nc.Block())
        released = (y_mlp, h_T, m_T, o_sb, y_att, biased, z_sb, hm_done, ss_done, qk_T, z_T, z_ps)
        HALF = P // 2
        NLOAD = 5 + 4 + 3 + 2

        @block.sync
        def _(sp):
            for s in released:
                sp.sem_inc(s, START)
            sp.dma_start(mask[:], t["c_ffn_mask"]).then_inc(once, 16)
            sp.dma_start(rotary[:], t["c_rotary"]).then_inc(once, 16)
            sp.wait_ge(zeroed, 5)
            with sp.Fori(0, DEPTH) as l:
                sp.wait_ge(y_mlp, l * MLP_ROUNDS + START)
                ly = bass.ds(l, 1)

                def load(dst, src):
                    sp.dma_start(dst, src, allow_slow_non_contiguous=True).then_inc(w_loaded, 16)

                load(wqkv[:, :], t["L1_ffn_wqkv"][ly].rearrange("o p f -> p (o f)"))
                load(wo[:], t["L1_ffn_wo"][ly].rearrange("o (c p) f -> p (o c) f", p=P))
                load(w1[:, :], t["L1_ffn_w1"][ly].rearrange("o p f -> p (o f)"))
                load(w2[:, 0:2, :], t["L1_ffn_w2"][ly, 0:2 * P, :].rearrange("o (c p) f -> p (o c) f", p=P))
                load(w2[0:HID - 2 * P, 2:3, :], t["L1_ffn_w2"][ly, 2 * P:HID, :].rearrange("o p f -> p o f"))
                for j in range(2):
                    at = j * HID
                    load(b1[:, j, 0:2], t["L1_ffn_b1"][ly, at:at + 2 * P].rearrange("o (c p) -> p (o c)", p=P))
                    load(b1[0:HID - 2 * P, j, 2:3], t["L1_ffn_b1"][ly, at + 2 * P:at + HID].rearrange("o p -> p o"))
                for j, v in enumerate(("ln_g", "ln_b", "b2")):
                    load(vecs[:, j:j + 1], t["L1_ffn_" + v][ly].rearrange("o p -> p o"))
                for j, v in enumerate(("q_scale", "k_scale")):
                    load(scales[:, j, :], t["L1_ffn_" + v][ly].broadcast_to([P, FD]))
                with sp.Fori(0, NBATCH) as b:
                    n = l * NBATCH + b
                    sp.wait_ge(h_T, n + START)
                    sp.dma_start(hs[:, :, 0:HALF], Y[:, bass.ds(b * TPB, TPB), 0:HALF]).then_inc(staged, 16)
                    sp.dma_start(hs[1:P, :, HALF:P], Y[0:P - 1, bass.ds(b * TPB, TPB), HALF:P]).then_inc(staged, 16)
                    sp.dma_start(hs[0:1, 1, HALF:P], Y[P - 1:P, bass.ds(b * TPB, 1), HALF:P].rearrange("p o e -> p (o e)")).then_inc(staged, 16)
                with sp.Fori(0, MLP_ROUNDS) as r:
                    n = l * MLP_ROUNDS + r
                    sp.wait_ge(m_T, n + START)
                    sp.wait_ge(y_att, (l + 1) * NBATCH * TPB + START)
                    sp.dma_start(ms[:, :, 0:HALF], Y[:, bass.ds(r * 4, 4), 0:HALF]).then_inc(m_staged, 16)
                    sp.dma_start(ms[1:P, :, HALF:P], Y[0:P - 1, bass.ds(r * 4, 4), HALF:P]).then_inc(m_staged, 16)
                    for k in range(2):
                        sp.dma_start(ms[0:1, 2 * k + 1, HALF:P],
                                     Y[P - 1:P, bass.ds(r * 4 + 2 * k, 1), HALF:P].rearrange("p o e -> p (o e)")).then_inc(m_staged, 16)

        @block.gpsimd
        def _(pool):
            nc.gpsimd.memset(hs[:, 0, :], 0.0).then_inc(zeroed, 1)
            nc.gpsimd.memset(ms[:], 0.0).then_inc(zeroed, 1)
            nc.gpsimd.memset(hT[:, 0:WIN], 0.0).then_inc(zeroed, 1)
            nc.gpsimd.memset(kT[:, :, 0:WIN], 0.0).then_inc(zeroed, 1)
            nc.gpsimd.memset(V[:, :, :, :, FD:VW], 1.0).then_inc(zeroed, 1)
            with pool.Fori(0, DEPTH) as l:
                with pool.Fori(0, NBATCH) as b:
                    n = l * NBATCH + b
                    for k in range(TPB):
                        m = n * TPB + k
                        pool.wait_ge(qk_sb, m + 1)
                        pool.wait_ge(sin_done, m + 1)
                        for j in range(2):
                            cb = rot[:, k, 2 * j, :].unsqueeze(1).broadcast_to([P, FH, FD])
                            nc.gpsimd.tensor_tensor(qk[:, k, j], qk[:, k, j], cb, ALU.mult)
                        pool.drain()
                        nc.gpsimd.tensor_tensor(qk[:, k], qk[:, k], rt[:, k], ALU.add).then_inc(cos_done, 1)
                    for k in range(TPB):
                        pool.wait_ge(max_done, n * TPB + k + 1)
                        nc.gpsimd.tensor_tensor(prob[:, k], prob[:, k],
                                                nmax[:, k].unsqueeze(2).broadcast_to([P, FH, KW]),
                                                ALU.add).then_inc(shifted, 1)

        @block.tensor
        def _(pe):
            pe.wait_ge(zeroed, 5)
            with pe.Fori(0, DEPTH) as l:
                with pe.Fori(0, NBATCH) as b:
                    n = l * NBATCH + b
                    pe.wait_ge(w_loaded, (l + 1) * NLOAD * 16)
                    pe.wait_ge(staged, (n + 1) * 48)
                    pe.wait_ge(o_sb, n * TPB + START)
                    for k in range(TPB):
                        last = nc.tensor.transpose(ps[:, 6, k * P:(k + 1) * P], hs[:, k, :], ident[:, :])
                    last.then_inc(h_T, 1)
                    pe.wait_ge(h_sb, n + 1)
                    for k in range(TPB):
                        m = n * TPB + k
                        here = hT[:, WIN + P * k:WIN + P * (k + 1)]
                        before = hT[:, P * k:P * (k + 1)]
                        if k > 0:
                            pe.wait_ge(v_sb, m)
                        nc.tensor.matmul(ps[:, 6, :], here, wqkv[:, 0:INNER], start=True, stop=True)
                        nc.tensor.matmul(ps[:, 7, :], here, wqkv[:, INNER:2 * INNER], start=True, stop=True).then_inc(qk_ps, 1)
                        pe.wait_ge(qk_sb, m + 1)
                        pe.wait_ge(sq_sb, m + 1)
                        nc.tensor.matmul(ps[:, 6, :], here, wqkv[:, 2 * INNER:], start=True, stop=True)
                        nc.tensor.matmul(ps[:, 7, :], before, wqkv[:, 2 * INNER:], start=True, stop=True).then_inc(v_ps, 1)
                    for k in range(TPB):
                        m = n * TPB + k
                        pe.wait_ge(qk_done, m + 1)
                        if k == 0:
                            pe.wait_ge(y_att, n * TPB + START)
                        else:
                            pe.wait_ge(k_sbT, m)
                            pe.wait_ge(q_sbT, m)
                        for j in range(2):
                            flat = qk[:, k, j].rearrange("p h d -> p (h d)")
                            for u in range(4):
                                last = nc.tensor.transpose(ps[:, 4 + j, u * P:(u + 1) * P], flat[:, u * P:(u + 1) * P], ident[:, :])
                        last.then_inc(qk_T, 1)
                        pe.wait_ge(zeroed, 5)
                        pe.wait_ge(q_sbT, m + 1)
                        pe.wait_ge(k_sbT, m + 1)
                        pe.wait_ge(biased, n * TPB + START)
                        for h in range(FH):
                            r, u = FD * (h % 2), h // 2
                            bank, col = 2 * k + h % 2, u * KW
                            for a in range(2):
                                blk = 2 * k + a
                                last = nc.tensor.matmul(ps[WIN * a:WIN * (a + 1), bank, col:col + KW],
                                                        qT[r:r + FD, u, WIN * blk:WIN * (blk + 1)],
                                                        kT[r:r + FD, u, WIN * blk:WIN * blk + KW], start=True, stop=True)
                        last.then_inc(scores, 1)
                    for k in range(TPB):
                        m = n * TPB + k
                        pe.wait_ge(exped, m + 1)
                        if k > 0:
                            pe.wait_ge(pT_sb, m)
                        flat = prob[:, k].rearrange("p a k -> p (a k)")
                        for u in range(8):
                            last = nc.tensor.transpose(ps[:, 4 + u // 4, (u % 4) * P:(u % 4 + 1) * P],
                                                       flat[:, u * P:(u + 1) * P], ident[:, :])
                        last.then_inc(p_T, 1)
                        pe.wait_ge(pT_sb, m + 1)
                        if k == 0:
                            pe.wait_ge(v_sb, m + 2)
                        else:
                            pe.wait_ge(o_sb, m + START)
                        for h in range(FH):
                            slot = h % 2 * 4 + h // 2
                            for a in range(2):
                                last = nc.tensor.matmul(ps[WIN * a:WIN * (a + 1), 6 + h // 4, (h % 4) * VW:(h % 4 + 1) * VW],
                                                        probT[:, k, slot * P + WIN * a:slot * P + WIN * (a + 1)],
                                                        V[:, 1 - a, k, h, :], start=True, stop=True)
                        last.then_inc(pv_done, 1)
                    for k in range(TPB):
                        m = n * TPB + k
                        pe.wait_ge(o_sb, m + 1 + START)
                        if k > 0:
                            pe.wait_ge(oT_sb, m)
                        flat = o[:, k].rearrange("p h d -> p (h d)")
                        for u in range(4):
                            last = nc.tensor.transpose(ps[:, 4, u * P:(u + 1) * P], flat[:, u * P:(u + 1) * P], ident[:, :])
                        last.then_inc(o_T, 1)
                        pe.wait_ge(oT_sb, m + 1)
                        if k > 0:
                            pe.wait_ge(y_att, m + START)
                        for u in range(4):
                            last = nc.tensor.matmul(ps[:, 5, 0:P], oT[:, k, u, :], wo[:, u, :], start=(u == 0), stop=(u == 3))
                        last.then_inc(y_ps, 1)
                with pe.Fori(0, MLP_ROUNDS) as r:
                    n = l * MLP_ROUNDS + r
                    pe.wait_ge(m_norm, n + 1)
                    pe.wait_ge(y_mlp, n + START)
                    pe.wait_ge(y_att, (l + 1) * NBATCH * TPB + START)
                    for k in range(4):
                        last = nc.tensor.transpose(ps[:, 6, k * P:(k + 1) * P], ms[:, k, :], ident[:, :])
                    last.then_inc(m_T, 1)
                    pe.wait_ge(m_sb, n + 1)
                    for s in range(NC + 1):
                        if s < NC:
                            a, w = CH[s]
                            pe.wait_ge(hm_done, n * NC + max(s - 1, 0) + START)
                            nc.tensor.matmul(ps[0:w, 2 + s % 2, :], w1[:, HID + a:HID + a + w], mT[:, :], start=True, stop=True).then_inc(g_ps, 1)
                            nc.tensor.matmul(ps[0:w, s % 2, :], w1[:, a:a + w], mT[:, :], start=True, stop=True).then_inc(a_ps, 1)
                        if s >= 1:
                            u = s - 1
                            w = CH[u][1]
                            pe.wait_ge(hm_done, n * NC + u + 1 + START)
                            if u == 0:
                                pe.wait_ge(z_sb, n + START)
                            nc.tensor.matmul(ps[:, 7, :], w2[0:w, u, :], hm[0:w, u % 2, :],
                                             start=(u == 0), stop=(u == NC - 1)).then_inc(z_ps, 1)
                    pe.wait_ge(z_sb, n + 1 + START)
                    for k in range(4):
                        last = nc.tensor.transpose(ps[:, 6, k * P:(k + 1) * P], zT[:, k * P:(k + 1) * P], ident[:, :])
                    last.then_inc(z_T, 1)

        @block.scalar
        def _(act):
            act.wait_ge(zeroed, 5)
            with act.Fori(0, DEPTH) as l:
                act.wait_ge(w_loaded, (l + 1) * NLOAD * 16)
                with act.Fori(0, NBATCH) as b:
                    n = l * NBATCH + b
                    act.wait_ge(h_T, n + 1 + START)
                    nc.scalar.activation(hT[:, WIN:WIN + SEQ], ps[:, 6, 0:SEQ], ACT.Copy).then_inc(h_sb, 1)
                    for k in range(TPB):
                        m = n * TPB + k
                        act.wait_ge(qk_ps, m + 1)
                        act.wait_ge(ss_done, n * TPB + START)
                        act.wait_ge(qk_T, n * TPB + START)
                        src = ps[:, 6:8, :].rearrange("p j (h d) -> p j h d", h=FH)
                        nc.scalar.activation(sq[:, k], src, ACT.Square).then_inc(sq_sb, 1)
                        nc.scalar.activation(qk[:, k], src, ACT.Copy).then_inc(qk_sb, 1)
                        act.wait_ge(v_ps, m + 1)
                        nc.scalar.activation(V[:, :, k, :, 0:FD], src, ACT.Copy).then_inc(v_sb, 1)
                    for k in range(TPB):
                        m = n * TPB + k
                        act.wait_ge(qk_T, m + 1 + START)
                        nc.scalar.activation(qT[:, :, P * k:P * (k + 1)], ps[:, 4, :].rearrange("p (u q) -> p u q", u=4),
                                             ACT.Copy).then_inc(q_sbT, 1)
                        nc.scalar.activation(kT[:, :, WIN + P * k:WIN + P * (k + 1)],
                                             ps[:, 5, :].rearrange("p (u q) -> p u q", u=4), ACT.Copy).then_inc(k_sbT, 1)
                    for k in range(TPB):
                        m = n * TPB + k
                        act.wait_ge(shifted, m + 1)
                        nc.scalar.activation(prob[:, k], prob[:, k], ACT.Exp).then_inc(exped, 1)
                        act.wait_ge(p_T, m + 1)
                        nc.scalar.activation(probT[:, k, :].rearrange("p (b q) -> p b q", b=2), ps[:, 4:6, :],
                                             ACT.Copy).then_inc(pT_sb, 1)
                    for k in range(TPB):
                        m = n * TPB + k
                        act.wait_ge(o_T, m + 1)
                        nc.scalar.activation(oT[:, k], ps[:, 4, :].rearrange("p (u q) -> p u q", u=4), ACT.Copy).then_inc(oT_sb, 1)
                with act.Fori(0, MLP_ROUNDS) as r:
                    n = l * MLP_ROUNDS + r
                    act.wait_ge(m_T, n + 1 + START)
                    nc.scalar.activation(mT[:, :], ps[:, 6, :], ACT.Identity, scale=vecs[:, 0:1], bias=vecs[:, 1:2]).then_inc(m_sb, 1)
                    for s, (a, w) in enumerate(CH):
                        act.wait_ge(g_ps, n * NC + s + 1)
                        act.wait_ge(hm_done, n * NC + max(s - 1, 0) + START)
                        nc.scalar.activation(ge[0:w, s % 2, :], ps[0:w, 2 + s % 2, :], ACT.Gelu,
                                             bias=b1[0:w, 1, s:s + 1]).then_inc(g_sb, 1)
                    act.wait_ge(z_ps, (n + 1) * NC + START)
                    act.wait_ge(z_T, n + START)
                    nc.scalar.activation(zT[:, :], ps[:, 7, :], ACT.Identity, bias=vecs[:, 2:3]).then_inc(z_sb, 1)

        @block.vector
        def _(dve):
            dve.wait_ge(once, 32)
            dve.wait_ge(zeroed, 5)
            HF = FD // 2
            with dve.Fori(0, DEPTH) as l:
                dve.wait_ge(w_loaded, (l + 1) * NLOAD * 16)
                for k in range(TPB):
                    for j in range(2):
                        nc.vector.tensor_tensor(rot[:, k, 2 * j, :], rotary[:, k, 2 * j, :], scales[:, j, :], ALU.mult)
                        nc.vector.tensor_tensor(rot[:, k, 2 * j + 1, 0:HF], rotary[:, k, 2 * j + 1, 0:HF], scales[:, j, HF:FD], ALU.mult)
                        nc.vector.tensor_tensor(rot[:, k, 2 * j + 1, HF:FD], rotary[:, k, 2 * j + 1, HF:FD], scales[:, j, 0:HF], ALU.mult)
                dve.drain()
                with dve.Fori(0, NBATCH) as b:
                    n = l * NBATCH + b
                    for k in range(TPB):
                        m = n * TPB + k
                        dve.wait_ge(sq_sb, m + 1)
                        nc.vector.tensor_reduce(ss[:, :], sq[:, k].rearrange("p j h d -> p (j h) d"), AX.X, ALU.add).then_inc(ss_done, 1)
                        dve.wait_ge(qk_sb, m + 1)
                        for j in range(2):
                            for lo, hi in ((0, HF), (HF, 0)):
                                sbc = rot[:, k, 2 * j + 1, lo:lo + HF].unsqueeze(1).broadcast_to([P, FH, HF])
                                last = nc.vector.tensor_tensor(rt[:, k, j, :, lo:lo + HF], qk[:, k, j, :, hi:hi + HF], sbc, ALU.mult)
                        last.then_inc(sin_done, 1)
                        dve.drain()
                        nc.vector.tensor_scalar(ss[:, :], ss[:, :], 1e-24, None, ALU.max)
                        dve.drain()
                        rsqrt(nc, dve, rn[:, :], ss[:, :], rtmp[:, :])
                        dve.wait_ge(cos_done, m + 1)
                        flat = qk[:, k].rearrange("p j h d -> p (j h) d")
                        nc.vector.tensor_tensor(flat, flat, rn[:, :].unsqueeze(2).broadcast_to([P, 2 * FH, FD]),
                                                ALU.mult).then_inc(qk_done, 1)
                    for k in range(TPB):
                        m = n * TPB + k
                        dve.wait_ge(scores, m + 1)
                        mb = mask[:, k:k + 1, :].broadcast_to([P, FH, KW])
                        nc.vector.tensor_tensor(prob[:, k], ps[:, 2 * k:2 * k + 2, :].rearrange("p b (a k) -> p (b a) k", k=KW), mb,
                                                ALU.add).then_inc(biased, 1)
                        dve.drain()
                        nc.vector.tensor_reduce(nmax[:, k], prob[:, k], AX.X, ALU.max, negate=True).then_inc(max_done, 1)
                    for k in range(TPB):
                        m = n * TPB + k
                        dve.wait_ge(pv_done, m + 1)
                        acc = ps[:, 6:8, 0:4 * VW].rearrange("p b (h d) -> p b h d", d=VW)
                        nc.vector.reciprocal(rden[:, :].rearrange("p (b h) -> p b h", b=2), acc[:, :, :, FD])
                        dve.drain()
                        nc.vector.tensor_tensor(o[:, k].rearrange("p (b h) d -> p b h d", b=2), acc[:, :, :, 0:FD],
                                                rden[:, :].rearrange("p (b h) -> p b h", b=2).unsqueeze(3).broadcast_to([P, 2, 4, FD]),
                                                ALU.mult).then_inc(o_sb, 1)
                        dve.drain()
                    for k in range(TPB):
                        m = n * TPB + k
                        dve.wait_ge(y_ps, m + 1)
                        dst = Y[:, bass.ds(b * TPB + k, 1), :]
                        nc.vector.tensor_tensor(dst, ps[:, 5, 0:P].unsqueeze(1), dst, ALU.add).then_inc(y_att, 1)
                with dve.Fori(0, MLP_ROUNDS) as r:
                    n = l * MLP_ROUNDS + r
                    dve.wait_ge(m_staged, (n + 1) * 64)
                    for k in range(4):
                        nc.vector.bn_stats(st[:, k, :], ms[:, k, :])
                    dve.drain()
                    moments(nc, dve, st, mean[:, :], rstd[:, :], mtmp, 4)
                    for k in range(4):
                        last = nc.vector.tensor_scalar(ms[:, k, :], ms[:, k, :], mean[:, k:k + 1], rstd[:, k:k + 1],
                                                       ALU.subtract, ALU.mult)
                    last.then_inc(m_norm, 1)
                    for s, (a, w) in enumerate(CH):
                        dve.wait_ge(a_ps, n * NC + s + 1)
                        dve.wait_ge(g_sb, n * NC + s + 1)
                        dve.wait_ge(z_ps, n * NC + max(s - 1, 0) + START)
                        nc.vector.scalar_tensor_tensor(hm[0:w, s % 2, :], ps[0:w, s % 2, :], b1[0:w, 0, s:s + 1],
                                                       ge[0:w, s % 2, :], ALU.add, ALU.mult).then_inc(hm_done, 1)
                    dve.wait_ge(z_T, n + 1 + START)
                    dst = Y[:, bass.ds(r * 4, 4), :]
                    nc.vector.tensor_tensor(dst, ps[:, 6, :].rearrange("p (k e) -> p k e", k=4), dst, ALU.add).then_inc(y_mlp, 1)


def finish(nc, X, Y, S, out):
    Q = NT // 4
    ov = out.rearrange("b (t p) e -> p (b t) e", p=P)
    with ExitStack() as c:
        sem = lambda n: c.enter_context(nc.semaphore("f_" + n))
        gated, product, total, stored = map(sem, ("gated", "product", "total", "stored"))
        block = c.enter_context(nc.Block())

        @block.scalar
        def _(act):
            for q in range(4):
                nc.scalar.activation(Y[:, q * Q:(q + 1) * Q, :], Y[:, q * Q:(q + 1) * Q, :], ACT.Silu).then_inc(gated, 1)

        @block.gpsimd
        def _(pool):
            for q in range(4):
                pool.wait_ge(gated, q + 1)
                s = slice(q * Q, (q + 1) * Q)
                nc.gpsimd.tensor_tensor(Y[:, s, :], Y[:, s, :], S[:, s, :], ALU.mult).then_inc(product, 1)

        @block.vector
        def _(dve):
            for q in range(4):
                dve.wait_ge(product, q + 1)
                s = slice(q * Q, (q + 1) * Q)
                nc.vector.tensor_tensor(X[:, s, :], Y[:, s, :], X[:, s, :], ALU.add).then_inc(total, 1)

        @block.sync
        def _(sp):
            for q in range(4):
                sp.wait_ge(total, q + 1)
                s = slice(q * Q, (q + 1) * Q)
                sp.dma_start(ov[:, s, :], X[:, s, :]).then_inc(stored, 16)
            sp.wait_ge(stored, 64)


_INS = ["L0_attn_x", "L0_attn_w_in", "L0_attn_w_out", "L0_ffn_gate_w", "L0_ffn_wg", "L0_ffn_wu", "L0_ffn_wd",
        "L0_ffn_swg", "L0_ffn_swu", "L0_ffn_swd", "L1_attn_Wq", "L1_attn_bq", "L1_attn_Wk", "L1_attn_bk",
        "L1_attn_Wv", "L1_attn_bv", "L1_attn_Wo", "L1_attn_bo", "L1_attn_rel_bias", "L1_ffn_wqkv",
        "L1_ffn_q_scale", "L1_ffn_k_scale", "L1_ffn_wo", "L1_ffn_ln_g", "L1_ffn_ln_b", "L1_ffn_w1", "L1_ffn_b1",
        "L1_ffn_w2", "L1_ffn_b2"]


def kernel(**inputs):
    import numpy as _np
    import concourse.bacc as _bacc
    from concourse import mybir as _mybir
    from concourse.bass_utils import run_bass_kernel_spmd as _run

    nc = _bacc.Bacc("TRN2", target_bir_lowering=False, num_devices=1)
    arrays, args = {}, {}
    named = [(name, inputs[name]) for name in _INS] + list(shape_constants().items())
    for name, value in named:
        a = _np.ascontiguousarray(value)
        arrays[f"in_{name}"] = a
        args[name] = nc.dram_tensor(f"in_{name}", a.shape, _mybir.dt.from_np(a.dtype), kind="ExternalInput").ap()
    out = nc.dram_tensor("out_0_dram", (NBATCH, SEQ, P), F32, kind="ExternalOutput").ap()
    build_kernel(nc, args, out)
    r = _run(nc, [arrays], core_ids=[0])
    return r.results[0]["out_0_dram"]
```

```python
import numpy as np
import concourse.bass as bass
from concourse import mybir
from contextlib import ExitStack

F32 = mybir.dt.float32
I32 = mybir.dt.int32
ALU = mybir.AluOpType
ACT = mybir.ActivationFunctionType
AX = mybir.AxisListType

P = 128
NBATCH, SEQ = 16, 256
TPB = SEQ // P
NT = NBATCH * TPB
H, D = 16, 8
WIN = 64
NE, INTER, SHARED = 8, 176, 352
ROUTED = NE * INTER
FEAT = ROUTED + SHARED
FH, FD = 8, 64
INNER = FH * FD
HID = 341
DEPTH = 2
MASKED = -1e30
START = 1
RSQRT_MAGIC = 1597463007.0


def chunks(n, size=P):
    return [(a, min(size, n - a)) for a in range(0, n, size)]


def window_masks():
    q = np.arange(P)[:, None] % WIN
    k = np.arange(2 * WIN)[None, :]
    delta = q - k + WIN
    valid = (delta >= 0) & (delta <= WIN)
    first = valid & ((np.arange(P)[:, None] >= WIN) | (k >= WIN))
    return np.stack([first, valid], 1), delta


def shape_constants():
    valid, delta = window_masks()
    ffn_mask = np.where(valid, 0.0, MASKED).astype(np.float32)
    ffn_mask[np.arange(P) < WIN] = np.roll(ffn_mask[np.arange(P) < WIN], WIN, -1)
    slopes = np.exp2(-(np.arange(H, dtype=np.float32) + 1.0) * 8.0 / H).astype(np.float32)
    bias = slopes[None, :, None] * delta[:, None, :].astype(np.float32)
    l0_table = np.where(valid[:, :, None, :], bias[:, None], MASKED).astype(np.float32)
    half = np.arange(0, FD, 2, dtype=np.float32)
    t = np.arange(SEQ, dtype=np.float32)
    freqs = t[:, None] * (np.float32(1.0) / np.float32(10000.0) ** (half / np.float32(FD)))[None, :]
    freqs = np.concatenate([freqs, freqs], -1).astype(np.float32)
    base = (half + np.float32(0.4 * FD)) / np.float32(1.4 * FD)
    power = (t - SEQ // 2) / np.float32(WIN // 2)
    scale = base[None, :] ** power[:, None]
    scale = np.concatenate([scale, scale], -1).astype(np.float32)
    sign = np.where(np.arange(FD) < FD // 2, -1.0, 1.0).astype(np.float32)
    cos, sin = np.cos(freqs), np.sin(freqs) * sign
    rot = np.stack([cos * scale * 8.0, sin * scale * 8.0, cos / scale, sin / scale], 1)
    rotary = rot.reshape(TPB, P, 4, FD).transpose(1, 0, 2, 3).astype(np.float32)
    select = np.zeros((NE, ROUTED), np.float32)
    select[np.arange(ROUTED) // INTER, np.arange(ROUTED)] = 1.0
    below = (np.arange(NE)[None, :] < np.arange(NE)[:, None]).astype(np.float32)
    return {
        "c_ident": np.eye(P, dtype=np.float32),
        "c_flip": np.eye(P, dtype=np.float32)[::-1].copy(),
        "c_l0_table": l0_table,
        "c_ffn_mask": ffn_mask,
        "c_rotary": rotary,
        "c_select": select,
        "c_heads": np.repeat(np.eye(H, dtype=np.float32), D, 0),
        "c_below": np.broadcast_to(below.reshape(1, NE * NE), (P, NE * NE)).copy(),
    }


def build_kernel(nc, t, out):
    ctx = ExitStack()
    with ctx:
        X = ctx.enter_context(nc.sbuf_tensor("X", [P, NT, P], F32))
        Y = ctx.enter_context(nc.sbuf_tensor("Y", [P, NT, P], F32))
        S = ctx.enter_context(nc.sbuf_tensor("S", [P, NT, P], F32))
        ident = ctx.enter_context(nc.sbuf_tensor("ident", [P, P], F32))
        wdense = ctx.enter_context(nc.sbuf_tensor("wdense", [P, NT, NE], F32))
        ps = ctx.enter_context(nc.psum_tensor("ps", [P, 8, 512], F32))
        skew = nc.dram_tensor("skew_scratch", (H, 512), F32, kind="Internal").ap()

        load_inputs(nc, t, X, ident)
        layernorm(nc, "ln0", X, Y)
        router(nc, t, ps, ident, Y, wdense)
        head_attention(nc, "a0", True, t, ps, ident, Y, S, skew)
        experts(nc, t, ps, ident, X, Y, S, wdense)
        layernorm(nc, "ln1", X, Y)
        head_attention(nc, "a1", False, t, ps, ident, Y, S, skew)
        inner_layers(nc, t, ps, ident, Y)
        finish(nc, X, Y, S, out)


def load_inputs(nc, t, X, ident):
    with nc.semaphore("x_loaded") as x_loaded, nc.Block() as block:
        @block.sync
        def _(sp):
            xv = t["L0_attn_x"].rearrange("b (t p) e -> p (b t) e", p=P)
            for q in range(4):
                sp.dma_start(X[:, 8 * q:8 * q + 8, :], xv[:, 8 * q:8 * q + 8, :]).then_inc(x_loaded, 16)
            sp.dma_start(ident[:, :], t["c_ident"]).then_inc(x_loaded, 16)
            sp.wait_ge(x_loaded, 80)


def rsqrt(nc, dve, r, v, tmp):
    nc.vector.tensor_scalar(r.bitcast(I32), v.bitcast(I32), -0.5, RSQRT_MAGIC, ALU.mult, ALU.add)
    dve.drain()
    for _ in range(3):
        nc.vector.scalar_tensor_tensor(tmp, v, -0.5, r, ALU.mult, ALU.mult)
        dve.drain()
        nc.vector.tensor_tensor(tmp, tmp, r, ALU.mult)
        dve.drain()
        nc.vector.scalar_tensor_tensor(r, tmp, 1.5, r, ALU.add, ALU.mult)
        dve.drain()


def moments(nc, dve, st, mean, rstd, tmp, n):
    nc.vector.tensor_tensor(mean, st[:, :, 1], st[:, :, 4], ALU.add)
    nc.vector.tensor_tensor(tmp[:, 0, :], st[:, :, 1], st[:, :, 4], ALU.subtract)
    nc.vector.tensor_tensor(tmp[:, 1, :], st[:, :, 2], st[:, :, 5], ALU.add)
    dve.drain()
    nc.vector.tensor_scalar_mul(mean, mean, 0.5)
    nc.vector.scalar_tensor_tensor(tmp[:, 0, :], tmp[:, 0, :], 0.25, tmp[:, 0, :], ALU.mult, ALU.mult)
    nc.vector.tensor_scalar(tmp[:, 1, :], tmp[:, 1, :], 1.0 / P, 1e-5, ALU.mult, ALU.add)
    dve.drain()
    nc.vector.tensor_tensor(tmp[:, 0, :], tmp[:, 0, :], tmp[:, 1, :], ALU.add)
    dve.drain()
    rsqrt(nc, dve, rstd, tmp[:, 0, :], tmp[:, 1, :])


def layernorm(nc, name, X, Y):
    with ExitStack() as c:
        st = c.enter_context(nc.sbuf_tensor(name + "_st", [P, NT, 6], F32))
        mean = c.enter_context(nc.sbuf_tensor(name + "_mean", [P, NT], F32))
        rstd = c.enter_context(nc.sbuf_tensor(name + "_rstd", [P, NT], F32))
        tmp = c.enter_context(nc.sbuf_tensor(name + "_tmp", [P, 2, NT], F32))
        block = c.enter_context(nc.Block())

        @block.vector
        def _(dve):
            with dve.Fori(0, NT) as i:
                nc.vector.bn_stats(st[:, bass.ds(i, 1), :], X[:, bass.ds(i, 1), :])
            dve.drain()
            moments(nc, dve, st, mean[:, :], rstd[:, :], tmp, NT)
            nc.vector.tensor_tensor(Y[:], X[:], mean[:, :].unsqueeze(2).broadcast_to([P, NT, P]), ALU.subtract)
            dve.drain()
            nc.vector.tensor_tensor(Y[:], Y[:], rstd[:, :].unsqueeze(2).broadcast_to([P, NT, P]), ALU.mult)
            dve.drain()


def router(nc, t, ps, ident, Y, wdense):
    with ExitStack() as c:
        gw = c.enter_context(nc.sbuf_tensor("r_gw", [NE, P], F32))
        gwT = c.enter_context(nc.sbuf_tensor("r_gwT", [P, NE], F32))
        below = c.enter_context(nc.sbuf_tensor("r_below", [P, NE * NE], F32))
        xs = c.enter_context(nc.sbuf_tensor("r_xs", [P, 4, P], F32))
        xT = c.enter_context(nc.sbuf_tensor("r_xT", [P, 512], F32))
        lg = c.enter_context(nc.sbuf_tensor("r_lg", [P, NT, NE], F32))
        st = c.enter_context(nc.sbuf_tensor("r_st", [P, NT], F32))
        gt = c.enter_context(nc.sbuf_tensor("r_gt", [P, NT, NE, NE], F32))
        eq = c.enter_context(nc.sbuf_tensor("r_eq", [P, NT, NE, NE], F32))
        rank = c.enter_context(nc.sbuf_tensor("r_rank", [P, NT, NE], F32))
        sem = lambda n: c.enter_context(nc.semaphore("r_" + n))
        loaded, gate_T, gate_sb, staged, x_T, x_sb, logits, lg_sb, shifted, exped = map(sem, (
            "loaded", "gate_T", "gate_sb", "staged", "x_T", "x_sb", "logits", "lg_sb", "shifted", "exped"))
        block = c.enter_context(nc.Block())
        released = (x_T, x_sb, lg_sb, logits)
        ROUNDS = NT // 4

        @block.sync
        def _(sp):
            for s in released:
                sp.sem_inc(s, START)
            sp.dma_start(gw[:, :], t["L0_ffn_gate_w"]).then_inc(loaded, 16)
            sp.dma_start(below[:, :], t["c_below"]).then_inc(loaded, 16)

        @block.gpsimd
        def _(pool):
            with pool.Fori(0, ROUNDS) as i:
                pool.wait_ge(x_T, i + START)
                nc.gpsimd.tensor_copy(xs[:], Y[:, bass.ds(i * 4, 4), :]).then_inc(staged, 1)

        @block.tensor
        def _(pe):
            pe.wait_ge(loaded, 32)
            nc.tensor.transpose(ps[:, 0, 0:NE], gw[:, :], ident[0:NE, 0:NE]).then_inc(gate_T, 1)
            pe.wait_ge(gate_sb, 1)
            with pe.Fori(0, ROUNDS) as i:
                pe.wait_ge(staged, i + 1)
                pe.wait_ge(x_sb, i + START)
                for k in range(4):
                    last = nc.tensor.transpose(ps[:, 1, k * P:(k + 1) * P], xs[:, k, :], ident[:, :])
                last.then_inc(x_T, 1)
                pe.wait_ge(x_sb, i + 1 + START)
                pe.wait_ge(lg_sb, i + START)
                for k in range(4):
                    last = nc.tensor.matmul(ps[:, 2, k * NE:(k + 1) * NE], xT[:, k * P:(k + 1) * P], gwT[:, :],
                                            start=True, stop=True)
                last.then_inc(logits, 1)

        @block.scalar
        def _(act):
            act.wait_ge(gate_T, 1)
            nc.scalar.activation(gwT[:, :], ps[:, 0, 0:NE], ACT.Copy).then_inc(gate_sb, 1)
            with act.Fori(0, ROUNDS) as i:
                act.wait_ge(x_T, i + 1 + START)
                act.wait_ge(logits, i + START)
                nc.scalar.activation(xT[:, :], ps[:, 1, :], ACT.Copy).then_inc(x_sb, 1)
            act.wait_ge(shifted, 1)
            nc.scalar.activation(lg[:], lg[:], ACT.Exp).then_inc(exped, 1)

        @block.vector
        def _(dve):
            with dve.Fori(0, ROUNDS) as i:
                dve.wait_ge(logits, i + 1 + START)
                nc.vector.tensor_copy(lg[:, bass.ds(i * 4, 4), :],
                                      ps[:, 2, 0:4 * NE].rearrange("p (k e) -> p k e", e=NE)).then_inc(lg_sb, 1)
            dve.drain()
            bc = lambda a: a[:, :].unsqueeze(2).broadcast_to([P, NT, NE])
            nc.vector.tensor_reduce(st[:, :], lg[:], AX.X, ALU.max)
            dve.drain()
            nc.vector.tensor_tensor(lg[:], lg[:], bc(st), ALU.subtract).then_inc(shifted, 1)
            dve.wait_ge(exped, 1)
            nc.vector.tensor_reduce(st[:, :], lg[:], AX.X, ALU.add)
            dve.drain()
            nc.vector.reciprocal(st[:, :], st[:, :])
            dve.drain()
            nc.vector.tensor_tensor(lg[:], lg[:], bc(st), ALU.mult)
            dve.drain()
            other = lg[:].unsqueeze(2).broadcast_to([P, NT, NE, NE])
            own = lg[:].unsqueeze(3).broadcast_to([P, NT, NE, NE])
            lower = below[:, :].rearrange("p (a b) -> p a b", b=NE).unsqueeze(1).broadcast_to([P, NT, NE, NE])
            nc.vector.tensor_tensor(gt[:], other, own, ALU.is_gt)
            nc.vector.tensor_tensor(eq[:], other, own, ALU.is_equal)
            dve.drain()
            dve.wait_ge(loaded, 32)
            nc.vector.tensor_tensor(eq[:], eq[:], lower, ALU.mult)
            dve.drain()
            nc.vector.tensor_tensor(gt[:], gt[:], eq[:], ALU.add)
            dve.drain()
            nc.vector.tensor_reduce(rank[:], gt[:], AX.X, ALU.add)
            dve.drain()
            nc.vector.tensor_scalar(rank[:], rank[:], 1.5, None, ALU.is_lt)
            dve.drain()
            nc.vector.tensor_tensor(wdense[:], lg[:], rank[:], ALU.mult)
            dve.drain()
            nc.vector.tensor_reduce(st[:, :], wdense[:], AX.X, ALU.add)
            dve.drain()
            nc.vector.tensor_scalar(st[:, :], st[:, :], 1e-20, None, ALU.add)
            dve.drain()
            nc.vector.reciprocal(st[:, :], st[:, :])
            dve.drain()
            nc.vector.tensor_tensor(wdense[:], wdense[:], bc(st), ALU.mult)
            dve.drain()


def head_attention(nc, name, windowed, t, ps, ident, Y, S, skew):
    KW = 2 * WIN if windowed else SEQ
    HG = 1024 // KW
    GPT = H // HG
    G = TPB * GPT
    PAD = WIN if windowed else 0
    NBUF = 4
    SCALE = float(1.0 / np.sqrt(np.float32(D)))
    NVT = 2 if windowed else 1
    HB = 512 // KW
    QG = 4
    NQ = H // QG

    with ExitStack() as c:
        sb = lambda n, s: c.enter_context(nc.sbuf_tensor(name + "_" + n, s, F32))
        sem = lambda n: c.enter_context(nc.semaphore(name + "_" + n))
        wnat = sb("wnat", [P, 4, P])
        wT = sb("wT", [P, 4, P])
        heads = sb("heads", [P, H])
        table = sb("table", [P, TPB, H, KW])
        xs = sb("xs", [P, TPB, P])
        xT = sb("xT", [P, PAD + SEQ])
        qT = sb("qT", [P, 2, SEQ])
        kT = sb("kT", [P, SEQ])
        kM = sb("kM", [P, 2, H, PAD + SEQ])
        V = sb("V", [P, 2, NVT, TPB, NQ, QG, 40])
        prob = sb("prob", [P, NBUF, HG, KW])
        nmax = sb("nmax", [P, NBUF, HG])
        den = sb("den", [P, NBUF, HG])
        probT = sb("probT", [P, 2, 1024])
        oT = sb("oT", [P, P])
        bvo = sb("bvo", [P, 2, P])
        if not windowed:
            bqk = sb("bqk", [P, 2])
            rel = sb("rel", [H, 257])
            ext = sb("ext", [H, 512])
            flip = sb("flip", [P, P])
            rel_loaded, rel_ext, rel_out, rel_in, flipped, turned, bq_scaled = map(sem, (
                "rel_loaded", "rel_ext", "rel_out", "rel_in", "flipped", "turned", "bq_scaled"))
        (w_loaded, b_loaded, zeroed, wT_ps, wT_sb, staged, aux_ps, aux_free, masked, scores, biased, max_done,
         exped, inverted, normed, p_T, pT_sb, pv_done, o_sb) = map(sem, (
            "w_loaded", "b_loaded", "zeroed", "wT_ps", "wT_sb", "staged", "aux_ps", "aux_free", "masked", "scores",
            "biased", "max_done", "exped", "inverted", "normed", "p_T", "pT_sb", "pv_done", "o_sb"))
        block = c.enter_context(nc.Block())
        NWL = 64 if not windowed else 32

        if windowed:
            AHEAD = 2
            FRONT = [(0, "A", "x"), (0, "B", "qk"), (1, "C", "v")]
            MASKS = {1: (0, 1), 2: (2, 3)}
        else:
            AHEAD = 3
            FRONT = [(0, "B", "x"), (1, "B", "qk"), (3, "B", "v")]
            MASKS = {2: (0,), 3: (1,), 4: (2,), 5: (3,)}
        JOBS = [(g, s, kind, -1, 0) for g, s, kind in FRONT]
        for tile in range(TPB):
            at = (tile + 1) * GPT - 1 + 2
            JOBS.append((at % G, "C", "y", at // G, tile))
        JOBS.sort(key=lambda j: (j[0], j[1], j[2]))

        def has(i, job):
            return not isinstance(i, int) or 0 <= i - job[3] < NBATCH

        def jobs_before(i):
            if isinstance(i, int):
                return len(FRONT) + sum(has(j, job) for j in range(i) for job in JOBS)
            return i * len(JOBS) + (jobs_before(1) - len(JOBS))

        def jobs_at(i, g, slots):
            count = 0
            for job in JOBS:
                if has(i, job):
                    if job[0] == g and job[1] in slots:
                        yield jobs_before(i) + count, job[2], i - job[3], job[4]
                    count += 1

        def job_of(i, kind):
            if isinstance(i, int) and i == 0:
                return [job[2] for job in FRONT].index(kind) + 1
            return jobs_before(i - 1) + [job[2] for job in JOBS if has(i - 1, job)].index(kind) + 1

        def sequences(eng, part):
            part(0, 0)
            with eng.Fori(0, (NBATCH - 2) // 2) as r:
                part(r * 2 + 1, 1)
                part(r * 2 + 2, 0)
            part(NBATCH - 1, 1)
            part(NBATCH, 0)

        def after(eng, signal, count):
            if not isinstance(count, int) or count > 0:
                eng.wait_ge(signal, count)

        def group_at(i, g, ahead):
            at = g + ahead
            return i + at // G, at % G, i * G + at

        def exists(i):
            return not isinstance(i, int) or 0 <= i < NBATCH

        NBL = 32 if windowed else 16 * 6

        @block.sync
        def _(sp):
            if windowed:
                wi = t["L0_attn_w_in"].rearrange("(c p) e -> p c e", p=P)
                sp.dma_start(wnat[:, 0:3, :], wi).then_inc(w_loaded, 16)
                sp.dma_start(wnat[:, 3, :], t["L0_attn_w_out"]).then_inc(w_loaded, 16)
                sp.dma_start(heads[:, :], t["c_heads"]).then_inc(b_loaded, 16)
                sp.dma_start(table[:], t["c_l0_table"]).then_inc(b_loaded, 16)
            else:
                sp.dma_start(rel[:, :], t["L1_attn_rel_bias"]).then_inc(rel_loaded, 16)
                for j, w in enumerate(("Wq", "Wk", "Wv", "Wo")):
                    sp.dma_start(wnat[:, j, :], t["L1_attn_" + w]).then_inc(w_loaded, 16)
                sp.dma_start(heads[:, :], t["c_heads"]).then_inc(b_loaded, 16)
                sp.dma_start(flip[:, :], t["c_flip"]).then_inc(b_loaded, 16)
                for j, b in enumerate(("bq", "bk")):
                    sp.dma_start(bqk[:, j:j + 1], t["L1_attn_" + b].unsqueeze(1),
                                 allow_slow_non_contiguous=True).then_inc(b_loaded, 16)
                for j, b in enumerate(("bv", "bo")):
                    sp.dma_start(bvo[:, j, :], t["L1_attn_" + b].unsqueeze(0).broadcast_to([P, P])).then_inc(b_loaded, 16)
                sp.wait_ge(rel_ext, 3)
                sp.dma_start(skew, ext[:, :]).then_inc(rel_out, 16)
                sp.wait_ge(rel_out, 16)
                for tile in range(TPB):
                    sp.wait_ge(flipped, tile) if tile else None
                    src = bass.AP(tensor=skew.tensor, offset=skew.offset + P - P * tile,
                                  ap=[[1, P], [512, H], [1, SEQ]])
                    sp.dma_start(prob[:].rearrange("p n a k -> p (n a) k"), src).then_inc(rel_in, 16)

            def stage(i):
                sp.dma_start(xs[:], Y[:, bass.ds(i * TPB, TPB), :]).then_inc(staged, 16)

            stage(0)
            for i in range(1, 3):
                sp.wait_ge(aux_ps, job_of(i - 1, "x"))
                stage(i)
            with sp.Fori(3, NBATCH) as i:
                sp.wait_ge(aux_ps, job_of(i - 1, "x"))
                stage(i)
            sp.wait_ge(staged, 16 * NBATCH)

        NZERO = 3 if windowed else 1

        @block.gpsimd
        def _(pool):
            nc.gpsimd.memset(V[:], 0.0).then_inc(zeroed, 1)
            if windowed:
                nc.gpsimd.memset(xT[:, 0:PAD], 0.0).then_inc(zeroed, 1)
                nc.gpsimd.memset(kM[:, :, :, 0:PAD], 0.0).then_inc(zeroed, 1)

            def normalise(n, slot):
                pool.wait_ge(inverted, n + 1)
                s = prob[:, slot]
                nc.gpsimd.tensor_tensor(s, s, den[:, slot].unsqueeze(2).broadcast_to([P, HG, KW]),
                                        ALU.mult).then_inc(normed, 1)

            def part(i, parity):
                for g in range(G):
                    seq, gg, n = group_at(i, g, AHEAD - 1)
                    if exists(seq):
                        normalise(n, gg % NBUF)

            for g in range(AHEAD - 1):
                normalise(g, g)
            sequences(pool, part)

        @block.tensor
        def _(pe):
            pe.wait_ge(w_loaded, NWL)
            for j in range(4):
                last = nc.tensor.transpose(ps[:, 0, j * P:(j + 1) * P], wnat[:, j, :], ident[:, :])
            last.then_inc(wT_ps, 1)
            pe.wait_ge(wT_sb, 1)
            if not windowed:
                pe.wait_ge(b_loaded, NBL)
                rows = prob[:].rearrange("p n a k -> p (n a k)")
                for tile in range(TPB):
                    pe.wait_ge(rel_in, 16 * (tile + 1))
                    after(pe, turned, tile)
                    for b in range(8):
                        last = nc.tensor.matmul(ps[:, b, :], flip[:, :], rows[:, b * 512:(b + 1) * 512], start=True, stop=True)
                    last.then_inc(flipped, 1)
                pe.wait_ge(turned, TPB)
            pe.wait_ge(zeroed, NZERO)

            def job(before, kind, i, parity, tile):
                after(pe, aux_free, before)
                if kind == "x":
                    pe.wait_ge(staged, 16 * (i + 1))
                    for k in range(TPB):
                        last = nc.tensor.transpose(ps[:, 6, k * P:(k + 1) * P], xs[:, k, :], ident[:, :])
                elif kind == "qk":
                    for j in range(2):
                        last = nc.tensor.matmul(ps[:, 6, j * SEQ:(j + 1) * SEQ], wT[:, j, :], xT[:, PAD:PAD + SEQ],
                                                start=True, stop=True)
                elif kind == "v":
                    for v in range(NVT):
                        for k in range(TPB):
                            at = PAD + P * k - WIN * v
                            last = nc.tensor.matmul(ps[:, 6, (v * TPB + k) * P:(v * TPB + k + 1) * P],
                                                    xT[:, at:at + P], wT[:, 2, :], start=True, stop=True)
                else:
                    pe.wait_ge(o_sb, i * TPB + tile + 1)
                    last = nc.tensor.matmul(ps[:, 6, 0:P], oT[:, :], wT[:, 3, :], start=True, stop=True)
                last.then_inc(aux_ps, 1)

            def score(i, g, n, parity, banks):
                tile, h0 = g // GPT, (g % GPT) * HG
                if 0 in banks:
                    after(pe, biased, n - 1)
                    after(pe, masked, i * NQ + (h0 + HG) // QG)
                for b in banks:
                    h, bank = h0 + b * HB, 2 * (g % 2) + b
                    if windowed:
                        for half in range(2):
                            at = WIN * (2 * tile + half)
                            last = nc.tensor.matmul(ps[WIN * half:WIN * (half + 1), bank, :], qT[:, parity, at:at + WIN],
                                                    kM[:, parity, h:h + HB, at:at + KW], start=True, stop=True)
                    else:
                        last = nc.tensor.matmul(ps[:, bank, :], qT[:, parity, P * tile:P * (tile + 1)],
                                                kM[:, parity, h:h + HB, :], start=True, stop=True)
                if 1 in banks:
                    last.then_inc(scores, 1)

            def transposes(g, n):
                after(pe, pT_sb, n)
                pe.wait_ge(normed, n + 1)
                flat = prob[:, g % NBUF].rearrange("p a k -> p (a k)")
                for b in range(8):
                    last = nc.tensor.transpose(ps[:, 4 + b // 4, (b % 4) * P:(b % 4 + 1) * P],
                                               flat[:, b * P:(b + 1) * P], ident[:, :])
                last.then_inc(p_T, 1)

            def values(parity, v, k, h):
                group = V[:, parity, v, k, h // QG].rearrange("p x d -> p (x d)")
                return group[:, 32 * (h % QG):32 * (h % QG) + 32]

            def sums(i, g, n, parity):
                tile, h0 = g // GPT, (g % GPT) * HG
                if g % GPT == 0:
                    after(pe, o_sb, i * TPB + tile)
                if g == 0:
                    pe.wait_ge(aux_free, job_of(i, "v"))
                pe.wait_ge(pT_sb, n + 1)
                for q in range(HG // QG):
                    rows = slice(32 * (h0 // QG + q), 32 * (h0 // QG + q + 1))
                    if windowed:
                        for half in range(2):
                            for x in range(QG):
                                a = q * QG + x
                                last = nc.tensor.matmul(ps[rows, 7, WIN * half:WIN * (half + 1)],
                                                        values(parity, 1 - half, tile, h0 + a),
                                                        probT[:, g % 2, a * P + WIN * half:a * P + WIN * (half + 1)],
                                                        start=(x == 0), stop=(x == QG - 1))
                    else:
                        for x in range(QG):
                            for k in range(TPB):
                                b = (q * QG + x) * TPB + k
                                last = nc.tensor.matmul(ps[rows, 7, 0:P], values(parity, 0, k, h0 + q * QG + x),
                                                        probT[:, g % 2, b * P:(b + 1) * P],
                                                        start=(x == 0 and k == 0), stop=(x == QG - 1 and k == TPB - 1))
                if g % GPT == GPT - 1:
                    last.then_inc(pv_done, 1)

            def part(i, parity):
                for g in range(G):
                    def small(slots):
                        for before, kind, seq, tile in jobs_at(i, g, slots):
                            job(before, kind, seq, parity ^ (kind != "y"), tile)

                    seq, gg, n = group_at(i, g, AHEAD)
                    par = parity ^ (g + AHEAD >= G)
                    small("A")
                    if exists(seq):
                        score(seq, gg, n, par, (0,))
                    small("B")
                    if exists(seq):
                        score(seq, gg, n, par, (1,))
                    small("C")
                    if exists(i):
                        transposes(g, i * G + g)
                    small("D")
                    seq, gg, n = group_at(i, g, -1)
                    if exists(seq):
                        sums(seq, gg, n, parity ^ (g == 0))
                    small("E")

            for before, (_, _, kind) in enumerate(FRONT):
                job(before, kind, 0, 0, 0)
            for g in range(AHEAD):
                score(0, g, g, 0, (0, 1))
            sequences(pe, part)

        @block.scalar
        def _(act):
            nc.scalar.preload_act_table(ACT.Exp)
            act.wait_ge(wT_ps, 1)
            act.wait_ge(zeroed, NZERO)
            nc.scalar.activation(wT[:], ps[:, 0, :].rearrange("p (c e) -> p c e", c=4), ACT.Copy).then_inc(wT_sb, 1)
            if not windowed:
                act.wait_ge(b_loaded, NBL)
                for tile in range(TPB):
                    act.wait_ge(flipped, tile + 1)
                    nc.scalar.activation(table[:, tile], ps[:].rearrange("p b (a k) -> p (b a) k", k=KW), ACT.Copy).then_inc(turned, 1)

            def job(before, kind, parity):
                if kind == "x":
                    act.wait_ge(aux_ps, before + 1)
                    nc.scalar.activation(xT[:, PAD:PAD + SEQ], ps[:, 6, 0:SEQ], ACT.Copy).then_inc(aux_free, 1)

            def exp(n, slot):
                act.wait_ge(max_done, n + 1)
                for a in range(HG):
                    last = nc.scalar.activation(prob[:, slot, a, :], prob[:, slot, a, :], ACT.Exp,
                                                bias=nmax[:, slot, a:a + 1], accum_out=den[:, slot, a:a + 1])
                last.then_inc(exped, 1)

            def copy_sums(count):
                act.wait_ge(pv_done, count)
                nc.scalar.activation(oT[:, :], ps[:, 7, 0:P], ACT.Copy).then_inc(o_sb, 1)

            def part(i, parity):
                for g in range(G):
                    seq, gg, _ = group_at(i, g, -2)
                    if gg % GPT == GPT - 1 and exists(seq):
                        copy_sums(seq * TPB + gg // GPT + 1)
                    for before, kind, _, _ in jobs_at(i, g, "A"):
                        job(before, kind, parity ^ (kind != "y"))
                    seq, gg, n = group_at(i, g, AHEAD - 1)
                    if exists(seq):
                        exp(n, gg % NBUF)
                    for before, kind, _, _ in jobs_at(i, g, "BC"):
                        job(before, kind, parity ^ (kind != "y"))
                    if exists(i):
                        n = i * G + g
                        act.wait_ge(p_T, n + 1)
                        nc.scalar.activation(probT[:, g % 2, :].rearrange("p (b n) -> p b n", b=2), ps[:, 4:6, :],
                                             ACT.Copy).then_inc(pT_sb, 1)
                    for before, kind, _, _ in jobs_at(i, g, "DE"):
                        job(before, kind, parity ^ (kind != "y"))

            for before, (_, _, kind) in enumerate(FRONT):
                job(before, kind, 0)
            for g in range(AHEAD - 1):
                exp(g, g)
            sequences(act, part)

        @block.vector
        def _(dve):
            if not windowed:
                dve.wait_ge(rel_loaded, 16)
                nc.vector.tensor_copy(ext[:, 127:384], rel[:, ::-1]).then_inc(rel_ext, 1)
                nc.vector.tensor_copy(ext[:, 0:127], rel[:, 256:257].broadcast_to([H, 127])).then_inc(rel_ext, 1)
                nc.vector.tensor_copy(ext[:, 384:512], rel[:, 0:1].broadcast_to([H, 128])).then_inc(rel_ext, 1)
            dve.wait_ge(b_loaded, NBL)
            dve.wait_ge(zeroed, NZERO)
            if not windowed:
                dve.wait_ge(turned, TPB)

            def job(before, kind, i, parity, tile):
                if kind == "x":
                    return
                dve.wait_ge(aux_ps, before + 1)
                if kind == "qk":
                    q, k = ps[:, 6, 0:SEQ], ps[:, 6, SEQ:2 * SEQ]
                    if windowed:
                        nc.vector.tensor_scalar_mul(qT[:, parity, :], q, SCALE)
                        last = nc.vector.tensor_copy(kT[:, :], k)
                    else:
                        nc.vector.tensor_scalar(qT[:, parity, :], q, bqk[:, 0:1], SCALE, ALU.add, ALU.mult)
                        last = nc.vector.tensor_scalar(kT[:, :], k, bqk[:, 1:2], None, ALU.add)
                elif kind == "v":
                    for v in range(NVT):
                        for k in range(TPB):
                            split = lambda a: a.rearrange("p (g x d) -> p g x d", g=NQ, x=QG)
                            src = split(ps[:, 6, (v * TPB + k) * P:(v * TPB + k + 1) * P])
                            dst = V[:, parity, v, k, :, :, 0:D]
                            if windowed:
                                last = nc.vector.tensor_copy(dst, src)
                            else:
                                last = nc.vector.tensor_tensor(dst, src, split(bvo[:, 0, :]), ALU.add)
                else:
                    dst = S[:, bass.ds(i * TPB + tile, 1), :]
                    src = ps[:, 6, 0:P].unsqueeze(1)
                    if windowed:
                        last = nc.vector.tensor_copy(dst, src)
                    else:
                        last = nc.vector.tensor_tensor(dst, src, bvo[:, 1:2, :], ALU.add)
                last.then_inc(aux_free, 1)

            def mask_keys(parity, quarters):
                for r in quarters:
                    own = heads[:, QG * r:QG * (r + 1)].unsqueeze(2).broadcast_to([P, QG, SEQ])
                    nc.vector.tensor_tensor(kM[:, parity, QG * r:QG * (r + 1), PAD:PAD + SEQ],
                                            kT[:, :].unsqueeze(1).broadcast_to([P, QG, SEQ]), own,
                                            ALU.mult).then_inc(masked, 1)

            def bias_max(g, n):
                tile, h0, slot = g // GPT, (g % GPT) * HG, g % NBUF
                dve.wait_ge(scores, n + 1)
                s = prob[:, slot]
                nc.vector.tensor_tensor(s.rearrange("p (b a) k -> p b (a k)", b=2),
                                        ps[:, 2 * (g % 2):2 * (g % 2) + 2, :],
                                        table[:, tile, h0:h0 + HG, :].rearrange("p (b a) k -> p b (a k)", b=2),
                                        ALU.add).then_inc(biased, 1)
                dve.drain()
                nc.vector.tensor_reduce(nmax[:, slot], s, AX.X, ALU.max, negate=True).then_inc(max_done, 1)

            def invert(n, slot):
                dve.wait_ge(exped, n + 1)
                nc.vector.reciprocal(den[:, slot], den[:, slot]).then_inc(inverted, 1)

            def part(i, parity):
                for g in range(G):
                    for before, kind, at, tile in jobs_at(i, g, "AB"):
                        job(before, kind, at, parity ^ (kind != "y"), tile)
                    if exists(i + 1) and g in MASKS:
                        mask_keys(1 - parity, MASKS[g])
                    seq, gg, n = group_at(i, g, AHEAD)
                    if exists(seq):
                        bias_max(gg, n)
                    seq, gg, n = group_at(i, g, AHEAD - 1)
                    if exists(seq):
                        invert(n, gg % NBUF)
                    for before, kind, at, tile in jobs_at(i, g, "CDE"):
                        job(before, kind, at, parity ^ (kind != "y"), tile)

            for before, (_, _, kind) in enumerate(FRONT):
                job(before, kind, 0, 0, 0)
            dve.drain()
            mask_keys(0, range(NQ))
            for g in range(AHEAD):
                bias_max(g, g)
            for g in range(AHEAD - 1):
                invert(g, g)
            sequences(dve, part)


def experts(nc, t, ps, ident, X, Y, S, wdense):
    CH = chunks(FEAT)
    NC, NR = len(CH), ROUTED // P
    N = 512
    ROUNDS = NBATCH * SEQ // N
    with ExitStack() as c:
        sb = lambda n, s: c.enter_context(nc.sbuf_tensor("e_" + n, s, F32))
        sem = lambda n: c.enter_context(nc.semaphore("e_" + n))
        wgu = sb("wgu", [P, 2, FEAT])
        wd = sb("wd", [P, NC, P])
        sel = sb("sel", [NE, ROUTED])
        xs = sb("xs", [P, 4, P])
        ws = sb("ws", [P, 4, NE])
        xT = sb("xT", [P, N])
        wT = sb("wT", [NE, N])
        sg = sb("sg", [P, 2, N])
        h = sb("h", [P, 2, N])
        gT = sb("gT", [P, N])
        upd = sb("upd", [P, 4, P])
        (loaded, staged, x_T, x_sb, w_T, w_sb, gate_ps, up_ps, route_ps, gate_sb, h1, h2, down, down_all, out_sb,
         out_T, x_new) = map(sem, (
            "loaded", "staged", "x_T", "x_sb", "w_T", "w_sb", "gate_ps", "up_ps", "route_ps", "gate_sb", "h1", "h2",
            "down", "down_all", "out_sb", "out_T", "x_new"))
        block = c.enter_context(nc.Block())
        released = (w_T, x_new, h2, gate_sb, h1, out_sb, down, out_T)

        @block.sync
        def _(sp):
            for s in released:
                sp.sem_inc(s, START)
            for j, (w, sw) in enumerate((("wg", "swg"), ("wu", "swu"))):
                sp.dma_start(wgu[:, j, 0:ROUTED].rearrange("p (e i) -> p e i", e=NE),
                             t["L0_ffn_" + w].rearrange("e h i -> h e i")).then_inc(loaded, 16)
                sp.dma_start(wgu[:, j, ROUTED:FEAT], t["L0_ffn_" + sw]).then_inc(loaded, 16)
            wdf = t["L0_ffn_wd"].rearrange("e i h -> (e i) h")
            sp.dma_start(wd[:, 0:NR, :], wdf.rearrange("(c p) h -> p c h", p=P)).then_inc(loaded, 16)
            full = SHARED // P
            sp.dma_start(wd[:, NR:NR + full, :],
                         t["L0_ffn_swd"][0:full * P, :].rearrange("(c p) h -> p c h", p=P)).then_inc(loaded, 16)
            sp.dma_start(wd[0:SHARED - full * P, NR + full, :], t["L0_ffn_swd"][full * P:SHARED, :]).then_inc(loaded, 16)
            sp.dma_start(sel[:, :], t["c_select"]).then_inc(loaded, 16)

        @block.gpsimd
        def _(pool):
            with pool.Fori(0, ROUNDS) as i:
                pool.wait_ge(w_T, i + START)
                nc.gpsimd.tensor_copy(xs[:], Y[:, bass.ds(i * 4, 4), :]).then_inc(staged, 1)
                nc.gpsimd.tensor_copy(ws[:], wdense[:, bass.ds(i * 4, 4), :]).then_inc(staged, 1)

        @block.tensor
        def _(pe):
            pe.wait_ge(loaded, 16 * 8)
            with pe.Fori(0, ROUNDS) as i:
                pe.wait_ge(staged, 2 * i + 2)
                pe.wait_ge(x_new, i + START)
                for k in range(4):
                    last = nc.tensor.transpose(ps[:, 6, k * P:(k + 1) * P], xs[:, k, :], ident[:, :])
                last.then_inc(x_T, 1)
                pe.wait_ge(h2, i * NR + START)
                for k in range(4):
                    last = nc.tensor.transpose(ps[0:NE, 4, k * P:(k + 1) * P], ws[:, k, :], ident[:, :])
                last.then_inc(w_T, 1)
                pe.wait_ge(x_sb, i + 1)
                pe.wait_ge(w_sb, i + 1)
                for s in range(NC + 1):
                    if s < NC:
                        a, n = CH[s]
                        pe.wait_ge(gate_sb, i * NC + max(s - 1, 0) + START)
                        nc.tensor.matmul(ps[0:n, s % 2, :], wgu[:, 0, a:a + n], xT[:, :], start=True, stop=True).then_inc(gate_ps, 1)
                        pe.wait_ge(h1, i * NC + max(s - 1, 0) + START)
                        nc.tensor.matmul(ps[0:n, 2 + s % 2, :], wgu[:, 1, a:a + n], xT[:, :], start=True, stop=True).then_inc(up_ps, 1)
                        if s < NR:
                            if s >= 2:
                                pe.wait_ge(h2, i * NR + s - 1 + START)
                            nc.tensor.matmul(ps[:, 4 + s % 2, :], sel[:, a:a + n], wT[:, :], start=True, stop=True).then_inc(route_ps, 1)
                    if s >= 1:
                        b = s - 1
                        n = CH[b][1]
                        if b < NR:
                            pe.wait_ge(h2, i * NR + b + 1 + START)
                        else:
                            pe.wait_ge(h1, i * NC + b + 1 + START)
                        if b == 0:
                            pe.wait_ge(out_sb, i + START)
                        nc.tensor.matmul(ps[:, 7, :], wd[0:n, b, :], h[0:n, b % 2, :],
                                         start=(b == 0), stop=(b == NC - 1)).then_inc(down, 1)
                pe.wait_ge(out_sb, i + 1 + START)
                for k in range(4):
                    last = nc.tensor.transpose(ps[:, 6, k * P:(k + 1) * P], gT[:, k * P:(k + 1) * P], ident[:, :])
                last.then_inc(out_T, 1)

        @block.scalar
        def _(act):
            nc.scalar.preload_act_table(ACT.Silu)
            with act.Fori(0, ROUNDS) as i:
                act.wait_ge(x_T, i + 1)
                nc.scalar.activation(xT[:, :], ps[:, 6, :], ACT.Copy).then_inc(x_sb, 1)
                act.wait_ge(w_T, i + 1 + START)
                nc.scalar.activation(wT[:, :], ps[0:NE, 4, :], ACT.Copy).then_inc(w_sb, 1)
                for s, (a, n) in enumerate(CH):
                    act.wait_ge(gate_ps, i * NC + s + 1)
                    act.wait_ge(h1, i * NC + max(s - 1, 0) + START)
                    nc.scalar.activation(sg[0:n, s % 2, :], ps[0:n, s % 2, :], ACT.Silu).then_inc(gate_sb, 1)
                act.wait_ge(down, (i + 1) * NC + START)
                act.wait_ge(out_T, i + START)
                nc.scalar.activation(gT[:, :], ps[:, 7, :], ACT.Silu).then_inc(out_sb, 1)

        @block.vector
        def _(dve):
            with dve.Fori(0, ROUNDS) as i:
                for s, (a, n) in enumerate(CH):
                    dve.wait_ge(gate_sb, i * NC + s + 1 + START)
                    dve.wait_ge(up_ps, i * NC + s + 1)
                    dve.wait_ge(down, i * NC + max(s - 1, 0) + START)
                    hs = h[0:n, s % 2, :]
                    nc.vector.tensor_tensor(hs, ps[0:n, 2 + s % 2, :], sg[0:n, s % 2, :], ALU.mult).then_inc(h1, 1)
                    if s < NR:
                        dve.drain()
                        dve.wait_ge(route_ps, i * NR + s + 1)
                        nc.vector.tensor_tensor(hs, ps[0:n, 4 + s % 2, :], hs, ALU.mult).then_inc(h2, 1)
                dve.wait_ge(out_T, i + 1 + START)
                nc.vector.tensor_tensor(upd[:], ps[:, 6, :].rearrange("p (k e) -> p k e", k=4),
                                        S[:, bass.ds(i * 4, 4), :], ALU.mult)
                dve.drain()
                nc.vector.tensor_tensor(X[:, bass.ds(i * 4, 4), :], X[:, bass.ds(i * 4, 4), :], upd[:],
                                        ALU.add).then_inc(x_new, 1)
                dve.drain()


def inner_layers(nc, t, ps, ident, Y):
    KW = 2 * WIN
    N = 512
    MLP_ROUNDS = NBATCH * SEQ // N
    TILES = NBATCH * TPB
    CH = chunks(HID)
    NC = len(CH)
    with ExitStack() as c:
        sb = lambda n, s: c.enter_context(nc.sbuf_tensor("i_" + n, s, F32))
        sem = lambda n: c.enter_context(nc.semaphore("i_" + n))
        mask = sb("mask", [P, TPB, KW])
        rotary = sb("rotary", [P, TPB, 4, FD])
        scales = sb("scales", [P, 2, FD])
        rot = sb("rot", [P, TPB, 4, FD])
        wqkv = sb("wqkv", [P, 3 * INNER])
        wo = sb("wo", [P, 4, P])
        w1 = sb("w1", [P, 2 * HID])
        w2 = sb("w2", [P, NC, P])
        b1 = sb("b1", [P, 2, NC])
        vecs = sb("vecs", [P, 3])
        hs = sb("hs", [P, TPB, P])
        hT = sb("hT", [P, 2, SEQ])
        qk = sb("qk", [P, TPB, 2, FH, FD])
        rt = sb("rt", [P, TPB, 2, FH, FD])
        sq = sb("sq", [P, 2, FH, FD])
        ss = sb("ss", [P, TPB, 2 * FH])
        rn = sb("rn", [P, TPB, 2 * FH])
        rtmp = sb("rtmp", [P, 2 * FH])
        qT = sb("qT", [P, 4, P])
        kT = sb("kT", [P, 4, WIN + SEQ])
        V = sb("V", [P, 2, 2, TPB, INNER])
        prob = sb("prob", [P, TPB, FH, KW])
        nmax = sb("nmax", [P, TPB, FH])
        den = sb("den", [P, TPB, FH])
        probT = sb("probT", [P, 1024])
        oT = sb("oT", [P, 4, P])
        ms = sb("ms", [P, 4, P])
        st = sb("st", [P, 4, 6])
        mean = sb("mean", [P, 4])
        rstd = sb("rstd", [P, 4])
        mtmp = sb("mtmp", [P, 2, 4])
        mT = sb("mT", [P, N])
        ge = sb("ge", [P, 2, N])
        hm = sb("hm", [P, 2, N])
        zT = sb("zT", [P, N])
        (once, w_loaded, zeroed, staged, h_T, h_sb, qk_ps, qk_sb, sq_sb, ss_done, cos_done, sin_done,
         qk_done, v_ps, v_sb, qk_T, qkT_sb, scores, biased, max_done, exped, inverted, normed, p_T, pT_sb, pv_done,
         o_sb, y_ps, y_att, m_staged, m_norm, m_T, m_sb, a_ps, g_ps, g_sb, hm_done, z_ps, z_sb, z_T,
         y_mlp) = map(sem, (
            "once", "w_loaded", "zeroed", "staged", "h_T", "h_sb", "qk_ps", "qk_sb", "sq_sb", "ss_done",
            "cos_done", "sin_done", "qk_done", "v_ps", "v_sb", "qk_T", "qkT_sb", "scores", "biased",
            "max_done", "exped", "inverted", "normed", "p_T", "pT_sb", "pv_done", "o_sb", "y_ps", "y_att",
            "m_staged", "m_norm", "m_T", "m_sb", "a_ps", "g_ps", "g_sb", "hm_done", "z_ps", "z_sb", "z_T", "y_mlp"))
        block = c.enter_context(nc.Block())
        CREDIT = 2
        released = (y_mlp, h_T, h_sb, m_T, o_sb, y_att, biased, z_sb, hm_done, ss_done, qk_T, p_T, pT_sb, v_sb,
                    z_T, z_ps)
        HALF = P // 2
        NLOAD = 5 + 4 + 3 + 2
        NZERO = 4

        def sequences(eng, part):
            part(-1, 1)
            part(0, 0)
            with eng.Fori(0, (NBATCH - 4) // 2) as r:
                part(r * 2 + 1, 1)
                part(r * 2 + 2, 0)
            for i in range(NBATCH - 3, NBATCH + 1):
                part(i, i % 2)

        def tile_at(i, k, ahead):
            return i + (k + ahead) // TPB, (k + ahead) % TPB

        def exists(i):
            return not isinstance(i, int) or 0 <= i < NBATCH

        def mlp_rounds(eng, main):
            main(0)
            with eng.Fori(1, MLP_ROUNDS - 1) as r:
                main(r)
            main(MLP_ROUNDS - 1)
            main(MLP_ROUNDS)

        def is_round(r):
            return not isinstance(r, int) or 0 <= r < MLP_ROUNDS

        @block.sync
        def _(sp):
            for s in released:
                sp.sem_inc(s, CREDIT)
            sp.dma_start(mask[:], t["c_ffn_mask"]).then_inc(once, 16)
            sp.dma_start(rotary[:], t["c_rotary"]).then_inc(once, 16)
            sp.wait_ge(zeroed, NZERO)
            with sp.Fori(0, DEPTH) as l:
                sp.wait_ge(y_mlp, l * MLP_ROUNDS + CREDIT)
                ly = bass.ds(l, 1)

                def load(dst, src):
                    sp.dma_start(dst, src, allow_slow_non_contiguous=True).then_inc(w_loaded, 16)

                load(wqkv[:, :], t["L1_ffn_wqkv"][ly].rearrange("o p f -> p (o f)"))
                load(wo[:], t["L1_ffn_wo"][ly].rearrange("o (c p) f -> p (o c) f", p=P))
                load(w1[:, :], t["L1_ffn_w1"][ly].rearrange("o p f -> p (o f)"))
                load(w2[:, 0:2, :], t["L1_ffn_w2"][ly, 0:2 * P, :].rearrange("o (c p) f -> p (o c) f", p=P))
                load(w2[0:HID - 2 * P, 2:3, :], t["L1_ffn_w2"][ly, 2 * P:HID, :].rearrange("o p f -> p o f"))
                for j in range(2):
                    at = j * HID
                    load(b1[:, j, 0:2], t["L1_ffn_b1"][ly, at:at + 2 * P].rearrange("o (c p) -> p (o c)", p=P))
                    load(b1[0:HID - 2 * P, j, 2:3], t["L1_ffn_b1"][ly, at + 2 * P:at + HID].rearrange("o p -> p o"))
                for j, v in enumerate(("ln_g", "ln_b", "b2")):
                    load(vecs[:, j:j + 1], t["L1_ffn_" + v][ly].rearrange("o p -> p o"))
                for j, v in enumerate(("q_scale", "k_scale")):
                    load(scales[:, j, :], t["L1_ffn_" + v][ly].broadcast_to([P, FD]))
                with sp.Fori(0, NBATCH) as b:
                    n = l * NBATCH + b
                    sp.wait_ge(h_T, n + CREDIT)
                    sp.dma_start(hs[:, :, 0:HALF], Y[:, bass.ds(b * TPB, TPB), 0:HALF]).then_inc(staged, 16)
                    sp.dma_start(hs[1:P, :, HALF:P], Y[0:P - 1, bass.ds(b * TPB, TPB), HALF:P]).then_inc(staged, 16)
                    sp.dma_start(hs[0:1, 1, HALF:P], Y[P - 1:P, bass.ds(b * TPB, 1), HALF:P].rearrange("p o e -> p (o e)")).then_inc(staged, 16)
                with sp.Fori(0, MLP_ROUNDS) as r:
                    n = l * MLP_ROUNDS + r
                    sp.wait_ge(m_T, n + CREDIT)
                    sp.wait_ge(y_att, (l + 1) * TILES + CREDIT)
                    sp.dma_start(ms[:, :, 0:HALF], Y[:, bass.ds(r * 4, 4), 0:HALF]).then_inc(m_staged, 16)
                    sp.dma_start(ms[1:P, :, HALF:P], Y[0:P - 1, bass.ds(r * 4, 4), HALF:P]).then_inc(m_staged, 16)
                    for k in range(2):
                        sp.dma_start(ms[0:1, 2 * k + 1, HALF:P],
                                     Y[P - 1:P, bass.ds(r * 4 + 2 * k, 1), HALF:P].rearrange("p o e -> p (o e)")).then_inc(m_staged, 16)

        @block.gpsimd
        def _(pool):
            nc.gpsimd.memset(hs[:, 0, :], 0.0).then_inc(zeroed, 1)
            nc.gpsimd.memset(ms[:], 0.0).then_inc(zeroed, 1)
            nc.gpsimd.memset(kT[:, :, 0:WIN], 0.0).then_inc(zeroed, 1)
            nc.gpsimd.memset(V[:, :, 1, 0, :], 0.0).then_inc(zeroed, 1)
            with pool.Fori(0, DEPTH) as l:
                def rotate(i, k):
                    m = (l * NBATCH + i) * TPB + k
                    pool.wait_ge(qk_sb, m + 1)
                    pool.wait_ge(sin_done, m + 1)
                    for j in range(2):
                        cb = rot[:, k, 2 * j, :].unsqueeze(1).broadcast_to([P, FH, FD])
                        nc.gpsimd.tensor_tensor(qk[:, k, j], qk[:, k, j], cb, ALU.mult)
                    pool.drain()
                    nc.gpsimd.tensor_tensor(qk[:, k], qk[:, k], rt[:, k], ALU.add).then_inc(cos_done, 1)

                def normalise(i, k):
                    pool.wait_ge(inverted, (l * NBATCH + i) * TPB + k + 1)
                    nc.gpsimd.tensor_tensor(prob[:, k], prob[:, k],
                                            den[:, k].unsqueeze(2).broadcast_to([P, FH, KW]),
                                            ALU.mult).then_inc(normed, 1)

                def part(i, parity):
                    for k in range(TPB):
                        if exists(i + 1):
                            rotate(i + 1, k)
                        if exists(i):
                            normalise(i, k)

                sequences(pool, part)

        @block.tensor
        def _(pe):
            pe.wait_ge(zeroed, NZERO)
            with pe.Fori(0, DEPTH) as l:
                count = lambda i, k=0: (l * NBATCH + i) * TPB + k

                def tokens(i):
                    n = l * NBATCH + i
                    pe.wait_ge(staged, (n + 1) * 48)
                    outputs = (i - 2) * TPB if not isinstance(i, int) else max(i - 2, 0) * TPB
                    pe.wait_ge(y_att, count(0) + outputs + CREDIT)
                    for k in range(TPB):
                        last = nc.tensor.transpose(ps[:, 7, k * P:(k + 1) * P], hs[:, k, :], ident[:, :])
                    last.then_inc(h_T, 1)

                def project_qk(i, k, parity):
                    m = count(i, k)
                    pe.wait_ge(v_sb, m + CREDIT)
                    pe.wait_ge(h_sb, l * NBATCH + i + 1 + CREDIT)
                    here = hT[:, parity, P * k:P * (k + 1)]
                    nc.tensor.matmul(ps[:, 0, :], here, wqkv[:, 0:INNER], start=True, stop=True)
                    nc.tensor.matmul(ps[:, 1, :], here, wqkv[:, INNER:2 * INNER], start=True, stop=True).then_inc(qk_ps, 1)

                def project_v(i, k, parity):
                    m = count(i, k)
                    pe.wait_ge(qk_sb, m + 1)
                    pe.wait_ge(sq_sb, m + 1)
                    nc.tensor.matmul(ps[:, 0, :], hT[:, parity, P * k:P * (k + 1)], wqkv[:, 2 * INNER:],
                                     start=True, stop=True).then_inc(v_ps, 1)

                def transpose_qk(i, k):
                    m = count(i, k)
                    pe.wait_ge(qk_done, m + 1)
                    pe.wait_ge(pT_sb, m - 1 + CREDIT)
                    for j in range(2):
                        flat = qk[:, k, j].rearrange("p h d -> p (h d)")
                        for u in range(4):
                            last = nc.tensor.transpose(ps[:, 4 + j, u * P:(u + 1) * P], flat[:, u * P:(u + 1) * P], ident[:, :])
                    last.then_inc(qk_T, 1)

                def score_ready(i, k):
                    m = count(i, k)
                    pe.wait_ge(qkT_sb, m + 1)
                    pe.wait_ge(biased, m + CREDIT)

                def score(i, k):
                    for h in range(FH):
                        r, u = FD * (h % 2), h // 2
                        keys = kT[r:r + FD, u].rearrange("p (b w) -> p b w", w=WIN)
                        for a in range(2):
                            if a:
                                window = keys[:, 2 * k + 1:2 * k + 3]
                            else:
                                window = keys[:, 2 * k + 1:(2 * k - 1 if k else None):-1]
                            last = nc.tensor.matmul(ps[WIN * a:WIN * (a + 1), 2 + h % 2, u * KW:(u + 1) * KW],
                                                    qT[r:r + FD, u, WIN * a:WIN * (a + 1)], window, start=True, stop=True)
                    last.then_inc(scores, 1)

                def transpose_prob(i, k):
                    m = count(i, k)
                    pe.wait_ge(normed, m + 1)
                    flat = prob[:, k].rearrange("p a k -> p (a k)")
                    for u in range(8):
                        last = nc.tensor.transpose(ps[:, 4 + u // 4, (u % 4) * P:(u % 4 + 1) * P],
                                                   flat[:, u * P:(u + 1) * P], ident[:, :])
                    last.then_inc(p_T, 1)

                def sums(i, k, parity):
                    m = count(i, k)
                    pe.wait_ge(zeroed, NZERO)
                    pe.wait_ge(v_sb, m + 1 + CREDIT)
                    pe.wait_ge(o_sb, m + CREDIT)
                    pe.wait_ge(pT_sb, m + 1 + CREDIT)
                    for h in range(FH):
                        slot = h % 2 * 4 + h // 2
                        for a in range(2):
                            last = nc.tensor.matmul(ps[FD * (h % 2):FD * (h % 2 + 1), 6, h // 2 * P + WIN * a:h // 2 * P + WIN * (a + 1)],
                                                    V[:, parity, 1 - a, k, FD * h:FD * (h + 1)],
                                                    probT[:, slot * P + WIN * a:slot * P + WIN * (a + 1)],
                                                    start=True, stop=True)
                    last.then_inc(pv_done, 1)

                def project_out(i, k):
                    m = count(i, k)
                    pe.wait_ge(o_sb, m + 1 + CREDIT)
                    pe.wait_ge(y_att, m + CREDIT)
                    ahead = i + 3 if not isinstance(i, int) else min(i + 3, NBATCH)
                    pe.wait_ge(h_sb, l * NBATCH + ahead + CREDIT)
                    for u in range(4):
                        last = nc.tensor.matmul(ps[:, 7, 2 * P:3 * P], oT[:, u, :], wo[:, u, :], start=(u == 0), stop=(u == 3))
                    last.then_inc(y_ps, 1)

                def part(i, parity):
                    for k in range(TPB):
                        last = tile_at(i, k, -1)
                        if exists(i):
                            score_ready(i, k)
                        if exists(i + 1):
                            project_qk(i + 1, k, 1 - parity)
                        elif exists(last[0]):
                            transpose_prob(*last)
                        if exists(i):
                            score(i, k)
                        if exists(i + 1) and exists(last[0]):
                            transpose_prob(*last)
                        if exists(i - 1):
                            project_out(i - 1, k)
                        if exists(last[0]):
                            sums(*last, parity ^ (k == 0))
                        if exists(i + 1):
                            project_v(i + 1, k, 1 - parity)
                        ahead = tile_at(i, k, 1)
                        if exists(ahead[0]):
                            transpose_qk(*ahead)
                        if k == TPB - 1 and exists(i + 2):
                            tokens(i + 2)

                pe.wait_ge(w_loaded, (l + 1) * NLOAD * 16)
                tokens(0)
                sequences(pe, part)

                def front(r):
                    n = l * MLP_ROUNDS + r
                    pe.wait_ge(m_norm, n + 1)
                    for k in range(4):
                        last = nc.tensor.transpose(ps[:, 6, k * P:(k + 1) * P], ms[:, k, :], ident[:, :])
                    last.then_inc(m_T, 1)

                def tail(r):
                    n = l * MLP_ROUNDS + r
                    pe.wait_ge(z_sb, n + 1 + CREDIT)
                    pe.wait_ge(y_mlp, n + CREDIT)
                    for k in range(4):
                        last = nc.tensor.transpose(ps[:, 5, k * P:(k + 1) * P], zT[:, k * P:(k + 1) * P], ident[:, :])
                    last.then_inc(z_T, 1)

                def main(r):
                    n = l * MLP_ROUNDS + r
                    if is_round(r):
                        pe.wait_ge(m_sb, n + 1)
                    for s in range(NC + 1):
                        if s < NC and is_round(r):
                            a, w = CH[s]
                            pe.wait_ge(hm_done, n * NC + max(s - 1, 0) + CREDIT)
                            nc.tensor.matmul(ps[0:w, 2 + s % 2, :], w1[:, HID + a:HID + a + w], mT[:, :], start=True, stop=True).then_inc(g_ps, 1)
                            nc.tensor.matmul(ps[0:w, s % 2, :], w1[:, a:a + w], mT[:, :], start=True, stop=True).then_inc(a_ps, 1)
                        if s == 1 and is_round(r - 1):
                            tail(r - 1)
                        if s == NC and is_round(r + 1):
                            front(r + 1)
                        if s >= 1 and is_round(r):
                            u = s - 1
                            w = CH[u][1]
                            pe.wait_ge(hm_done, n * NC + u + 1 + CREDIT)
                            if u == 0:
                                pe.wait_ge(z_sb, n + CREDIT)
                            nc.tensor.matmul(ps[:, 7, :], w2[0:w, u, :], hm[0:w, u % 2, :],
                                             start=(u == 0), stop=(u == NC - 1)).then_inc(z_ps, 1)

                pe.wait_ge(y_att, (l + 1) * TILES + CREDIT)
                front(0)
                mlp_rounds(pe, main)

        @block.scalar
        def _(act):
            act.wait_ge(zeroed, NZERO)
            with act.Fori(0, DEPTH) as l:
                count = lambda i, k=0: (l * NBATCH + i) * TPB + k
                act.wait_ge(w_loaded, (l + 1) * NLOAD * 16)

                def keep_qk(i, k):
                    m = count(i, k)
                    act.wait_ge(qk_ps, m + 1)
                    act.wait_ge(ss_done, m + CREDIT)
                    act.wait_ge(qk_T, m - 1 + CREDIT)
                    src = ps[:, 0:2, :].rearrange("p j (h d) -> p j h d", h=FH)
                    nc.scalar.activation(sq[:], src, ACT.Square).then_inc(sq_sb, 1)
                    nc.scalar.activation(qk[:, k], src, ACT.Copy).then_inc(qk_sb, 1)

                def keep_v(i, k, parity):
                    act.wait_ge(v_ps, count(i, k) + 1)
                    last = nc.scalar.activation(V[:, parity, 0, k, :], ps[:, 0, :], ACT.Copy)
                    if k + 1 < TPB:
                        nc.scalar.activation(V[WIN:P, parity, 1, k + 1, :], ps[WIN:P, 0, :], ACT.Copy)
                    last = nc.scalar.activation(V[0:WIN, parity, 1, k, :], ps[0:WIN, 0, :], ACT.Copy)
                    last.then_inc(v_sb, 1)

                def keep_qkT(i, k):
                    act.wait_ge(qk_T, count(i, k) + 1 + CREDIT)
                    nc.scalar.activation(qT[:], ps[:, 4, :].rearrange("p (u q) -> p u q", u=4), ACT.Copy)
                    nc.scalar.activation(kT[:, :, WIN + P * k:WIN + P * (k + 1)],
                                         ps[:, 5, :].rearrange("p (u q) -> p u q", u=4), ACT.Copy).then_inc(qkT_sb, 1)

                def exp(i, k):
                    act.wait_ge(max_done, count(i, k) + 1)
                    for h in range(FH):
                        last = nc.scalar.activation(prob[:, k, h, :], prob[:, k, h, :], ACT.Exp,
                                                    bias=nmax[:, k, h:h + 1], accum_out=den[:, k, h:h + 1])
                    last.then_inc(exped, 1)

                def keep_probT(i, k):
                    act.wait_ge(p_T, count(i, k) + 1 + CREDIT)
                    nc.scalar.activation(probT[:, :].rearrange("p (b q) -> p b q", b=2), ps[:, 4:6, :],
                                         ACT.Copy).then_inc(pT_sb, 1)

                def keep_sums(i, k):
                    act.wait_ge(pv_done, count(i, k) + 1)
                    nc.scalar.activation(oT[:], ps[:, 6, :].rearrange("p (u q) -> p u q", u=4), ACT.Copy).then_inc(o_sb, 1)

                def part(i, parity):
                    for k in range(TPB):
                        last, ahead = tile_at(i, k, -1), tile_at(i, k, 1)
                        if exists(i + 1):
                            keep_qk(i + 1, k)
                        if exists(last[0]):
                            keep_probT(*last)
                        if exists(i):
                            exp(i, k)
                        if exists(last[0]):
                            keep_sums(*last)
                        if exists(i + 1):
                            keep_v(i + 1, k, 1 - parity)
                        if exists(ahead[0]):
                            keep_qkT(*ahead)

                sequences(act, part)

                def front(r):
                    act.wait_ge(m_T, l * MLP_ROUNDS + r + 1 + CREDIT)
                    nc.scalar.activation(mT[:, :], ps[:, 6, :], ACT.Identity, scale=vecs[:, 0:1], bias=vecs[:, 1:2]).then_inc(m_sb, 1)

                def keep_z(r):
                    n = l * MLP_ROUNDS + r
                    act.wait_ge(z_ps, (n + 1) * NC + CREDIT)
                    act.wait_ge(z_T, n + CREDIT)
                    nc.scalar.activation(zT[:, :], ps[:, 7, :], ACT.Identity, bias=vecs[:, 2:3]).then_inc(z_sb, 1)

                def main(r):
                    n = l * MLP_ROUNDS + r
                    if is_round(r):
                        for s, (a, w) in enumerate(CH):
                            act.wait_ge(g_ps, n * NC + s + 1)
                            act.wait_ge(hm_done, n * NC + max(s - 1, 0) + CREDIT)
                            nc.scalar.activation(ge[0:w, s % 2, :], ps[0:w, 2 + s % 2, :], ACT.Gelu,
                                                 bias=b1[0:w, 1, s:s + 1]).then_inc(g_sb, 1)
                    if is_round(r + 1):
                        front(r + 1)
                    if is_round(r):
                        keep_z(r)

                nc.scalar.preload_act_table(ACT.Gelu)
                front(0)
                mlp_rounds(act, main)

        @block.vector
        def _(dve):
            dve.wait_ge(once, 32)
            dve.wait_ge(zeroed, NZERO)
            HF = FD // 2
            with dve.Fori(0, DEPTH) as l:
                count = lambda i, k=0: (l * NBATCH + i) * TPB + k
                dve.wait_ge(w_loaded, (l + 1) * NLOAD * 16)
                for k in range(TPB):
                    for j in range(2):
                        nc.vector.tensor_tensor(rot[:, k, 2 * j, :], rotary[:, k, 2 * j, :], scales[:, j, :], ALU.mult)
                        nc.vector.tensor_tensor(rot[:, k, 2 * j + 1, 0:HF], rotary[:, k, 2 * j + 1, 0:HF], scales[:, j, HF:FD], ALU.mult)
                        nc.vector.tensor_tensor(rot[:, k, 2 * j + 1, HF:FD], rotary[:, k, 2 * j + 1, HF:FD], scales[:, j, 0:HF], ALU.mult)
                dve.drain()

                def tokens(i, parity):
                    dve.wait_ge(h_T, l * NBATCH + i + 1 + CREDIT)
                    nc.vector.tensor_copy(hT[:, parity, :], ps[:, 7, 0:SEQ]).then_inc(h_sb, 1)

                def squares_and_sines(i, k):
                    m = count(i, k)
                    dve.wait_ge(sq_sb, m + 1)
                    nc.vector.tensor_reduce(ss[:, k], sq[:].rearrange("p j h d -> p (j h) d"), AX.X, ALU.add).then_inc(ss_done, 1)
                    dve.wait_ge(qk_sb, m + 1)
                    for j in range(2):
                        for lo, hi in ((0, HF), (HF, 0)):
                            sbc = rot[:, k, 2 * j + 1, lo:lo + HF].unsqueeze(1).broadcast_to([P, FH, HF])
                            last = nc.vector.tensor_tensor(rt[:, k, j, :, lo:lo + HF], qk[:, k, j, :, hi:hi + HF], sbc, ALU.mult)
                    last.then_inc(sin_done, 1)

                def inverse_norms(k):
                    dve.drain()
                    nc.vector.tensor_scalar(ss[:, k], ss[:, k], 1e-24, None, ALU.max)
                    dve.drain()
                    rsqrt(nc, dve, rn[:, k], ss[:, k], rtmp[:, :])

                def scale_qk(i, k):
                    dve.wait_ge(cos_done, count(i, k) + 1)
                    flat = qk[:, k].rearrange("p j h d -> p (j h) d")
                    nc.vector.tensor_tensor(flat, flat, rn[:, k].unsqueeze(2).broadcast_to([P, 2 * FH, FD]),
                                            ALU.mult).then_inc(qk_done, 1)

                def mask_max(i, k):
                    m = count(i, k)
                    dve.wait_ge(scores, m + 1)
                    dve.wait_ge(p_T, m - 1 + CREDIT)
                    mb = mask[:, k:k + 1, :].broadcast_to([P, FH, KW])
                    nc.vector.tensor_tensor(prob[:, k], ps[:, 2:4, :].rearrange("p b (a k) -> p (b a) k", k=KW), mb,
                                            ALU.add).then_inc(biased, 1)
                    dve.drain()
                    nc.vector.tensor_reduce(nmax[:, k], prob[:, k], AX.X, ALU.max, negate=True).then_inc(max_done, 1)

                def invert(i, k):
                    dve.wait_ge(exped, count(i, k) + 1)
                    nc.vector.reciprocal(den[:, k], den[:, k]).then_inc(inverted, 1)

                def add_out(i, k):
                    dve.wait_ge(y_ps, count(i, k) + 1)
                    dst = Y[:, bass.ds(i * TPB + k, 1), :]
                    nc.vector.tensor_tensor(dst, ps[:, 7, 2 * P:3 * P].unsqueeze(1), dst, ALU.add).then_inc(y_att, 1)

                def part(i, parity):
                    for k in range(TPB):
                        ahead = tile_at(i, k, 1)
                        if exists(ahead[0]):
                            scale_qk(*ahead)
                        if exists(i):
                            mask_max(i, k)
                        if exists(i + 1):
                            squares_and_sines(i + 1, k)
                            inverse_norms(k)
                        if exists(i - 1):
                            add_out(i - 1, k)
                        if exists(i):
                            invert(i, k)
                        if k == TPB - 1 and exists(i + 2):
                            tokens(i + 2, parity)

                tokens(0, 0)
                sequences(dve, part)

                def front(r):
                    dve.wait_ge(m_staged, (l * MLP_ROUNDS + r + 1) * 64)
                    for k in range(4):
                        nc.vector.bn_stats(st[:, k, :], ms[:, k, :])
                    dve.drain()
                    moments(nc, dve, st, mean[:, :], rstd[:, :], mtmp, 4)
                    for k in range(4):
                        last = nc.vector.tensor_scalar(ms[:, k, :], ms[:, k, :], mean[:, k:k + 1], rstd[:, k:k + 1],
                                                       ALU.subtract, ALU.mult)
                    last.then_inc(m_norm, 1)

                def tail(r):
                    dve.wait_ge(z_T, l * MLP_ROUNDS + r + 1 + CREDIT)
                    dst = Y[:, bass.ds(r * 4, 4), :]
                    nc.vector.tensor_tensor(dst, ps[:, 5, :].rearrange("p (k e) -> p k e", k=4), dst, ALU.add).then_inc(y_mlp, 1)

                def main(r):
                    n = l * MLP_ROUNDS + r
                    if is_round(r):
                        for s, (a, w) in enumerate(CH):
                            dve.wait_ge(a_ps, n * NC + s + 1)
                            dve.wait_ge(g_sb, n * NC + s + 1)
                            dve.wait_ge(z_ps, n * NC + max(s - 1, 0) + CREDIT)
                            nc.vector.scalar_tensor_tensor(hm[0:w, s % 2, :], ps[0:w, s % 2, :], b1[0:w, 0, s:s + 1],
                                                           ge[0:w, s % 2, :], ALU.add, ALU.mult).then_inc(hm_done, 1)
                            if s == 0 and is_round(r + 1):
                                front(r + 1)
                    if is_round(r - 1):
                        tail(r - 1)

                front(0)
                mlp_rounds(dve, main)


def finish(nc, X, Y, S, out):
    Q = NT // 4
    ov = out.rearrange("b (t p) e -> p (b t) e", p=P)
    with ExitStack() as c:
        sem = lambda n: c.enter_context(nc.semaphore("f_" + n))
        gated, product, total, stored = map(sem, ("gated", "product", "total", "stored"))
        block = c.enter_context(nc.Block())

        @block.scalar
        def _(act):
            for q in range(4):
                nc.scalar.activation(Y[:, q * Q:(q + 1) * Q, :], Y[:, q * Q:(q + 1) * Q, :], ACT.Silu).then_inc(gated, 1)

        @block.gpsimd
        def _(pool):
            for q in range(4):
                pool.wait_ge(gated, q + 1)
                s = slice(q * Q, (q + 1) * Q)
                nc.gpsimd.tensor_tensor(Y[:, s, :], Y[:, s, :], S[:, s, :], ALU.mult).then_inc(product, 1)

        @block.vector
        def _(dve):
            for q in range(4):
                dve.wait_ge(product, q + 1)
                s = slice(q * Q, (q + 1) * Q)
                nc.vector.tensor_tensor(X[:, s, :], Y[:, s, :], X[:, s, :], ALU.add).then_inc(total, 1)

        @block.sync
        def _(sp):
            for q in range(4):
                sp.wait_ge(total, q + 1)
                s = slice(q * Q, (q + 1) * Q)
                sp.dma_start(ov[:, s, :], X[:, s, :]).then_inc(stored, 16)
            sp.wait_ge(stored, 64)


_INS = ["L0_attn_x", "L0_attn_w_in", "L0_attn_w_out", "L0_ffn_gate_w", "L0_ffn_wg", "L0_ffn_wu", "L0_ffn_wd",
        "L0_ffn_swg", "L0_ffn_swu", "L0_ffn_swd", "L1_attn_Wq", "L1_attn_bq", "L1_attn_Wk", "L1_attn_bk",
        "L1_attn_Wv", "L1_attn_bv", "L1_attn_Wo", "L1_attn_bo", "L1_attn_rel_bias", "L1_ffn_wqkv",
        "L1_ffn_q_scale", "L1_ffn_k_scale", "L1_ffn_wo", "L1_ffn_ln_g", "L1_ffn_ln_b", "L1_ffn_w1", "L1_ffn_b1",
        "L1_ffn_w2", "L1_ffn_b2"]


def kernel(**inputs):
    import numpy as _np
    import concourse.bacc as _bacc
    from concourse import mybir as _mybir
    from concourse.bass_utils import run_bass_kernel_spmd as _run

    nc = _bacc.Bacc("TRN2", target_bir_lowering=False, num_devices=1)
    arrays, args = {}, {}
    named = [(name, inputs[name]) for name in _INS] + list(shape_constants().items())
    for name, value in named:
        a = _np.ascontiguousarray(value)
        arrays[f"in_{name}"] = a
        args[name] = nc.dram_tensor(f"in_{name}", a.shape, _mybir.dt.from_np(a.dtype), kind="ExternalInput").ap()
    out = nc.dram_tensor("out_0_dram", (NBATCH, SEQ, P), F32, kind="ExternalOutput").ap()
    build_kernel(nc, args, out)
    r = _run(nc, [arrays], core_ids=[0])
    return r.results[0]["out_0_dram"]
```

```python
import numpy as np
import concourse.bass as bass
from concourse import mybir
from contextlib import ExitStack

F32 = mybir.dt.float32
F32R = mybir.dt.float32r
BF16 = mybir.dt.bfloat16
I32 = mybir.dt.int32
ALU = mybir.AluOpType
ACT = mybir.ActivationFunctionType
AX = mybir.AxisListType

P = 128
NBATCH, SEQ = 16, 256
TPB = SEQ // P
NT = NBATCH * TPB
H, D = 16, 8
WIN = 64
NE, INTER, SHARED = 8, 176, 352
ROUTED = NE * INTER
FEAT = ROUTED + SHARED
FH, FD = 8, 64
INNER = FH * FD
HID = 341
DEPTH = 2
MASKED = -1e30
START = 1
RSQRT_MAGIC = 1597463007.0


def chunks(n, size=P):
    return [(a, min(size, n - a)) for a in range(0, n, size)]


def window_masks():
    q = np.arange(P)[:, None] % WIN
    k = np.arange(2 * WIN)[None, :]
    delta = q - k + WIN
    valid = (delta >= 0) & (delta <= WIN)
    first = valid & ((np.arange(P)[:, None] >= WIN) | (k >= WIN))
    return np.stack([first, valid], 1), delta


def shape_constants():
    valid, delta = window_masks()
    ffn_mask = np.where(valid, 0.0, MASKED).astype(np.float32)
    ffn_mask[np.arange(P) < WIN] = np.roll(ffn_mask[np.arange(P) < WIN], WIN, -1)
    slopes = np.exp2(-(np.arange(H, dtype=np.float32) + 1.0) * 8.0 / H).astype(np.float32)
    bias = slopes[None, :, None] * delta[:, None, :].astype(np.float32)
    l0_table = np.where(valid[:, :, None, :], bias[:, None], MASKED).astype(np.float32)
    half = np.arange(0, FD, 2, dtype=np.float32)
    t = np.arange(SEQ, dtype=np.float32)
    freqs = t[:, None] * (np.float32(1.0) / np.float32(10000.0) ** (half / np.float32(FD)))[None, :]
    freqs = np.concatenate([freqs, freqs], -1).astype(np.float32)
    base = (half + np.float32(0.4 * FD)) / np.float32(1.4 * FD)
    power = (t - SEQ // 2) / np.float32(WIN // 2)
    scale = base[None, :] ** power[:, None]
    scale = np.concatenate([scale, scale], -1).astype(np.float32)
    sign = np.where(np.arange(FD) < FD // 2, -1.0, 1.0).astype(np.float32)
    cos, sin = np.cos(freqs), np.sin(freqs) * sign
    rot = np.stack([cos * scale * 8.0, sin * scale * 8.0, cos / scale, sin / scale], 1)
    rotary = rot.reshape(TPB, P, 4, FD).transpose(1, 0, 2, 3).astype(np.float32)
    select = np.zeros((NE, ROUTED), np.float32)
    select[np.arange(ROUTED) // INTER, np.arange(ROUTED)] = 1.0
    below = (np.arange(NE)[None, :] < np.arange(NE)[:, None]).astype(np.float32)
    return {
        "c_ident": np.eye(P, dtype=np.float32),
        "c_flip": np.eye(P, dtype=np.float32)[::-1].copy(),
        "c_l0_table": l0_table,
        "c_ffn_mask": ffn_mask,
        "c_rotary": rotary,
        "c_select": np.tile(select, (3, 1)),
        "c_heads": np.repeat(np.eye(H, dtype=np.float32), D, 0),
        "c_below": np.broadcast_to(below.reshape(1, NE * NE), (P, NE * NE)).copy(),
    }


def build_kernel(nc, t, out):
    ctx = ExitStack()
    with ctx:
        X = ctx.enter_context(nc.sbuf_tensor("X", [P, NT, P], F32))
        Y = ctx.enter_context(nc.sbuf_tensor("Y", [P, NT, P], F32))
        S = ctx.enter_context(nc.sbuf_tensor("S", [P, NT, P], F32))
        ident = ctx.enter_context(nc.sbuf_tensor("ident", [P, P], F32))
        wparts = ctx.enter_context(nc.sbuf_tensor("wparts", [P, NT, 3 * NE], F32))
        wgu = ctx.enter_context(nc.sbuf_tensor("wgu", [P, 2, FEAT], F32))
        wd = ctx.enter_context(nc.sbuf_tensor("wd", [P, len(chunks(FEAT)), P], F32))
        sel = ctx.enter_context(nc.sbuf_tensor("sel", [3 * NE, ROUTED], F32))
        experts_loaded = ctx.enter_context(nc.semaphore("experts_loaded"))
        ps = ctx.enter_context(nc.psum_tensor("ps", [P, 8, 512], F32))
        skew = nc.dram_tensor("skew_scratch", (H, 512), F32, kind="Internal").ap()

        load_inputs(nc, t, X, ident, wgu, wd, sel, experts_loaded)
        layernorm(nc, "ln0", X, Y)
        router(nc, t, ps, ident, Y, wparts)
        head_attention(nc, "a0", True, t, ps, ident, Y, S, skew)
        experts(nc, t, ps, ident, X, Y, S, wparts, (wgu, wd, sel, experts_loaded))
        layernorm(nc, "ln1", X, Y)
        head_attention(nc, "a1", False, t, ps, ident, Y, S, skew)
        inner_layers(nc, t, ps, ident, Y)
        finish(nc, X, Y, S, out)


def load_inputs(nc, t, X, ident, wgu, wd, sel, experts_loaded):
    NR, full = ROUTED // P, SHARED // P
    with nc.semaphore("x_loaded") as x_loaded, nc.Block() as block:
        @block.sync
        def _(sp):
            xv = t["L0_attn_x"].rearrange("b (t p) e -> p (b t) e", p=P)
            for q in range(4):
                sp.dma_start(X[:, 8 * q:8 * q + 8, :], xv[:, 8 * q:8 * q + 8, :]).then_inc(x_loaded, 16)
            sp.dma_start(ident[:, :], t["c_ident"]).then_inc(x_loaded, 16)
            for j, (w, sw) in enumerate((("wg", "swg"), ("wu", "swu"))):
                sp.dma_start(wgu[:, j, 0:ROUTED].rearrange("p (e i) -> p e i", e=NE),
                             t["L0_ffn_" + w].rearrange("e h i -> h e i")).then_inc(experts_loaded, 16)
                sp.dma_start(wgu[:, j, ROUTED:FEAT], t["L0_ffn_" + sw]).then_inc(experts_loaded, 16)
            wdf = t["L0_ffn_wd"].rearrange("e i h -> (e i) h")
            sp.dma_start(wd[:, 0:NR, :], wdf.rearrange("(c p) h -> p c h", p=P)).then_inc(experts_loaded, 16)
            sp.dma_start(wd[:, NR:NR + full, :],
                         t["L0_ffn_swd"][0:full * P, :].rearrange("(c p) h -> p c h", p=P)).then_inc(experts_loaded, 16)
            sp.dma_start(wd[0:SHARED - full * P, NR + full, :], t["L0_ffn_swd"][full * P:SHARED, :]).then_inc(experts_loaded, 16)
            sp.dma_start(sel[:, :], t["c_select"]).then_inc(experts_loaded, 16)
            sp.wait_ge(x_loaded, 80)


def rsqrt(nc, dve, r, v, tmp):
    nc.vector.tensor_scalar(r.bitcast(I32), v.bitcast(I32), -0.5, RSQRT_MAGIC, ALU.mult, ALU.add)
    dve.drain()
    for _ in range(3):
        nc.vector.scalar_tensor_tensor(tmp, v, -0.5, r, ALU.mult, ALU.mult)
        dve.drain()
        nc.vector.tensor_tensor(tmp, tmp, r, ALU.mult)
        dve.drain()
        nc.vector.scalar_tensor_tensor(r, tmp, 1.5, r, ALU.add, ALU.mult)
        dve.drain()


def moments(nc, dve, st, mean, rstd, tmp, n):
    nc.vector.tensor_tensor(mean, st[:, :, 1], st[:, :, 4], ALU.add)
    nc.vector.tensor_tensor(tmp[:, 0, :], st[:, :, 1], st[:, :, 4], ALU.subtract)
    nc.vector.tensor_tensor(tmp[:, 1, :], st[:, :, 2], st[:, :, 5], ALU.add)
    dve.drain()
    nc.vector.tensor_scalar_mul(mean, mean, 0.5)
    nc.vector.scalar_tensor_tensor(tmp[:, 0, :], tmp[:, 0, :], 0.25, tmp[:, 0, :], ALU.mult, ALU.mult)
    nc.vector.tensor_scalar(tmp[:, 1, :], tmp[:, 1, :], 1.0 / P, 1e-5, ALU.mult, ALU.add)
    dve.drain()
    nc.vector.tensor_tensor(tmp[:, 0, :], tmp[:, 0, :], tmp[:, 1, :], ALU.add)
    dve.drain()
    rsqrt(nc, dve, rstd, tmp[:, 0, :], tmp[:, 1, :])


def layernorm(nc, name, X, Y):
    with ExitStack() as c:
        st = c.enter_context(nc.sbuf_tensor(name + "_st", [P, NT, 6], F32))
        mean = c.enter_context(nc.sbuf_tensor(name + "_mean", [P, NT], F32))
        rstd = c.enter_context(nc.sbuf_tensor(name + "_rstd", [P, NT], F32))
        tmp = c.enter_context(nc.sbuf_tensor(name + "_tmp", [P, 2, NT], F32))
        block = c.enter_context(nc.Block())

        @block.vector
        def _(dve):
            with dve.Fori(0, NT // 8) as i:
                for k in range(8):
                    nc.vector.bn_stats(st[:, bass.ds(i * 8 + k, 1), :], X[:, bass.ds(i * 8 + k, 1), :])
            dve.drain()
            moments(nc, dve, st, mean[:, :], rstd[:, :], tmp, NT)
            nc.vector.tensor_tensor(Y[:], X[:], mean[:, :].unsqueeze(2).broadcast_to([P, NT, P]), ALU.subtract)
            dve.drain()
            nc.vector.tensor_tensor(Y[:], Y[:], rstd[:, :].unsqueeze(2).broadcast_to([P, NT, P]), ALU.mult)
            dve.drain()


def router(nc, t, ps, ident, Y, wparts):
    with ExitStack() as c:
        gw = c.enter_context(nc.sbuf_tensor("r_gw", [NE, P], F32))
        gwT = c.enter_context(nc.sbuf_tensor("r_gwT", [P, NE], F32))
        below = c.enter_context(nc.sbuf_tensor("r_below", [P, NE * NE], F32))
        xs = c.enter_context(nc.sbuf_tensor("r_xs", [P, 4, P], F32))
        xT = c.enter_context(nc.sbuf_tensor("r_xT", [P, 512], F32))
        lg = c.enter_context(nc.sbuf_tensor("r_lg", [P, NT, NE], F32))
        st = c.enter_context(nc.sbuf_tensor("r_st", [P, NT], F32))
        gt = c.enter_context(nc.sbuf_tensor("r_gt", [P, NT, NE, NE], F32))
        eq = c.enter_context(nc.sbuf_tensor("r_eq", [P, NT, NE, NE], F32))
        rank = c.enter_context(nc.sbuf_tensor("r_rank", [P, NT, NE], F32))
        wdense = c.enter_context(nc.sbuf_tensor("r_wdense", [P, NT, NE], F32))
        rounded = c.enter_context(nc.sbuf_tensor("r_rounded", [P, NT, NE], BF16))
        sem = lambda n: c.enter_context(nc.semaphore("r_" + n))
        loaded, gate_T, gate_sb, staged, x_T, x_sb, logits, lg_sb, shifted, exped = map(sem, (
            "loaded", "gate_T", "gate_sb", "staged", "x_T", "x_sb", "logits", "lg_sb", "shifted", "exped"))
        block = c.enter_context(nc.Block())
        released = (x_T, x_sb, lg_sb, logits)
        ROUNDS = NT // 4

        @block.sync
        def _(sp):
            for s in released:
                sp.sem_inc(s, START)
            sp.dma_start(gw[:, :], t["L0_ffn_gate_w"]).then_inc(loaded, 16)
            sp.dma_start(below[:, :], t["c_below"]).then_inc(loaded, 16)

        @block.gpsimd
        def _(pool):
            with pool.Fori(0, ROUNDS) as i:
                pool.wait_ge(x_T, i + START)
                nc.gpsimd.tensor_copy(xs[:], Y[:, bass.ds(i * 4, 4), :]).then_inc(staged, 1)

        @block.tensor
        def _(pe):
            pe.wait_ge(loaded, 32)
            nc.tensor.transpose(ps[:, 0, 0:NE], gw[:, :], ident[0:NE, 0:NE]).then_inc(gate_T, 1)
            pe.wait_ge(gate_sb, 1)
            with pe.Fori(0, ROUNDS) as i:
                pe.wait_ge(staged, i + 1)
                pe.wait_ge(x_sb, i + START)
                for k in range(4):
                    last = nc.tensor.transpose(ps[:, 1, k * P:(k + 1) * P], xs[:, k, :], ident[:, :])
                last.then_inc(x_T, 1)
                pe.wait_ge(x_sb, i + 1 + START)
                pe.wait_ge(lg_sb, i + START)
                for k in range(4):
                    last = nc.tensor.matmul(ps[:, 2, k * NE:(k + 1) * NE], xT[:, k * P:(k + 1) * P], gwT[:, :],
                                            start=True, stop=True)
                last.then_inc(logits, 1)

        @block.scalar
        def _(act):
            act.wait_ge(gate_T, 1)
            nc.scalar.activation(gwT[:, :], ps[:, 0, 0:NE], ACT.Copy).then_inc(gate_sb, 1)
            with act.Fori(0, ROUNDS) as i:
                act.wait_ge(x_T, i + 1 + START)
                act.wait_ge(logits, i + START)
                nc.scalar.activation(xT[:, :], ps[:, 1, :], ACT.Copy).then_inc(x_sb, 1)
            act.wait_ge(shifted, 1)
            nc.scalar.activation(lg[:], lg[:], ACT.Exp).then_inc(exped, 1)

        @block.vector
        def _(dve):
            with dve.Fori(0, ROUNDS) as i:
                dve.wait_ge(logits, i + 1 + START)
                nc.vector.tensor_copy(lg[:, bass.ds(i * 4, 4), :],
                                      ps[:, 2, 0:4 * NE].rearrange("p (k e) -> p k e", e=NE)).then_inc(lg_sb, 1)
            dve.drain()
            bc = lambda a: a[:, :].unsqueeze(2).broadcast_to([P, NT, NE])
            nc.vector.tensor_reduce(st[:, :], lg[:], AX.X, ALU.max)
            dve.drain()
            nc.vector.tensor_tensor(lg[:], lg[:], bc(st), ALU.subtract).then_inc(shifted, 1)
            dve.wait_ge(exped, 1)
            nc.vector.tensor_reduce(st[:, :], lg[:], AX.X, ALU.add)
            dve.drain()
            nc.vector.reciprocal(st[:, :], st[:, :])
            dve.drain()
            nc.vector.tensor_tensor(lg[:], lg[:], bc(st), ALU.mult)
            dve.drain()
            other = lg[:].unsqueeze(2).broadcast_to([P, NT, NE, NE])
            own = lg[:].unsqueeze(3).broadcast_to([P, NT, NE, NE])
            lower = below[:, :].rearrange("p (a b) -> p a b", b=NE).unsqueeze(1).broadcast_to([P, NT, NE, NE])
            nc.vector.tensor_tensor(gt[:], other, own, ALU.is_gt)
            nc.vector.tensor_tensor(eq[:], other, own, ALU.is_equal)
            dve.drain()
            dve.wait_ge(loaded, 32)
            nc.vector.tensor_tensor(eq[:], eq[:], lower, ALU.mult)
            dve.drain()
            nc.vector.tensor_tensor(gt[:], gt[:], eq[:], ALU.add)
            dve.drain()
            nc.vector.tensor_reduce(rank[:], gt[:], AX.X, ALU.add)
            dve.drain()
            nc.vector.tensor_scalar(rank[:], rank[:], 1.5, None, ALU.is_lt)
            dve.drain()
            nc.vector.tensor_tensor(wdense[:], lg[:], rank[:], ALU.mult)
            dve.drain()
            nc.vector.tensor_reduce(st[:, :], wdense[:], AX.X, ALU.add)
            dve.drain()
            nc.vector.tensor_scalar(st[:, :], st[:, :], 1e-20, None, ALU.add)
            dve.drain()
            nc.vector.reciprocal(st[:, :], st[:, :])
            dve.drain()
            nc.vector.tensor_tensor(wdense[:], wdense[:], bc(st), ALU.mult)
            dve.drain()
            for v in range(3):
                part = wparts[:, :, NE * v:NE * (v + 1)]
                nc.vector.tensor_copy(rounded[:], wdense[:])
                dve.drain()
                nc.vector.tensor_copy(part, rounded[:])
                dve.drain()
                if v < 2:
                    nc.vector.tensor_tensor(wdense[:], wdense[:], part, ALU.subtract)
                    dve.drain()


def head_attention(nc, name, windowed, t, ps, ident, Y, S, skew):
    KW = 2 * WIN if windowed else SEQ
    HG = 1024 // KW
    GPT = H // HG
    G = TPB * GPT
    PAD = WIN if windowed else 0
    NBUF = 4
    SCALE = float(1.0 / np.sqrt(np.float32(D)))
    NVT = 2 if windowed else 1
    HB = 512 // KW
    QG = 4
    NQ = H // QG

    with ExitStack() as c:
        sb = lambda n, s: c.enter_context(nc.sbuf_tensor(name + "_" + n, s, F32))
        sem = lambda n: c.enter_context(nc.semaphore(name + "_" + n))
        wnat = sb("wnat", [P, 4, P])
        wT = sb("wT", [P, 4, P])
        heads = sb("heads", [P, H])
        table = sb("table", [P, TPB, H, KW])
        xs = sb("xs", [P, TPB, P])
        xT = sb("xT", [P, PAD + SEQ])
        qT = sb("qT", [P, 2, SEQ])
        kT = sb("kT", [P, SEQ])
        kM = sb("kM", [P, 2, H, PAD + SEQ])
        V = sb("V", [P, 2, NVT, TPB, NQ, QG, 40])
        prob = sb("prob", [P, NBUF, HG, KW])
        nmax = sb("nmax", [P, NBUF, HG])
        den = sb("den", [P, NBUF, HG])
        probT = sb("probT", [P, 2, 1024])
        oT = sb("oT", [P, P])
        bvo = sb("bvo", [P, 2, P])
        if not windowed:
            bqk = sb("bqk", [P, 2])
            rel = sb("rel", [H, 257])
            ext = sb("ext", [H, 512])
            flip = sb("flip", [P, P])
            rel_loaded, rel_ext, rel_out, rel_in, flipped, turned, bq_scaled = map(sem, (
                "rel_loaded", "rel_ext", "rel_out", "rel_in", "flipped", "turned", "bq_scaled"))
        (w_loaded, b_loaded, zeroed, wT_ps, wT_sb, staged, aux_ps, aux_free, masked, scores, biased, max_done,
         exped, inverted, normed, p_T, pT_sb, pv_done, o_sb) = map(sem, (
            "w_loaded", "b_loaded", "zeroed", "wT_ps", "wT_sb", "staged", "aux_ps", "aux_free", "masked", "scores",
            "biased", "max_done", "exped", "inverted", "normed", "p_T", "pT_sb", "pv_done", "o_sb"))
        block = c.enter_context(nc.Block())
        NWL = 64 if not windowed else 32

        if windowed:
            AHEAD = 2
            FRONT = [(0, "A", "x"), (0, "B", "qk"), (1, "C", "v")]
            MASKS = {1: (0, 1), 2: (2, 3)}
        else:
            AHEAD = 3
            FRONT = [(0, "B", "x"), (1, "B", "qk"), (3, "B", "v")]
            MASKS = {2: (0,), 3: (1,), 4: (2,), 5: (3,)}
        JOBS = [(g, s, kind, -1, 0) for g, s, kind in FRONT]
        for tile in range(TPB):
            at = (tile + 1) * GPT - 1 + 2
            JOBS.append((at % G, "C", "y", at // G, tile))
        JOBS.sort(key=lambda j: (j[0], j[1], j[2]))

        def has(i, job):
            return not isinstance(i, int) or 0 <= i - job[3] < NBATCH

        def jobs_before(i):
            if isinstance(i, int):
                return len(FRONT) + sum(has(j, job) for j in range(i) for job in JOBS)
            return i * len(JOBS) + (jobs_before(1) - len(JOBS))

        def jobs_at(i, g, slots):
            count = 0
            for job in JOBS:
                if has(i, job):
                    if job[0] == g and job[1] in slots:
                        yield jobs_before(i) + count, job[2], i - job[3], job[4]
                    count += 1

        def job_of(i, kind):
            if isinstance(i, int) and i == 0:
                return [job[2] for job in FRONT].index(kind) + 1
            return jobs_before(i - 1) + [job[2] for job in JOBS if has(i - 1, job)].index(kind) + 1

        def sequences(eng, part):
            part(0, 0)
            with eng.Fori(0, (NBATCH - 2) // 2) as r:
                part(r * 2 + 1, 1)
                part(r * 2 + 2, 0)
            part(NBATCH - 1, 1)
            part(NBATCH, 0)

        def after(eng, signal, count):
            if not isinstance(count, int) or count > 0:
                eng.wait_ge(signal, count)

        def group_at(i, g, ahead):
            at = g + ahead
            return i + at // G, at % G, i * G + at

        def exists(i):
            return not isinstance(i, int) or 0 <= i < NBATCH

        NBL = 32 if windowed else 16 * 6

        @block.sync
        def _(sp):
            if windowed:
                wi = t["L0_attn_w_in"].rearrange("(c p) e -> p c e", p=P)
                sp.dma_start(wnat[:, 0:3, :], wi).then_inc(w_loaded, 16)
                sp.dma_start(wnat[:, 3, :], t["L0_attn_w_out"]).then_inc(w_loaded, 16)
                sp.dma_start(heads[:, :], t["c_heads"]).then_inc(b_loaded, 16)
                sp.dma_start(table[:], t["c_l0_table"]).then_inc(b_loaded, 16)
            else:
                sp.dma_start(rel[:, :], t["L1_attn_rel_bias"]).then_inc(rel_loaded, 16)
                for j, w in enumerate(("Wq", "Wk", "Wv", "Wo")):
                    sp.dma_start(wnat[:, j, :], t["L1_attn_" + w]).then_inc(w_loaded, 16)
                sp.dma_start(heads[:, :], t["c_heads"]).then_inc(b_loaded, 16)
                sp.dma_start(flip[:, :], t["c_flip"]).then_inc(b_loaded, 16)
                for j, b in enumerate(("bq", "bk")):
                    sp.dma_start(bqk[:, j:j + 1], t["L1_attn_" + b].unsqueeze(1),
                                 allow_slow_non_contiguous=True).then_inc(b_loaded, 16)
                for j, b in enumerate(("bv", "bo")):
                    sp.dma_start(bvo[:, j, :], t["L1_attn_" + b].unsqueeze(0).broadcast_to([P, P])).then_inc(b_loaded, 16)
                sp.wait_ge(rel_ext, 3)
                sp.dma_start(skew, ext[:, :]).then_inc(rel_out, 16)
                sp.wait_ge(rel_out, 16)
                for tile in range(TPB):
                    after(sp, flipped, tile)
                    src = bass.AP(tensor=skew.tensor, offset=skew.offset + P - P * tile,
                                  ap=[[1, P], [512, H], [1, SEQ]])
                    sp.dma_start(prob[:].rearrange("p n a k -> p (n a) k"), src).then_inc(rel_in, 16)

            def stage(i):
                sp.dma_start(xs[:], Y[:, bass.ds(i * TPB, TPB), :]).then_inc(staged, 16)

            stage(0)
            for i in range(1, 3):
                sp.wait_ge(aux_ps, job_of(i - 1, "x"))
                stage(i)
            with sp.Fori(3, NBATCH) as i:
                sp.wait_ge(aux_ps, job_of(i - 1, "x"))
                stage(i)
            sp.wait_ge(staged, 16 * NBATCH)

        NZERO = 3 if windowed else 1

        @block.gpsimd
        def _(pool):
            nc.gpsimd.memset(V[:], 0.0).then_inc(zeroed, 1)
            if windowed:
                nc.gpsimd.memset(xT[:, 0:PAD], 0.0).then_inc(zeroed, 1)
                nc.gpsimd.memset(kM[:, :, :, 0:PAD], 0.0).then_inc(zeroed, 1)

            def normalise(n, slot):
                pool.wait_ge(inverted, n + 1)
                s = prob[:, slot]
                nc.gpsimd.tensor_tensor(s, s, den[:, slot].unsqueeze(2).broadcast_to([P, HG, KW]),
                                        ALU.mult).then_inc(normed, 1)

            def part(i, parity):
                for g in range(G):
                    seq, gg, n = group_at(i, g, AHEAD - 1)
                    if exists(seq):
                        normalise(n, gg % NBUF)

            for g in range(AHEAD - 1):
                normalise(g, g)
            sequences(pool, part)

        @block.tensor
        def _(pe):
            pe.wait_ge(w_loaded, NWL)
            for j in range(4):
                last = nc.tensor.transpose(ps[:, 0, j * P:(j + 1) * P], wnat[:, j, :], ident[:, :])
            last.then_inc(wT_ps, 1)
            pe.wait_ge(wT_sb, 1)
            if not windowed:
                pe.wait_ge(b_loaded, NBL)
                rows = prob[:].rearrange("p n a k -> p (n a k)")
                for tile in range(TPB):
                    pe.wait_ge(rel_in, 16 * (tile + 1))
                    after(pe, turned, tile)
                    for b in range(8):
                        last = nc.tensor.matmul(ps[:, b, :], flip[:, :], rows[:, b * 512:(b + 1) * 512], start=True, stop=True)
                    last.then_inc(flipped, 1)
                pe.wait_ge(turned, TPB)
            pe.wait_ge(zeroed, NZERO)

            def job(before, kind, i, parity, tile):
                after(pe, aux_free, before)
                if kind == "x":
                    pe.wait_ge(staged, 16 * (i + 1))
                    for k in range(TPB):
                        last = nc.tensor.transpose(ps[:, 6, k * P:(k + 1) * P], xs[:, k, :], ident[:, :])
                elif kind == "qk":
                    for j in range(2):
                        last = nc.tensor.matmul(ps[:, 6, j * SEQ:(j + 1) * SEQ], wT[:, j, :], xT[:, PAD:PAD + SEQ],
                                                start=True, stop=True)
                elif kind == "v":
                    for v in range(NVT):
                        for k in range(TPB):
                            at = PAD + P * k - WIN * v
                            last = nc.tensor.matmul(ps[:, 6, (v * TPB + k) * P:(v * TPB + k + 1) * P],
                                                    xT[:, at:at + P], wT[:, 2, :], start=True, stop=True)
                else:
                    pe.wait_ge(o_sb, i * TPB + tile + 1)
                    last = nc.tensor.matmul(ps[:, 6, 0:P], oT[:, :], wT[:, 3, :], start=True, stop=True)
                last.then_inc(aux_ps, 1)

            def score(i, g, n, parity, banks):
                tile, h0 = g // GPT, (g % GPT) * HG
                if 0 in banks:
                    after(pe, biased, n - 1)
                    after(pe, masked, i * NQ + (h0 + HG) // QG)
                for b in banks:
                    h, bank = h0 + b * HB, 2 * (g % 2) + b
                    if windowed:
                        for half in range(2):
                            at = WIN * (2 * tile + half)
                            last = nc.tensor.matmul(ps[WIN * half:WIN * (half + 1), bank, :], qT[:, parity, at:at + WIN],
                                                    kM[:, parity, h:h + HB, at:at + KW], start=True, stop=True)
                    else:
                        last = nc.tensor.matmul(ps[:, bank, :], qT[:, parity, P * tile:P * (tile + 1)],
                                                kM[:, parity, h:h + HB, :], start=True, stop=True)
                if 1 in banks:
                    last.then_inc(scores, 1)

            def transposes(g, n):
                after(pe, pT_sb, n)
                pe.wait_ge(normed, n + 1)
                flat = prob[:, g % NBUF].rearrange("p a k -> p (a k)")
                for b in range(8):
                    last = nc.tensor.transpose(ps[:, 4 + b // 4, (b % 4) * P:(b % 4 + 1) * P],
                                               flat[:, b * P:(b + 1) * P], ident[:, :])
                last.then_inc(p_T, 1)

            def values(parity, v, k, h):
                group = V[:, parity, v, k, h // QG].rearrange("p x d -> p (x d)")
                return group[:, 32 * (h % QG):32 * (h % QG) + 32]

            def sums(i, g, n, parity):
                tile, h0 = g // GPT, (g % GPT) * HG
                if g % GPT == 0:
                    after(pe, o_sb, i * TPB + tile)
                if g == 0:
                    pe.wait_ge(aux_free, job_of(i, "v"))
                pe.wait_ge(pT_sb, n + 1)
                for q in range(HG // QG):
                    rows = slice(32 * (h0 // QG + q), 32 * (h0 // QG + q + 1))
                    if windowed:
                        for half in range(2):
                            for x in range(QG):
                                a = q * QG + x
                                last = nc.tensor.matmul(ps[rows, 7, WIN * half:WIN * (half + 1)],
                                                        values(parity, 1 - half, tile, h0 + a),
                                                        probT[:, g % 2, a * P + WIN * half:a * P + WIN * (half + 1)],
                                                        start=(x == 0), stop=(x == QG - 1))
                    else:
                        for x in range(QG):
                            for k in range(TPB):
                                b = (q * QG + x) * TPB + k
                                last = nc.tensor.matmul(ps[rows, 7, 0:P], values(parity, 0, k, h0 + q * QG + x),
                                                        probT[:, g % 2, b * P:(b + 1) * P],
                                                        start=(x == 0 and k == 0), stop=(x == QG - 1 and k == TPB - 1))
                if g % GPT == GPT - 1:
                    last.then_inc(pv_done, 1)

            def part(i, parity):
                for g in range(G):
                    def small(slots):
                        for before, kind, seq, tile in jobs_at(i, g, slots):
                            job(before, kind, seq, parity ^ (kind != "y"), tile)

                    seq, gg, n = group_at(i, g, AHEAD)
                    par = parity ^ (g + AHEAD >= G)
                    small("A")
                    if exists(seq):
                        score(seq, gg, n, par, (0,))
                    small("B")
                    if exists(seq):
                        score(seq, gg, n, par, (1,))
                    small("C")
                    if exists(i):
                        transposes(g, i * G + g)
                    small("D")
                    seq, gg, n = group_at(i, g, -1)
                    if exists(seq):
                        sums(seq, gg, n, parity ^ (g == 0))
                    small("E")

            for before, (_, _, kind) in enumerate(FRONT):
                job(before, kind, 0, 0, 0)
            for g in range(AHEAD):
                score(0, g, g, 0, (0, 1))
            sequences(pe, part)

        @block.scalar
        def _(act):
            nc.scalar.preload_act_table(ACT.Exp)
            act.wait_ge(wT_ps, 1)
            act.wait_ge(zeroed, NZERO)
            nc.scalar.activation(wT[:], ps[:, 0, :].rearrange("p (c e) -> p c e", c=4), ACT.Copy).then_inc(wT_sb, 1)
            if not windowed:
                act.wait_ge(b_loaded, NBL)
                for tile in range(TPB):
                    act.wait_ge(flipped, tile + 1)
                    nc.scalar.activation(table[:, tile], ps[:].rearrange("p b (a k) -> p (b a) k", k=KW), ACT.Copy).then_inc(turned, 1)

            def job(before, kind, parity):
                if kind == "x":
                    act.wait_ge(aux_ps, before + 1)
                    nc.scalar.activation(xT[:, PAD:PAD + SEQ], ps[:, 6, 0:SEQ], ACT.Copy).then_inc(aux_free, 1)

            def exp(n, slot):
                act.wait_ge(max_done, n + 1)
                for a in range(HG):
                    last = nc.scalar.activation(prob[:, slot, a, :], prob[:, slot, a, :], ACT.Exp,
                                                bias=nmax[:, slot, a:a + 1], accum_out=den[:, slot, a:a + 1])
                last.then_inc(exped, 1)

            def copy_sums(count):
                act.wait_ge(pv_done, count)
                nc.scalar.activation(oT[:, :], ps[:, 7, 0:P], ACT.Copy).then_inc(o_sb, 1)

            def part(i, parity):
                for g in range(G):
                    seq, gg, _ = group_at(i, g, -2)
                    if gg % GPT == GPT - 1 and exists(seq):
                        copy_sums(seq * TPB + gg // GPT + 1)
                    for before, kind, _, _ in jobs_at(i, g, "A"):
                        job(before, kind, parity ^ (kind != "y"))
                    seq, gg, n = group_at(i, g, AHEAD - 1)
                    if exists(seq):
                        exp(n, gg % NBUF)
                    for before, kind, _, _ in jobs_at(i, g, "BC"):
                        job(before, kind, parity ^ (kind != "y"))
                    if exists(i):
                        n = i * G + g
                        act.wait_ge(p_T, n + 1)
                        nc.scalar.activation(probT[:, g % 2, :].rearrange("p (b n) -> p b n", b=2), ps[:, 4:6, :],
                                             ACT.Copy).then_inc(pT_sb, 1)
                    for before, kind, _, _ in jobs_at(i, g, "DE"):
                        job(before, kind, parity ^ (kind != "y"))

            for before, (_, _, kind) in enumerate(FRONT):
                job(before, kind, 0)
            for g in range(AHEAD - 1):
                exp(g, g)
            sequences(act, part)

        @block.vector
        def _(dve):
            if not windowed:
                dve.wait_ge(rel_loaded, 16)
                nc.vector.tensor_copy(ext[:, 127:384], rel[:, ::-1]).then_inc(rel_ext, 1)
                nc.vector.tensor_copy(ext[:, 0:127], rel[:, 256:257].broadcast_to([H, 127])).then_inc(rel_ext, 1)
                nc.vector.tensor_copy(ext[:, 384:512], rel[:, 0:1].broadcast_to([H, 128])).then_inc(rel_ext, 1)
            dve.wait_ge(b_loaded, NBL)
            dve.wait_ge(zeroed, NZERO)
            if not windowed:
                dve.wait_ge(turned, TPB)

            def job(before, kind, i, parity, tile):
                if kind == "x":
                    return
                dve.wait_ge(aux_ps, before + 1)
                if kind == "qk":
                    q, k = ps[:, 6, 0:SEQ], ps[:, 6, SEQ:2 * SEQ]
                    if windowed:
                        nc.vector.tensor_scalar_mul(qT[:, parity, :], q, SCALE)
                        last = nc.vector.tensor_copy(kT[:, :], k)
                    else:
                        nc.vector.tensor_scalar(qT[:, parity, :], q, bqk[:, 0:1], SCALE, ALU.add, ALU.mult)
                        last = nc.vector.tensor_scalar(kT[:, :], k, bqk[:, 1:2], None, ALU.add)
                elif kind == "v":
                    for v in range(NVT):
                        for k in range(TPB):
                            split = lambda a: a.rearrange("p (g x d) -> p g x d", g=NQ, x=QG)
                            src = split(ps[:, 6, (v * TPB + k) * P:(v * TPB + k + 1) * P])
                            dst = V[:, parity, v, k, :, :, 0:D]
                            if windowed:
                                last = nc.vector.tensor_copy(dst, src)
                            else:
                                last = nc.vector.tensor_tensor(dst, src, split(bvo[:, 0, :]), ALU.add)
                else:
                    dst = S[:, bass.ds(i * TPB + tile, 1), :]
                    src = ps[:, 6, 0:P].unsqueeze(1)
                    if windowed:
                        last = nc.vector.tensor_copy(dst, src)
                    else:
                        last = nc.vector.tensor_tensor(dst, src, bvo[:, 1:2, :], ALU.add)
                last.then_inc(aux_free, 1)

            def mask_keys(parity, quarters):
                for r in quarters:
                    own = heads[:, QG * r:QG * (r + 1)].unsqueeze(2).broadcast_to([P, QG, SEQ])
                    nc.vector.tensor_tensor(kM[:, parity, QG * r:QG * (r + 1), PAD:PAD + SEQ],
                                            kT[:, :].unsqueeze(1).broadcast_to([P, QG, SEQ]), own,
                                            ALU.mult).then_inc(masked, 1)

            def bias_max(g, n):
                tile, h0, slot = g // GPT, (g % GPT) * HG, g % NBUF
                dve.wait_ge(scores, n + 1)
                s = prob[:, slot]
                nc.vector.tensor_tensor(s.rearrange("p (b a) k -> p b (a k)", b=2),
                                        ps[:, 2 * (g % 2):2 * (g % 2) + 2, :],
                                        table[:, tile, h0:h0 + HG, :].rearrange("p (b a) k -> p b (a k)", b=2),
                                        ALU.add).then_inc(biased, 1)
                dve.drain()
                nc.vector.tensor_reduce(nmax[:, slot], s, AX.X, ALU.max, negate=True).then_inc(max_done, 1)

            def invert(n, slot):
                dve.wait_ge(exped, n + 1)
                nc.vector.reciprocal(den[:, slot], den[:, slot]).then_inc(inverted, 1)

            def part(i, parity):
                for g in range(G):
                    for before, kind, at, tile in jobs_at(i, g, "AB"):
                        job(before, kind, at, parity ^ (kind != "y"), tile)
                    if exists(i + 1) and g in MASKS:
                        mask_keys(1 - parity, MASKS[g])
                    seq, gg, n = group_at(i, g, AHEAD)
                    if exists(seq):
                        bias_max(gg, n)
                    seq, gg, n = group_at(i, g, AHEAD - 1)
                    if exists(seq):
                        invert(n, gg % NBUF)
                    for before, kind, at, tile in jobs_at(i, g, "CDE"):
                        job(before, kind, at, parity ^ (kind != "y"), tile)

            for before, (_, _, kind) in enumerate(FRONT):
                job(before, kind, 0, 0, 0)
            dve.drain()
            mask_keys(0, range(NQ))
            for g in range(AHEAD):
                bias_max(g, g)
            for g in range(AHEAD - 1):
                invert(g, g)
            sequences(dve, part)


def experts(nc, t, ps, ident, X, Y, S, wparts, weights):
    CH = chunks(FEAT)
    NC, NR = len(CH), ROUTED // P
    N = 512
    ROUNDS = NBATCH * SEQ // N
    wgu, wd, sel, loaded = weights
    HBUF = 3
    with ExitStack() as c:
        sb = lambda n, s, d=F32: c.enter_context(nc.sbuf_tensor("e_" + n, s, d))
        sem = lambda n: c.enter_context(nc.semaphore("e_" + n))
        wgu_hi, wgu_lo = sb("wgu_hi", [P, 2, FEAT], F32R), sb("wgu_lo", [P, 2, FEAT], F32R)
        wd_hi, wd_lo = sb("wd_hi", [P, NC, P], F32R), sb("wd_lo", [P, NC, P], F32R)
        sel16 = sb("sel16", [3 * NE, ROUTED], BF16)
        xs = sb("xs", [P, 4, P])
        ws = sb("ws", [P, 4, 3 * NE])
        xT = sb("xT", [P, 2, 2, N], F32R)
        wT = sb("wT", [3 * NE, 2, N], BF16)
        sg = sb("sg", [P, 2, N])
        h = sb("h", [P, HBUF, N])
        hh = sb("hh", [P, HBUF, 2, N], F32R)
        gT = sb("gT", [P, N])
        upd = sb("upd", [P, 4, P])
        (w_hi, w_lo, sel_sb, staged, x_T, x_hi, x_lo, w_T, w_sb, gate_ps, up_ps, route_ps, gate_sb, h1, h2, h_hi,
         h_lo, down, out_sb, out_T, x_new) = map(sem, (
            "w_hi", "w_lo", "sel_sb", "staged", "x_T", "x_hi", "x_lo", "w_T", "w_sb", "gate_ps", "up_ps", "route_ps",
            "gate_sb", "h1", "h2", "h_hi", "h_lo", "down", "out_sb", "out_T", "x_new"))
        block = c.enter_context(nc.Block())
        FETCH = 8

        def rounds(eng, part):
            part(0, 0)
            with eng.Fori(0, (ROUNDS - 2) // 2) as r:
                part(r * 2 + 1, 1)
                part(r * 2 + 2, 0)
            part(ROUNDS - 1, 1)
            part(ROUNDS, 0)

        def exists(i):
            return not isinstance(i, int) or 0 <= i < ROUNDS

        def after(eng, signal, count):
            if not isinstance(count, int) or count > 0:
                eng.wait_ge(signal, count)

        @block.sync
        def _(sp):
            def stage(i):
                sp.dma_start(xs[:], Y[:, bass.ds(i * 4, 4), :]).then_inc(staged, 16)
                sp.dma_start(ws[:], wparts[:, bass.ds(i * 4, 4), :]).then_inc(staged, 16)

            stage(0)
            with sp.Fori(1, ROUNDS) as i:
                sp.wait_ge(x_T, i)
                sp.wait_ge(w_T, i)
                stage(i)
            sp.wait_ge(staged, 32 * ROUNDS)

        @block.tensor
        def _(pe):
            def split_product(out, w_pair, x_pair, start=True, stop=True):
                nc.tensor.matmul(out, w_pair[0], x_pair[0], start=start, stop=False)
                nc.tensor.matmul(out, w_pair[0], x_pair[1], start=False, stop=False)
                return nc.tensor.matmul(out, w_pair[1], x_pair[0], start=False, stop=stop)

            def fetch(i):
                pe.wait_ge(staged, 32 * (i + 1))
                for k in range(4):
                    last = nc.tensor.transpose(ps[:, 6, k * P:(k + 1) * P], xs[:, k, :], ident[:, :])
                last.then_inc(x_T, 1)

            def fetch_w(i):
                for k in range(4):
                    last = nc.tensor.transpose(ps[0:3 * NE, 6, k * P:(k + 1) * P], ws[:, k, :], ident[:, :])
                last.then_inc(w_T, 1)

            def part(i, parity):
                here = [xT[:, parity, v, :] for v in range(2)]
                if exists(i):
                    pe.wait_ge(x_lo, i + 1)
                    pe.wait_ge(w_sb, i + 1)
                for s in range(NC + 2):
                    if s < NC and exists(i):
                        a, n = CH[s]
                        after(pe, gate_sb, i * NC + s - 1)
                        split_product(ps[0:n, s % 2, :], (wgu_hi[:, 0, a:a + n], wgu_lo[:, 0, a:a + n]), here).then_inc(gate_ps, 1)
                        after(pe, h1, i * NC + s - 1)
                        split_product(ps[0:n, 2 + s % 2, :], (wgu_hi[:, 1, a:a + n], wgu_lo[:, 1, a:a + n]), here).then_inc(up_ps, 1)
                        if s < NR:
                            after(pe, h2, i * NR + max(s - 1, 0))
                            nc.tensor.matmul(ps[:, 4 + s % 2, :], sel16[:, a:a + n], wT[:, parity, :], start=True, stop=True).then_inc(route_ps, 1)
                    if s == 2 and exists(i - 1):
                        pe.wait_ge(out_sb, i)
                        for k in range(4):
                            last = nc.tensor.transpose(ps[:, 6, k * P:(k + 1) * P], gT[:, k * P:(k + 1) * P], ident[:, :])
                        last.then_inc(out_T, 1)
                    if s == FETCH and exists(i + 1):
                        after(pe, x_new, i)
                        fetch(i + 1)
                    if s == FETCH + 2 and exists(i + 1):
                        pe.wait_ge(x_lo, i + 2)
                        fetch_w(i + 1)
                    if s >= 2 and exists(i):
                        b = s - 2
                        n = CH[b][1]
                        pe.wait_ge(h_lo, i * NC + b + 1)
                        if b == 0:
                            after(pe, out_sb, i)
                        split_product(ps[:, 7, :], (wd_hi[0:n, b, :], wd_lo[0:n, b, :]),
                                      [hh[0:n, b % HBUF, v, :] for v in range(2)],
                                      b == 0, b == NC - 1).then_inc(down, 1)

            fetch(0)
            pe.wait_ge(x_lo, 1)
            fetch_w(0)
            pe.wait_ge(w_hi, 2)
            pe.wait_ge(w_lo, 3)
            pe.wait_ge(sel_sb, 1)
            rounds(pe, part)

        @block.scalar
        def _(act):
            nc.scalar.preload_act_table(ACT.Silu)
            act.wait_ge(loaded, 16 * 8)
            nc.scalar.activation(wgu_hi[:], wgu[:], ACT.Copy).then_inc(w_hi, 1)
            nc.scalar.activation(wd_hi[:, 0:NC - 1, :], wd[:, 0:NC - 1, :], ACT.Copy)
            rest = CH[-1][1]
            nc.scalar.activation(wd_hi[0:rest, NC - 1, :], wd[0:rest, NC - 1, :], ACT.Copy).then_inc(w_hi, 1)
            nc.scalar.activation(sel16[:, :], sel[:, :], ACT.Copy).then_inc(sel_sb, 1)

            def fetch(i, parity):
                act.wait_ge(x_T, i + 1)
                nc.scalar.activation(xT[:, parity, 0, :], ps[:, 6, :], ACT.Copy).then_inc(x_hi, 1)

            def fetch_w(i, parity):
                act.wait_ge(w_T, i + 1)
                nc.scalar.activation(wT[:, parity, :], ps[0:3 * NE, 6, :], ACT.Copy).then_inc(w_sb, 1)

            def part(i, parity):
                for s in range(NC + 1):
                    if s < NC and exists(i):
                        n = CH[s][1]
                        act.wait_ge(gate_ps, i * NC + s + 1)
                        after(act, h1, i * NC + s - 1)
                        nc.scalar.activation(sg[0:n, s % 2, :], ps[0:n, s % 2, :], ACT.Silu).then_inc(gate_sb, 1)
                    if s == 0 and exists(i - 1):
                        act.wait_ge(down, i * NC)
                        after(act, out_T, i - 1)
                        nc.scalar.activation(gT[:, :], ps[:, 7, :], ACT.Silu).then_inc(out_sb, 1)
                    if s == FETCH and exists(i + 1):
                        fetch(i + 1, 1 - parity)
                    if s == FETCH + 2 and exists(i + 1):
                        fetch_w(i + 1, 1 - parity)
                    if s >= 1 and exists(i):
                        b = s - 1
                        n = CH[b][1]
                        if b < NR:
                            act.wait_ge(h2, i * NR + b + 1)
                        else:
                            act.wait_ge(h1, i * NC + b + 1)
                        after(act, down, i * NC + (b - HBUF + 1 if b >= HBUF else 0))
                        nc.scalar.activation(hh[0:n, b % HBUF, 0, :], h[0:n, b % HBUF, :], ACT.Copy).then_inc(h_hi, 1)

            fetch(0, 0)
            fetch_w(0, 0)
            rounds(act, part)

        @block.gpsimd
        def _(pool):
            def part(i, parity):
                if exists(i):
                    for b in range(NC):
                        n = CH[b][1]
                        pool.wait_ge(h_hi, i * NC + b + 1)
                        nc.gpsimd.tensor_tensor(hh[0:n, b % HBUF, 1, :], h[0:n, b % HBUF, :],
                                                hh[0:n, b % HBUF, 0, :].bitcast(F32), ALU.subtract).then_inc(h_lo, 1)

            rounds(pool, part)

        @block.vector
        def _(dve):
            def fetch(i, parity):
                dve.wait_ge(x_hi, i + 1)
                nc.vector.tensor_tensor(xT[:, parity, 1, :], ps[:, 6, :], xT[:, parity, 0, :].bitcast(F32),
                                        ALU.subtract).then_inc(x_lo, 1)

            def part(i, parity):
                for s in range(NC):
                    if exists(i):
                        n = CH[s][1]
                        dve.wait_ge(gate_sb, i * NC + s + 1)
                        dve.wait_ge(up_ps, i * NC + s + 1)
                        after(dve, h_lo, i * NC + (s - HBUF + 1 if s >= HBUF else 0))
                        hs = h[0:n, s % HBUF, :]
                        nc.vector.tensor_tensor(hs, ps[0:n, 2 + s % 2, :], sg[0:n, s % 2, :], ALU.mult).then_inc(h1, 1)
                        if s < NR:
                            dve.drain()
                            dve.wait_ge(route_ps, i * NR + s + 1)
                            nc.vector.tensor_tensor(hs, ps[0:n, 4 + s % 2, :], hs, ALU.mult).then_inc(h2, 1)
                    if s == 2 and exists(i - 1):
                        dve.wait_ge(out_T, i)
                        nc.vector.tensor_tensor(upd[:], ps[:, 6, :].rearrange("p (k e) -> p k e", k=4),
                                                S[:, bass.ds(i * 4 - 4, 4), :], ALU.mult)
                        dve.drain()
                        nc.vector.tensor_tensor(X[:, bass.ds(i * 4 - 4, 4), :], X[:, bass.ds(i * 4 - 4, 4), :], upd[:],
                                                ALU.add).then_inc(x_new, 1)
                        dve.drain()
                    if s == FETCH and exists(i + 1):
                        fetch(i + 1, 1 - parity)

            dve.wait_ge(loaded, 16 * 8)
            fetch(0, 0)
            dve.wait_ge(w_hi, 1)
            nc.vector.tensor_tensor(wgu_lo[:], wgu[:], wgu_hi[:].bitcast(F32), ALU.subtract).then_inc(w_lo, 1)
            dve.wait_ge(w_hi, 2)
            nc.vector.tensor_tensor(wd_lo[:, 0:NC - 1, :], wd[:, 0:NC - 1, :], wd_hi[:, 0:NC - 1, :].bitcast(F32),
                                    ALU.subtract).then_inc(w_lo, 1)
            rest = CH[-1][1]
            nc.vector.tensor_tensor(wd_lo[0:rest, NC - 1, :], wd[0:rest, NC - 1, :],
                                    wd_hi[0:rest, NC - 1, :].bitcast(F32), ALU.subtract).then_inc(w_lo, 1)
            rounds(dve, part)


def inner_layers(nc, t, ps, ident, Y):
    KW = 2 * WIN
    N = 512
    MLP_ROUNDS = NBATCH * SEQ // N
    TILES = NBATCH * TPB
    CH = chunks(HID)
    NC = len(CH)
    with ExitStack() as c:
        sb = lambda n, s: c.enter_context(nc.sbuf_tensor("i_" + n, s, F32))
        sem = lambda n: c.enter_context(nc.semaphore("i_" + n))
        mask = sb("mask", [P, TPB, KW])
        rotary = sb("rotary", [P, TPB, 4, FD])
        scales = sb("scales", [P, 2, FD])
        rot = sb("rot", [P, TPB, 4, FD])
        wqkv = sb("wqkv", [P, 3 * INNER])
        wo = sb("wo", [P, 4, P])
        w1 = sb("w1", [P, 2 * HID])
        w2 = sb("w2", [P, NC, P])
        b1 = sb("b1", [P, 2, NC])
        vecs = sb("vecs", [P, 3])
        hs = sb("hs", [P, TPB, P])
        hT = sb("hT", [P, 2, SEQ])
        qk = sb("qk", [P, TPB, 2, FH, FD])
        rt = sb("rt", [P, TPB, 2, FH, FD])
        sq = sb("sq", [P, 2, FH, FD])
        ss = sb("ss", [P, TPB, 2 * FH])
        rn = sb("rn", [P, TPB, 2 * FH])
        rtmp = sb("rtmp", [P, 2 * FH])
        qT = sb("qT", [P, 4, P])
        kT = sb("kT", [P, 4, WIN + SEQ])
        V = sb("V", [P, 2, 2, TPB, INNER])
        prob = sb("prob", [P, TPB, FH, KW])
        nmax = sb("nmax", [P, TPB, FH])
        den = sb("den", [P, TPB, FH])
        probT = sb("probT", [P, 1024])
        oT = sb("oT", [P, 4, P])
        ms = sb("ms", [P, 4, P])
        st = sb("st", [P, 4, 6])
        mean = sb("mean", [P, 4])
        rstd = sb("rstd", [P, 4])
        mtmp = sb("mtmp", [P, 2, 4])
        mT = sb("mT", [P, N])
        ge = sb("ge", [P, 2, N])
        hm = sb("hm", [P, 2, N])
        zT = sb("zT", [P, N])
        (once, w_loaded, zeroed, staged, h_T, h_sb, qk_ps, qk_sb, sq_sb, ss_done, cos_done, sin_done,
         qk_done, v_ps, v_sb, qk_T, qkT_sb, scores, biased, max_done, exped, inverted, normed, p_T, pT_sb, pv_done,
         o_sb, y_ps, y_att, m_staged, m_norm, m_T, m_sb, a_ps, g_ps, g_sb, hm_done, z_ps, z_sb, z_T,
         y_mlp) = map(sem, (
            "once", "w_loaded", "zeroed", "staged", "h_T", "h_sb", "qk_ps", "qk_sb", "sq_sb", "ss_done",
            "cos_done", "sin_done", "qk_done", "v_ps", "v_sb", "qk_T", "qkT_sb", "scores", "biased",
            "max_done", "exped", "inverted", "normed", "p_T", "pT_sb", "pv_done", "o_sb", "y_ps", "y_att",
            "m_staged", "m_norm", "m_T", "m_sb", "a_ps", "g_ps", "g_sb", "hm_done", "z_ps", "z_sb", "z_T", "y_mlp"))
        block = c.enter_context(nc.Block())
        CREDIT = 2
        released = (y_mlp, h_T, h_sb, m_T, o_sb, y_att, biased, z_sb, hm_done, ss_done, qk_T, p_T, pT_sb, v_sb,
                    z_T, z_ps)
        HALF = P // 2
        NLOAD = 5 + 4 + 3 + 2
        NZERO = 4

        def sequences(eng, part):
            part(-1, 1)
            part(0, 0)
            with eng.Fori(0, (NBATCH - 4) // 2) as r:
                part(r * 2 + 1, 1)
                part(r * 2 + 2, 0)
            for i in range(NBATCH - 3, NBATCH + 1):
                part(i, i % 2)

        def tile_at(i, k, ahead):
            return i + (k + ahead) // TPB, (k + ahead) % TPB

        def exists(i):
            return not isinstance(i, int) or 0 <= i < NBATCH

        def mlp_rounds(eng, main):
            main(0)
            with eng.Fori(1, MLP_ROUNDS - 1) as r:
                main(r)
            main(MLP_ROUNDS - 1)
            main(MLP_ROUNDS)

        def is_round(r):
            return not isinstance(r, int) or 0 <= r < MLP_ROUNDS

        @block.sync
        def _(sp):
            for s in released:
                sp.sem_inc(s, CREDIT)
            sp.dma_start(mask[:], t["c_ffn_mask"]).then_inc(once, 16)
            sp.dma_start(rotary[:], t["c_rotary"]).then_inc(once, 16)
            sp.wait_ge(zeroed, NZERO)
            with sp.Fori(0, DEPTH) as l:
                sp.wait_ge(y_mlp, l * MLP_ROUNDS + CREDIT)
                ly = bass.ds(l, 1)

                def load(dst, src):
                    sp.dma_start(dst, src, allow_slow_non_contiguous=True).then_inc(w_loaded, 16)

                load(wqkv[:, :], t["L1_ffn_wqkv"][ly].rearrange("o p f -> p (o f)"))
                load(wo[:], t["L1_ffn_wo"][ly].rearrange("o (c p) f -> p (o c) f", p=P))
                load(w1[:, :], t["L1_ffn_w1"][ly].rearrange("o p f -> p (o f)"))
                load(w2[:, 0:2, :], t["L1_ffn_w2"][ly, 0:2 * P, :].rearrange("o (c p) f -> p (o c) f", p=P))
                load(w2[0:HID - 2 * P, 2:3, :], t["L1_ffn_w2"][ly, 2 * P:HID, :].rearrange("o p f -> p o f"))
                for j in range(2):
                    at = j * HID
                    load(b1[:, j, 0:2], t["L1_ffn_b1"][ly, at:at + 2 * P].rearrange("o (c p) -> p (o c)", p=P))
                    load(b1[0:HID - 2 * P, j, 2:3], t["L1_ffn_b1"][ly, at + 2 * P:at + HID].rearrange("o p -> p o"))
                for j, v in enumerate(("ln_g", "ln_b", "b2")):
                    load(vecs[:, j:j + 1], t["L1_ffn_" + v][ly].rearrange("o p -> p o"))
                for j, v in enumerate(("q_scale", "k_scale")):
                    load(scales[:, j, :], t["L1_ffn_" + v][ly].broadcast_to([P, FD]))
                with sp.Fori(0, NBATCH) as b:
                    n = l * NBATCH + b
                    sp.wait_ge(h_T, n + CREDIT)
                    sp.dma_start(hs[:, :, 0:HALF], Y[:, bass.ds(b * TPB, TPB), 0:HALF]).then_inc(staged, 16)
                    sp.dma_start(hs[1:P, :, HALF:P], Y[0:P - 1, bass.ds(b * TPB, TPB), HALF:P]).then_inc(staged, 16)
                    sp.dma_start(hs[0:1, 1, HALF:P], Y[P - 1:P, bass.ds(b * TPB, 1), HALF:P].rearrange("p o e -> p (o e)")).then_inc(staged, 16)
                with sp.Fori(0, MLP_ROUNDS) as r:
                    n = l * MLP_ROUNDS + r
                    sp.wait_ge(m_T, n + CREDIT)
                    sp.wait_ge(y_att, (l + 1) * TILES + CREDIT)
                    sp.dma_start(ms[:, :, 0:HALF], Y[:, bass.ds(r * 4, 4), 0:HALF]).then_inc(m_staged, 16)
                    sp.dma_start(ms[1:P, :, HALF:P], Y[0:P - 1, bass.ds(r * 4, 4), HALF:P]).then_inc(m_staged, 16)
                    for k in range(2):
                        sp.dma_start(ms[0:1, 2 * k + 1, HALF:P],
                                     Y[P - 1:P, bass.ds(r * 4 + 2 * k, 1), HALF:P].rearrange("p o e -> p (o e)")).then_inc(m_staged, 16)

        @block.gpsimd
        def _(pool):
            nc.gpsimd.memset(hs[:, 0, :], 0.0).then_inc(zeroed, 1)
            nc.gpsimd.memset(ms[:], 0.0).then_inc(zeroed, 1)
            nc.gpsimd.memset(kT[:, :, 0:WIN], 0.0).then_inc(zeroed, 1)
            nc.gpsimd.memset(V[:, :, 1, 0, :], 0.0).then_inc(zeroed, 1)
            with pool.Fori(0, DEPTH) as l:
                def rotate(i, k):
                    m = (l * NBATCH + i) * TPB + k
                    pool.wait_ge(qk_sb, m + 1)
                    pool.wait_ge(sin_done, m + 1)
                    for j in range(2):
                        cb = rot[:, k, 2 * j, :].unsqueeze(1).broadcast_to([P, FH, FD])
                        nc.gpsimd.tensor_tensor(qk[:, k, j], qk[:, k, j], cb, ALU.mult)
                    pool.drain()
                    nc.gpsimd.tensor_tensor(qk[:, k, 1], qk[:, k, 1], rt[:, k, 1], ALU.add).then_inc(cos_done, 1)

                def normalise(i, k):
                    pool.wait_ge(inverted, (l * NBATCH + i) * TPB + k + 1)
                    nc.gpsimd.tensor_tensor(prob[:, k], prob[:, k],
                                            den[:, k].unsqueeze(2).broadcast_to([P, FH, KW]),
                                            ALU.mult).then_inc(normed, 1)

                def part(i, parity):
                    for k in range(TPB):
                        if exists(i + 1):
                            rotate(i + 1, k)
                        if exists(i):
                            normalise(i, k)

                sequences(pool, part)

        @block.tensor
        def _(pe):
            pe.wait_ge(zeroed, NZERO)
            with pe.Fori(0, DEPTH) as l:
                count = lambda i, k=0: (l * NBATCH + i) * TPB + k

                def tokens(i):
                    n = l * NBATCH + i
                    pe.wait_ge(staged, (n + 1) * 48)
                    outputs = (i - 2) * TPB if not isinstance(i, int) else max(i - 2, 0) * TPB
                    pe.wait_ge(y_att, count(0) + outputs + CREDIT)
                    for k in range(TPB):
                        last = nc.tensor.transpose(ps[:, 7, k * P:(k + 1) * P], hs[:, k, :], ident[:, :])
                    last.then_inc(h_T, 1)

                def project_qk(i, k, parity, between):
                    m = count(i, k)
                    pe.wait_ge(h_sb, l * NBATCH + i + 1 + CREDIT)
                    here = hT[:, parity, P * k:P * (k + 1)]
                    nc.tensor.matmul(ps[:, 0, :], here, wqkv[:, 0:INNER], start=True, stop=True)
                    between()
                    pe.wait_ge(v_sb, m + CREDIT)
                    nc.tensor.matmul(ps[:, 1, :], here, wqkv[:, INNER:2 * INNER], start=True, stop=True).then_inc(qk_ps, 1)

                def project_v(i, k, parity):
                    m = count(i, k)
                    pe.wait_ge(qk_sb, m + 1)
                    pe.wait_ge(sq_sb, m + 1)
                    nc.tensor.matmul(ps[:, 1, :], hT[:, parity, P * k:P * (k + 1)], wqkv[:, 2 * INNER:],
                                     start=True, stop=True).then_inc(v_ps, 1)

                def transpose_qk(i, k):
                    m = count(i, k)
                    pe.wait_ge(qk_done, m + 1)
                    pe.wait_ge(pT_sb, m - 1 + CREDIT)
                    for j in range(2):
                        flat = qk[:, k, j].rearrange("p h d -> p (h d)")
                        for u in range(4):
                            last = nc.tensor.transpose(ps[:, 4 + j, u * P:(u + 1) * P], flat[:, u * P:(u + 1) * P], ident[:, :])
                    last.then_inc(qk_T, 1)

                def score_ready(i, k):
                    m = count(i, k)
                    pe.wait_ge(qkT_sb, m + 1)
                    pe.wait_ge(biased, m + CREDIT)

                def score(i, k):
                    for h in range(FH):
                        r, u = FD * (h % 2), h // 2
                        keys = kT[r:r + FD, u].rearrange("p (b w) -> p b w", w=WIN)
                        for a in range(2):
                            if a:
                                window = keys[:, 2 * k + 1:2 * k + 3]
                            else:
                                window = keys[:, 2 * k + 1:(2 * k - 1 if k else None):-1]
                            last = nc.tensor.matmul(ps[WIN * a:WIN * (a + 1), 2 + h % 2, u * KW:(u + 1) * KW],
                                                    qT[r:r + FD, u, WIN * a:WIN * (a + 1)], window, start=True, stop=True)
                    last.then_inc(scores, 1)

                def transpose_prob(i, k):
                    m = count(i, k)
                    pe.wait_ge(normed, m + 1)
                    flat = prob[:, k].rearrange("p a k -> p (a k)")
                    for u in range(8):
                        last = nc.tensor.transpose(ps[:, 4 + u // 4, (u % 4) * P:(u % 4 + 1) * P],
                                                   flat[:, u * P:(u + 1) * P], ident[:, :])
                    last.then_inc(p_T, 1)

                def sums(i, k, parity):
                    m = count(i, k)
                    pe.wait_ge(zeroed, NZERO)
                    pe.wait_ge(v_sb, m + 1 + CREDIT)
                    pe.wait_ge(o_sb, m + CREDIT)
                    pe.wait_ge(pT_sb, m + 1 + CREDIT)
                    for h in range(FH):
                        slot = h % 2 * 4 + h // 2
                        for a in range(2):
                            last = nc.tensor.matmul(ps[FD * (h % 2):FD * (h % 2 + 1), 6, h // 2 * P + WIN * a:h // 2 * P + WIN * (a + 1)],
                                                    V[:, parity, 1 - a, k, FD * h:FD * (h + 1)],
                                                    probT[:, slot * P + WIN * a:slot * P + WIN * (a + 1)],
                                                    start=True, stop=True)
                    last.then_inc(pv_done, 1)

                def project_out(i, k):
                    m = count(i, k)
                    pe.wait_ge(o_sb, m + 1 + CREDIT)
                    pe.wait_ge(y_att, m + CREDIT)
                    ahead = i + 3 if not isinstance(i, int) else min(i + 3, NBATCH)
                    pe.wait_ge(h_sb, l * NBATCH + ahead + CREDIT)
                    for u in range(4):
                        last = nc.tensor.matmul(ps[:, 7, 2 * P:3 * P], oT[:, u, :], wo[:, u, :], start=(u == 0), stop=(u == 3))
                    last.then_inc(y_ps, 1)

                def part(i, parity):
                    for k in range(TPB):
                        last = tile_at(i, k, -1)
                        ready = lambda: score_ready(i, k) if exists(i) else None
                        if exists(i + 1):
                            project_qk(i + 1, k, 1 - parity, ready)
                        else:
                            ready()
                            if exists(last[0]):
                                transpose_prob(*last)
                        if exists(i):
                            score(i, k)
                        if exists(i + 1) and exists(last[0]):
                            transpose_prob(*last)
                        if exists(i - 1):
                            project_out(i - 1, k)
                        if exists(last[0]):
                            sums(*last, parity ^ (k == 0))
                        ahead = tile_at(i, k, 1)
                        if exists(ahead[0]):
                            transpose_qk(*ahead)
                        if exists(i + 1):
                            project_v(i + 1, k, 1 - parity)
                        if k == TPB - 1 and exists(i + 2):
                            tokens(i + 2)

                pe.wait_ge(w_loaded, (l + 1) * NLOAD * 16)
                tokens(0)
                sequences(pe, part)

                def front(r):
                    n = l * MLP_ROUNDS + r
                    pe.wait_ge(m_norm, n + 1)
                    for k in range(4):
                        last = nc.tensor.transpose(ps[:, 6, k * P:(k + 1) * P], ms[:, k, :], ident[:, :])
                    last.then_inc(m_T, 1)

                def tail(r):
                    n = l * MLP_ROUNDS + r
                    pe.wait_ge(z_sb, n + 1 + CREDIT)
                    pe.wait_ge(y_mlp, n + CREDIT)
                    for k in range(4):
                        last = nc.tensor.transpose(ps[:, 5, k * P:(k + 1) * P], zT[:, k * P:(k + 1) * P], ident[:, :])
                    last.then_inc(z_T, 1)

                def main(r):
                    n = l * MLP_ROUNDS + r
                    if is_round(r):
                        pe.wait_ge(m_sb, n + 1)
                    for s in range(NC + 1):
                        if s < NC and is_round(r):
                            a, w = CH[s]
                            pe.wait_ge(hm_done, n * NC + max(s - 1, 0) + CREDIT)
                            nc.tensor.matmul(ps[0:w, 2 + s % 2, :], w1[:, HID + a:HID + a + w], mT[:, :], start=True, stop=True).then_inc(g_ps, 1)
                            nc.tensor.matmul(ps[0:w, s % 2, :], w1[:, a:a + w], mT[:, :], start=True, stop=True).then_inc(a_ps, 1)
                        if s == 1 and is_round(r - 1):
                            tail(r - 1)
                        if s == NC and is_round(r + 1):
                            front(r + 1)
                        if s >= 1 and is_round(r):
                            u = s - 1
                            w = CH[u][1]
                            pe.wait_ge(hm_done, n * NC + u + 1 + CREDIT)
                            if u == 0:
                                pe.wait_ge(z_sb, n + CREDIT)
                            nc.tensor.matmul(ps[:, 7, :], w2[0:w, u, :], hm[0:w, u % 2, :],
                                             start=(u == 0), stop=(u == NC - 1)).then_inc(z_ps, 1)

                pe.wait_ge(y_att, (l + 1) * TILES + CREDIT)
                front(0)
                mlp_rounds(pe, main)

        @block.scalar
        def _(act):
            act.wait_ge(zeroed, NZERO)
            with act.Fori(0, DEPTH) as l:
                count = lambda i, k=0: (l * NBATCH + i) * TPB + k
                act.wait_ge(w_loaded, (l + 1) * NLOAD * 16)

                def keep_qk(i, k):
                    m = count(i, k)
                    act.wait_ge(qk_ps, m + 1)
                    act.wait_ge(ss_done, m + CREDIT)
                    act.wait_ge(qk_T, m - 1 + CREDIT)
                    src = ps[:, 0:2, :].rearrange("p j (h d) -> p j h d", h=FH)
                    nc.scalar.activation(sq[:], src, ACT.Square).then_inc(sq_sb, 1)
                    nc.scalar.activation(qk[:, k], src, ACT.Copy).then_inc(qk_sb, 1)

                def keep_v(i, k, parity):
                    act.wait_ge(v_ps, count(i, k) + 1)
                    nc.scalar.activation(V[:, parity, 0, k, :], ps[:, 1, :], ACT.Copy)
                    if k + 1 < TPB:
                        nc.scalar.activation(V[WIN:P, parity, 1, k + 1, :], ps[WIN:P, 1, :], ACT.Copy)
                    last = nc.scalar.activation(V[0:WIN, parity, 1, k, :], ps[0:WIN, 1, :], ACT.Copy)
                    last.then_inc(v_sb, 1)

                def keep_qkT(i, k):
                    act.wait_ge(qk_T, count(i, k) + 1 + CREDIT)
                    nc.scalar.activation(qT[:], ps[:, 4, :].rearrange("p (u q) -> p u q", u=4), ACT.Copy)
                    nc.scalar.activation(kT[:, :, WIN + P * k:WIN + P * (k + 1)],
                                         ps[:, 5, :].rearrange("p (u q) -> p u q", u=4), ACT.Copy).then_inc(qkT_sb, 1)

                def exp(i, k):
                    act.wait_ge(max_done, count(i, k) + 1)
                    for h in range(FH):
                        last = nc.scalar.activation(prob[:, k, h, :], prob[:, k, h, :], ACT.Exp,
                                                    bias=nmax[:, k, h:h + 1], accum_out=den[:, k, h:h + 1])
                    last.then_inc(exped, 1)

                def keep_probT(i, k):
                    act.wait_ge(p_T, count(i, k) + 1 + CREDIT)
                    nc.scalar.activation(probT[:, :].rearrange("p (b q) -> p b q", b=2), ps[:, 4:6, :],
                                         ACT.Copy).then_inc(pT_sb, 1)

                def keep_sums(i, k):
                    act.wait_ge(pv_done, count(i, k) + 1)
                    nc.scalar.activation(oT[:], ps[:, 6, :].rearrange("p (u q) -> p u q", u=4), ACT.Copy).then_inc(o_sb, 1)

                def part(i, parity):
                    for k in range(TPB):
                        last, ahead = tile_at(i, k, -1), tile_at(i, k, 1)
                        if exists(i + 1):
                            keep_qk(i + 1, k)
                        if exists(last[0]):
                            keep_probT(*last)
                        if exists(i):
                            exp(i, k)
                        if exists(last[0]):
                            keep_sums(*last)
                        if exists(i + 1):
                            keep_v(i + 1, k, 1 - parity)
                        if exists(ahead[0]):
                            keep_qkT(*ahead)

                sequences(act, part)

                def front(r):
                    act.wait_ge(m_T, l * MLP_ROUNDS + r + 1 + CREDIT)
                    nc.scalar.activation(mT[:, :], ps[:, 6, :], ACT.Identity, scale=vecs[:, 0:1], bias=vecs[:, 1:2]).then_inc(m_sb, 1)

                def keep_z(r):
                    n = l * MLP_ROUNDS + r
                    act.wait_ge(z_ps, (n + 1) * NC + CREDIT)
                    act.wait_ge(z_T, n + CREDIT)
                    nc.scalar.activation(zT[:, :], ps[:, 7, :], ACT.Identity, bias=vecs[:, 2:3]).then_inc(z_sb, 1)

                def main(r):
                    n = l * MLP_ROUNDS + r
                    if is_round(r):
                        for s, (a, w) in enumerate(CH):
                            act.wait_ge(g_ps, n * NC + s + 1)
                            act.wait_ge(hm_done, n * NC + max(s - 1, 0) + CREDIT)
                            nc.scalar.activation(ge[0:w, s % 2, :], ps[0:w, 2 + s % 2, :], ACT.Gelu,
                                                 bias=b1[0:w, 1, s:s + 1]).then_inc(g_sb, 1)
                    if is_round(r + 1):
                        front(r + 1)
                    if is_round(r):
                        keep_z(r)

                nc.scalar.preload_act_table(ACT.Gelu)
                front(0)
                mlp_rounds(act, main)

        @block.vector
        def _(dve):
            dve.wait_ge(once, 32)
            dve.wait_ge(zeroed, NZERO)
            HF = FD // 2
            with dve.Fori(0, DEPTH) as l:
                count = lambda i, k=0: (l * NBATCH + i) * TPB + k
                dve.wait_ge(w_loaded, (l + 1) * NLOAD * 16)
                for k in range(TPB):
                    for j in range(2):
                        nc.vector.tensor_tensor(rot[:, k, 2 * j, :], rotary[:, k, 2 * j, :], scales[:, j, :], ALU.mult)
                        nc.vector.tensor_tensor(rot[:, k, 2 * j + 1, 0:HF], rotary[:, k, 2 * j + 1, 0:HF], scales[:, j, HF:FD], ALU.mult)
                        nc.vector.tensor_tensor(rot[:, k, 2 * j + 1, HF:FD], rotary[:, k, 2 * j + 1, HF:FD], scales[:, j, 0:HF], ALU.mult)
                dve.drain()

                def tokens(i, parity):
                    dve.wait_ge(h_T, l * NBATCH + i + 1 + CREDIT)
                    nc.vector.tensor_copy(hT[:, parity, :], ps[:, 7, 0:SEQ]).then_inc(h_sb, 1)

                def squares_and_sines(i, k):
                    m = count(i, k)
                    dve.wait_ge(sq_sb, m + 1)
                    nc.vector.tensor_reduce(ss[:, k], sq[:].rearrange("p j h d -> p (j h) d"), AX.X, ALU.add).then_inc(ss_done, 1)
                    dve.wait_ge(qk_sb, m + 1)
                    for j in range(2):
                        for lo, hi in ((0, HF), (HF, 0)):
                            sbc = rot[:, k, 2 * j + 1, lo:lo + HF].unsqueeze(1).broadcast_to([P, FH, HF])
                            last = nc.vector.tensor_tensor(rt[:, k, j, :, lo:lo + HF], qk[:, k, j, :, hi:hi + HF], sbc, ALU.mult)
                    last.then_inc(sin_done, 1)

                def inverse_norms(k):
                    dve.drain()
                    nc.vector.tensor_scalar(ss[:, k], ss[:, k], 1e-24, None, ALU.max)
                    dve.drain()
                    rsqrt(nc, dve, rn[:, k], ss[:, k], rtmp[:, :])

                def scale_qk(i, k):
                    dve.wait_ge(cos_done, count(i, k) + 1)
                    nc.vector.tensor_tensor(qk[:, k, 0], qk[:, k, 0], rt[:, k, 0], ALU.add)
                    dve.drain()
                    flat = qk[:, k].rearrange("p j h d -> p (j h) d")
                    nc.vector.tensor_tensor(flat, flat, rn[:, k].unsqueeze(2).broadcast_to([P, 2 * FH, FD]),
                                            ALU.mult).then_inc(qk_done, 1)

                def mask_max(i, k):
                    m = count(i, k)
                    dve.wait_ge(scores, m + 1)
                    dve.wait_ge(p_T, m - 1 + CREDIT)
                    mb = mask[:, k:k + 1, :].broadcast_to([P, FH, KW])
                    nc.vector.tensor_tensor(prob[:, k], ps[:, 2:4, :].rearrange("p b (a k) -> p (b a) k", k=KW), mb,
                                            ALU.add).then_inc(biased, 1)
                    dve.drain()
                    nc.vector.tensor_reduce(nmax[:, k], prob[:, k], AX.X, ALU.max, negate=True).then_inc(max_done, 1)

                def invert(i, k):
                    dve.wait_ge(exped, count(i, k) + 1)
                    nc.vector.reciprocal(den[:, k], den[:, k]).then_inc(inverted, 1)

                def add_out(i, k):
                    dve.wait_ge(y_ps, count(i, k) + 1)
                    dst = Y[:, bass.ds(i * TPB + k, 1), :]
                    nc.vector.tensor_tensor(dst, ps[:, 7, 2 * P:3 * P].unsqueeze(1), dst, ALU.add).then_inc(y_att, 1)

                def part(i, parity):
                    for k in range(TPB):
                        ahead = tile_at(i, k, 1)
                        if exists(ahead[0]):
                            scale_qk(*ahead)
                        if exists(i):
                            mask_max(i, k)
                        if exists(i + 1):
                            squares_and_sines(i + 1, k)
                            inverse_norms(k)
                        if exists(i - 1):
                            add_out(i - 1, k)
                        if exists(i):
                            invert(i, k)
                        if k == TPB - 1 and exists(i + 2):
                            tokens(i + 2, parity)

                tokens(0, 0)
                sequences(dve, part)

                def front(r):
                    dve.wait_ge(m_staged, (l * MLP_ROUNDS + r + 1) * 64)
                    for k in range(4):
                        nc.vector.bn_stats(st[:, k, :], ms[:, k, :])
                    dve.drain()
                    moments(nc, dve, st, mean[:, :], rstd[:, :], mtmp, 4)
                    for k in range(4):
                        last = nc.vector.tensor_scalar(ms[:, k, :], ms[:, k, :], mean[:, k:k + 1], rstd[:, k:k + 1],
                                                       ALU.subtract, ALU.mult)
                    last.then_inc(m_norm, 1)

                def tail(r):
                    dve.wait_ge(z_T, l * MLP_ROUNDS + r + 1 + CREDIT)
                    dst = Y[:, bass.ds(r * 4, 4), :]
                    nc.vector.tensor_tensor(dst, ps[:, 5, :].rearrange("p (k e) -> p k e", k=4), dst, ALU.add).then_inc(y_mlp, 1)

                def main(r):
                    n = l * MLP_ROUNDS + r
                    if is_round(r):
                        for s, (a, w) in enumerate(CH):
                            dve.wait_ge(a_ps, n * NC + s + 1)
                            dve.wait_ge(g_sb, n * NC + s + 1)
                            dve.wait_ge(z_ps, n * NC + max(s - 1, 0) + CREDIT)
                            nc.vector.scalar_tensor_tensor(hm[0:w, s % 2, :], ps[0:w, s % 2, :], b1[0:w, 0, s:s + 1],
                                                           ge[0:w, s % 2, :], ALU.add, ALU.mult).then_inc(hm_done, 1)
                            if s == 0 and is_round(r + 1):
                                front(r + 1)
                    if is_round(r - 1):
                        tail(r - 1)

                front(0)
                mlp_rounds(dve, main)


def finish(nc, X, Y, S, out):
    Q = NT // 4
    ov = out.rearrange("b (t p) e -> p (b t) e", p=P)
    with ExitStack() as c:
        sem = lambda n: c.enter_context(nc.semaphore("f_" + n))
        gated, product, total, stored = map(sem, ("gated", "product", "total", "stored"))
        block = c.enter_context(nc.Block())

        @block.scalar
        def _(act):
            for q in range(4):
                nc.scalar.activation(Y[:, q * Q:(q + 1) * Q, :], Y[:, q * Q:(q + 1) * Q, :], ACT.Silu).then_inc(gated, 1)

        @block.gpsimd
        def _(pool):
            for q in range(4):
                pool.wait_ge(gated, q + 1)
                s = slice(q * Q, (q + 1) * Q)
                nc.gpsimd.tensor_tensor(Y[:, s, :], Y[:, s, :], S[:, s, :], ALU.mult).then_inc(product, 1)

        @block.vector
        def _(dve):
            for q in range(4):
                dve.wait_ge(product, q + 1)
                s = slice(q * Q, (q + 1) * Q)
                nc.vector.tensor_tensor(X[:, s, :], Y[:, s, :], X[:, s, :], ALU.add).then_inc(total, 1)

        @block.sync
        def _(sp):
            for q in range(4):
                sp.wait_ge(total, q + 1)
                s = slice(q * Q, (q + 1) * Q)
                sp.dma_start(ov[:, s, :], X[:, s, :]).then_inc(stored, 16)
            sp.wait_ge(stored, 64)


_INS = ["L0_attn_x", "L0_attn_w_in", "L0_attn_w_out", "L0_ffn_gate_w", "L0_ffn_wg", "L0_ffn_wu", "L0_ffn_wd",
        "L0_ffn_swg", "L0_ffn_swu", "L0_ffn_swd", "L1_attn_Wq", "L1_attn_bq", "L1_attn_Wk", "L1_attn_bk",
        "L1_attn_Wv", "L1_attn_bv", "L1_attn_Wo", "L1_attn_bo", "L1_attn_rel_bias", "L1_ffn_wqkv",
        "L1_ffn_q_scale", "L1_ffn_k_scale", "L1_ffn_wo", "L1_ffn_ln_g", "L1_ffn_ln_b", "L1_ffn_w1", "L1_ffn_b1",
        "L1_ffn_w2", "L1_ffn_b2"]


def kernel(**inputs):
    import numpy as _np
    import concourse.bacc as _bacc
    from concourse import mybir as _mybir
    from concourse.bass_utils import run_bass_kernel_spmd as _run

    nc = _bacc.Bacc("TRN2", target_bir_lowering=False, num_devices=1)
    arrays, args = {}, {}
    named = [(name, inputs[name]) for name in _INS] + list(shape_constants().items())
    for name, value in named:
        a = _np.ascontiguousarray(value)
        arrays[f"in_{name}"] = a
        args[name] = nc.dram_tensor(f"in_{name}", a.shape, _mybir.dt.from_np(a.dtype), kind="ExternalInput").ap()
    out = nc.dram_tensor("out_0_dram", (NBATCH, SEQ, P), F32, kind="ExternalOutput").ap()
    build_kernel(nc, args, out)
    r = _run(nc, [arrays], core_ids=[0])
    return r.results[0]["out_0_dram"]
```
